# Optimizing a Trainium2 kernel written in Bass

```python
import numpy as np
import jax
import jax.numpy as jnp

def _softmax(x, axis=-1):
    return jax.nn.softmax(x, axis=axis)

def _gelu(x):
    return jax.nn.gelu(x, approximate=True)

def _silu(x):
    return jax.nn.silu(x)

def _sigmoid(x):
    return jax.nn.sigmoid(x)

def _layernorm(x, axis=-1, eps=1e-05):
    m = jnp.mean(x, axis=axis, keepdims=True)
    v = jnp.var(x, axis=axis, keepdims=True)
    return (x - m) / jnp.sqrt(v + eps)

def _scatter_add(tgt, idx, src, axis=0):
    return tgt.at[idx].add(src)

def _segment_sum(src, seg, n):
    return jax.ops.segment_sum(src, seg, n)
kernel_name = 'mk_gnn_ffn_d1_gnn_r8_48fb08'

def setup_inputs(seed: int=0):
    np.random.seed(seed)
    _w = jnp.asarray

    def _rec_inputs():
        import jax
        import jax.numpy as jnp
        _gk = jax.random.key(seed)
        x = -0.0002117 + 1 * jax.random.normal(jax.random.fold_in(_gk, 1), (12500, 256), jnp.float32)
        src = jax.random.randint(jax.random.fold_in(_gk, 2), (200000,), 0, 12500, jnp.int32)
        dst = jax.random.randint(jax.random.fold_in(_gk, 3), (200000,), 0, 12500, jnp.int32)
        _o = jnp.argsort(dst, stable=True)
        src = src[_o]
        dst = dst[_o]
        return (x, src, dst)
    x, src, dst = _rec_inputs()

    def _L0_gnn_setup():
        import jax, jax.numpy as jnp
        import numpy as np
        N = 12500
        E = 100000
        IN_DIM = 256
        HEADS = 8
        OUT_DIM = 32
        OUT_ALL = HEADS * OUT_DIM
        NEG_SLOPE = 0.2
        key = jax.random.key(seed)
        ks = jax.random.split(key, 10)
        s_in = 1.0 / np.sqrt(IN_DIM)
        x = jax.random.normal(ks[0], (N, IN_DIM), dtype=jnp.float32)
        edge_index = jax.random.randint(ks[1], (2, E), 0, N, dtype=jnp.int64)
        Wl = jax.random.normal(ks[2], (IN_DIM, OUT_ALL), dtype=jnp.float32) * s_in
        bl = jnp.zeros((OUT_ALL,), dtype=jnp.float32)
        Wr = jax.random.normal(ks[3], (IN_DIM, OUT_ALL), dtype=jnp.float32) * s_in
        br = jnp.zeros((OUT_ALL,), dtype=jnp.float32)
        att = jax.random.normal(ks[4], (HEADS, OUT_DIM), dtype=jnp.float32) * (1.0 / np.sqrt(OUT_DIM))
        bias = jnp.zeros((OUT_ALL,), dtype=jnp.float32)
        gamma = jnp.ones((OUT_ALL,), dtype=jnp.float32)
        beta = jnp.zeros((OUT_ALL,), dtype=jnp.float32)
        return {'x': x, 'edge_index': edge_index, 'Wl': Wl, 'bl': bl, 'Wr': Wr, 'br': br, 'att': att, 'bias': bias, 'gamma': gamma, 'beta': beta}
    _L0_gnn_all = _L0_gnn_setup()
    _L0_gnn_in = {k: v for k, v in _L0_gnn_all.items() if k in ('Wl', 'bl', 'Wr', 'br', 'att', 'bias', 'gamma', 'beta')}
    del _L0_gnn_all

    def _L0_ffn_setup():
        import jax, jax.numpy as jnp
        import numpy as np
        C = 256
        HID = 1024
        E = 8
        TEMP = 1.0
        key = jax.random.key(seed)
        ks = jax.random.split(key, 7)
        x = jax.random.normal(ks[0], (8, 2048, C), dtype=jnp.float32)
        W1 = jax.random.normal(ks[1], (C, HID), dtype=jnp.float32) * 0.02
        b1 = jnp.zeros((HID,), dtype=jnp.float32)
        Wg = jax.random.normal(ks[2], (HID, E), dtype=jnp.float32) * 0.02
        bg = jnp.zeros((E,), dtype=jnp.float32)
        Wd = jax.random.normal(ks[3], (E, HID, C), dtype=jnp.float32) * 0.02
        bd = jnp.zeros((E, C), dtype=jnp.float32)
        return {'x': x, 'W1': W1, 'b1': b1, 'Wg': Wg, 'bg': bg, 'Wd': Wd, 'bd': bd}
    _L0_ffn_all = _L0_ffn_setup()
    _L0_ffn_in = {k: v for k, v in _L0_ffn_all.items() if k in ('W1', 'b1', 'Wg', 'bg', 'Wd', 'bd')}
    del _L0_ffn_all
    return {'x': x, 'src': src, 'dst': dst, 'L0_gnn_Wl': _L0_gnn_in['Wl'], 'L0_gnn_bl': _L0_gnn_in['bl'], 'L0_gnn_Wr': _L0_gnn_in['Wr'], 'L0_gnn_br': _L0_gnn_in['br'], 'L0_gnn_att': _L0_gnn_in['att'], 'L0_gnn_bias': _L0_gnn_in['bias'], 'L0_gnn_gamma': _L0_gnn_in['gamma'], 'L0_gnn_beta': _L0_gnn_in['beta'], 'L0_ffn_W1': _L0_ffn_in['W1'], 'L0_ffn_b1': _L0_ffn_in['b1'], 'L0_ffn_Wg': _L0_ffn_in['Wg'], 'L0_ffn_bg': _L0_ffn_in['bg'], 'L0_ffn_Wd': _L0_ffn_in['Wd'], 'L0_ffn_bd': _L0_ffn_in['bd']}

def reference(x, src, dst, L0_gnn_Wl, L0_gnn_bl, L0_gnn_Wr, L0_gnn_br, L0_gnn_att, L0_gnn_bias, L0_gnn_gamma, L0_gnn_beta, L0_ffn_W1, L0_ffn_b1, L0_ffn_Wg, L0_ffn_bg, L0_ffn_Wd, L0_ffn_bd):
    import jax
    import jax.numpy as jnp

    def _L0_gnn_ref(x, edge_index, Wl, bl, Wr, br, att, bias, gamma, beta):
        import jax, jax.numpy as jnp
        import numpy as np
        N = 12500
        E = 100000
        IN_DIM = 256
        HEADS = 8
        OUT_DIM = 32
        OUT_ALL = HEADS * OUT_DIM
        NEG_SLOPE = 0.2
        src, dst = (edge_index[0], edge_index[1])
        x_l = (x @ Wl + bl).reshape(N, HEADS, OUT_DIM)
        x_r = (x @ Wr + br).reshape(N, HEADS, OUT_DIM)
        s = jax.nn.leaky_relu(x_l[src] + x_r[dst], NEG_SLOPE)
        e = jnp.einsum('ehd,hd->eh', s, att)
        m = jax.ops.segment_max(e, dst, num_segments=N)
        p = jnp.exp(e - m[dst])
        denom = jax.ops.segment_sum(p, dst, num_segments=N)
        denom = jnp.where(denom == 0, 1.0, denom)
        alpha = p / denom[dst]
        msg = alpha[:, :, None] * x_l[src]
        out = jax.ops.segment_sum(msg, dst, num_segments=N)
        y = out.reshape(N, OUT_ALL) + bias
        z = y + x
        mu = jnp.mean(z, axis=-1, keepdims=True)
        var = jnp.var(z, axis=-1, keepdims=True)
        zn = (z - mu) * jax.lax.rsqrt(var + 1e-05) * gamma + beta
        return jax.nn.elu(zn)

    def _L0_ffn_ref(x, W1, b1, Wg, bg, Wd, bd):
        import jax, jax.numpy as jnp
        import numpy as np
        C = 256
        HID = 1024
        E = 8
        TEMP = 1.0
        orig_shape = x.shape
        xf = x.reshape(-1, orig_shape[-1])
        H = jax.nn.gelu(xf @ W1 + b1, approximate=False)
        probs = jax.nn.softmax((H @ Wg + bg) / TEMP, axis=-1)
        assign = jnp.argmax(probs, axis=-1)
        out = jnp.zeros_like(xf)
        for e in range(Wd.shape[0]):
            y = H @ Wd[e] + bd[e]
            sel = (assign == e)[:, None]
            out = out + jnp.where(sel, probs[:, e:e + 1] * y, 0.0)
        return out.reshape(orig_shape)
    edge_index = jnp.stack([src, dst])
    x = x + _L0_gnn_ref(_layernorm(x, axis=-1), edge_index, L0_gnn_Wl, L0_gnn_bl, L0_gnn_Wr, L0_gnn_br, L0_gnn_att, L0_gnn_bias, L0_gnn_gamma, L0_gnn_beta)
    x = x + _L0_ffn_ref(_layernorm(x, axis=-1)[None], L0_ffn_W1, L0_ffn_b1, L0_ffn_Wg, L0_ffn_bg, L0_ffn_Wd, L0_ffn_bd)[0]
    return x

_drawn_inputs = setup_inputs


def setup_inputs(seed=0):
    import zlib

    import numpy as np

    out = dict(_drawn_inputs(seed))
    spreads = {'L0_gnn_bl': (0.0, 0.1),
     'L0_gnn_br': (0.0, 0.8),
     'L0_gnn_bias': (0.0, 0.1),
     'L0_gnn_gamma': (1.0, 0.2),
     'L0_gnn_beta': (0.0, 0.1),
     'L0_ffn_b1': (0.0, 0.8),
     'L0_ffn_bg': (0.0, 0.672),
     'L0_ffn_bd': (0.0, 0.8)}
    factors = {'L0_ffn_W1': 4.622, 'L0_ffn_Wg': 4.965, 'L0_ffn_Wd': 5.663}
    for name, (base, spread) in spreads.items():
        noise = np.random.default_rng([zlib.crc32(name.encode()), seed]).standard_normal(out[name].shape)
        drawn = base * np.exp(spread * noise) if base else spread * noise
        out[name] = jnp.asarray(drawn.astype(out[name].dtype))
    for name, factor in factors.items():
        out[name] = (out[name] * factor).astype(out[name].dtype)
    return out
```

```python
from contextlib import ExitStack
import concourse.bass as bass
from concourse import mybir

P = 128
F32 = mybir.dt.float32
I32 = mybir.dt.int32
ALU = mybir.AluOpType
ACT = mybir.ActivationFunctionType
AX = mybir.AxisListType
EPS = 1e-5
NEG = -1e30
NODES, EDGES, D = 12500, 200000, 256
HEADS, HD = 8, 32
HS = HD + 1
C = 12
BLOCK = P * C
RING = 3
BLOCKS = -(-(-(-EDGES // BLOCK)) // RING) * RING
PADDED = BLOCKS * BLOCK
NODES_UP = (NODES // P + 2) * P
EXTRA = -(-(NODES // P) // RING) * RING
FAR = 20000
G = 3
SW = HEADS * HS + HEADS
XW = D + HEADS


def setup(nc, src, dst, src_pad, dst_pad, xr_d, st_d, rows_d, tabf_d, tabi_d):
    with ExitStack() as ctx:
        sb = lambda n, s, d=F32: ctx.enter_context(nc.sbuf_tensor(n, s, d))
        sem = lambda n: ctx.enter_context(nc.semaphore(n))
        tail = PADDED - EDGES
        tp = 64
        far = sb("far", [tp, tail // tp], I32); nil = sb("nil", [tp, tail // tp], I32)
        zx = sb("zx", [P, XW]); st0 = sb("st0", [P, SW])
        fi = sb("fi", [1, 2, BLOCKS], I32); ff = sb("ff", [1, 2, BLOCKS])
        sp_f = sb("sp_f", [1, BLOCKS]); sp_i = sb("sp_i", [1, BLOCKS], I32); sh_i = sb("sh_i", [1, BLOCKS], I32)
        rows = sb("rows", [1, 3, BLOCKS]); inc = sb("inc", [1, BLOCKS]); one = sb("one", [1, BLOCKS])
        bc = sb("bc", [EXTRA, 3, BLOCKS]); m1 = sb("m1", [EXTRA, BLOCKS]); m2 = sb("m2", [EXTRA, BLOCKS]); m3 = sb("m3", [EXTRA, BLOCKS])
        siota = sb("siota", [EXTRA, BLOCKS]); j = sb("j", [EXTRA, 1]); j128 = sb("j128", [EXTRA, 1])
        red = sb("red", [EXTRA, 3]); res = sb("res", [EXTRA, 2]); resi = sb("resi", [EXTRA, 2], I32)
        firsti = sb("firsti", [1, BLOCKS], I32); tot = sb("tot", [1, 1]); toti = sb("toti", [1, 1], I32); tmp = sb("tmp", [EXTRA, 1])
        made = sem("setup_made"); filled = sem("filled"); loaded = sem("loaded"); v = sem("table_step"); wrote = sem("table_rows"); back = sem("rows_back"); done = sem("tables_stored"); io = sem("setup_iota")
        block = ctx.enter_context(nc.Block())

        @block.gpsimd
        def _(pool):
            pool.iota(siota[:], [[1, BLOCKS]], base=0, channel_multiplier=0, allow_small_or_imprecise_dtypes=True).then_inc(io, 1)
            pool.iota(j[:], [[0, 1]], base=0, channel_multiplier=1, allow_small_or_imprecise_dtypes=True).then_inc(io, 1)
            pool.iota(j128[:], [[0, 1]], base=P, channel_multiplier=P, allow_small_or_imprecise_dtypes=True).then_inc(io, 1)

        @block.sync
        def _(sp):
            sp.dma_start(dst_pad[0:EDGES].rearrange("(a b) -> a b", a=125), dst.rearrange("(a b) -> a b", a=125)).then_inc(filled, 16)
            sp.dma_start(src_pad[0:EDGES].rearrange("(a b) -> a b", a=125), src.rearrange("(a b) -> a b", a=125)).then_inc(filled, 16)
            sp.wait_ge(made, 4)
            sp.dma_start(dst_pad[EDGES:PADDED].rearrange("(a b) -> a b", a=tp), far[:]).then_inc(filled, 16)
            sp.dma_start(src_pad[EDGES:PADDED].rearrange("(a b) -> a b", a=tp), nil[:]).then_inc(filled, 16)
            sp.dma_start(xr_d[NODES:NODES + P, :], zx[:]).then_inc(filled, 16)
            sp.dma_start(xr_d[NODES + P:NODES_UP, :], zx[0:NODES_UP - NODES - P, :]).then_inc(filled, 16)
            sp.dma_start(st_d.rearrange("(t p) c -> p t c", p=P), st0[:].rearrange("p (o c) -> p o c", o=1).to_broadcast([P, NODES_UP // P, SW])).then_inc(filled, 16)
            sp.wait_ge(filled, 7 * 16)
            ends = dst_pad.rearrange("(o s e) -> o s e", o=1, e=BLOCK)
            with nc.allow_non_contiguous_dma(reason="one destination of each block"):
                sp.dma_start(fi[:, 0, :], ends[:, :, 0]).then_inc(loaded, 16)
                sp.dma_start(fi[:, 1, :], ends[:, :, BLOCK - 1]).then_inc(loaded, 16)
            sp.wait_ge(v, 8)
            sp.dma_start(rows_d[None, :, :], rows[:]).then_inc(wrote, 16)
            sp.dma_start(tabf_d[None, 0:BLOCKS], rows[:, 2, :]).then_inc(done, 16)
            sp.dma_start(tabi_d[None, 0, 0:BLOCKS], firsti[:]).then_inc(done, 16)
            sp.dma_start(tabi_d[None, 1, BLOCKS + EXTRA:BLOCKS + EXTRA + 1], toti[:]).then_inc(done, 16)
            sp.wait_ge(wrote, 16)
            sp.dma_start(bc[:], rows_d[None, :, :].to_broadcast([EXTRA, 3, BLOCKS])).then_inc(back, 16)
            sp.wait_ge(v, 21)
            with nc.allow_non_contiguous_dma(reason="a table row"):
                sp.dma_start(tabf_d[BLOCKS:BLOCKS + EXTRA, None], res[:, 0:1]).then_inc(done, 16)
                sp.dma_start(tabi_d[0, BLOCKS:BLOCKS + EXTRA, None], resi[:, 0:1]).then_inc(done, 16)
                sp.dma_start(tabi_d[1, BLOCKS:BLOCKS + EXTRA, None], resi[:, 1:2]).then_inc(done, 16)
            sp.wait_ge(done, 6 * 16)

        @block.vector
        def _(dve):
            dve.memset(far[:], FAR).then_inc(made, 1)
            dve.memset(nil[:], 0).then_inc(made, 1)
            dve.memset(zx[:], 0.0).then_inc(made, 1)
            dve.memset(one[:], 1.0)
            dve.memset(st0[:, 0:HEADS * HS], 0.0)
            dve.memset(st0[:, HEADS * HS:SW], NEG).then_inc(made, 1)
            dve.wait_ge(loaded, 32)
            n = [0]

            def then(ins):
                n[0] += 1
                ins.then_inc(v, 1)
                dve.wait_ge(v, n[0])
            then(dve.tensor_scalar(ff[:, 0, :], fi[:, 0, :], float(NODES), None, ALU.min))
            then(dve.tensor_scalar(ff[:, 1, :], fi[:, 1, :], float(NODES - 1), None, ALU.min))
            then(dve.tensor_tensor(sp_f[:], ff[:, 1, :], ff[:, 0, :], ALU.subtract))
            then(dve.tensor_scalar(sp_i[:], sp_f[:], 0.0, None, ALU.max))
            then(dve.tensor_scalar(sh_i[:], sp_i[:], 7, None, ALU.arith_shift_right))
            dve.tensor_copy(firsti[:], ff[:, 0, :])
            dve.tensor_copy(rows[:, 2, :], ff[:, 0, :])
            then(dve.tensor_copy(rows[:, 1, :], sh_i[:]))
            then(dve.tensor_tensor_scan(inc[:], one[:], rows[:, 1, :], 0.0, ALU.mult, ALU.add))
            dve.tensor_copy(toti[:], inc[:, BLOCKS - 1:BLOCKS])
            then(dve.tensor_tensor(rows[:, 0, :], inc[:], rows[:, 1, :], ALU.subtract))
            dve.wait_ge(back, 16)
            dve.wait_ge(io, 3)
            then(dve.tensor_scalar(m1[:], bc[:, 0, :], j[:, 0:1], None, ALU.is_le))
            then(dve.tensor_tensor(m2[:], bc[:, 0, :], bc[:, 1, :], ALU.add))
            then(dve.tensor_scalar(m3[:], m2[:], j[:, 0:1], None, ALU.is_gt))
            then(dve.tensor_tensor(m1[:], m1[:], m3[:], ALU.mult))
            then(dve.tensor_scalar(m2[:], bc[:, 0, :], -float(P), j128[:, 0:1], ALU.mult, ALU.add))
            then(dve.tensor_tensor(m2[:], m2[:], bc[:, 2, :], ALU.add))
            then(dve.tensor_tensor(m2[:], m2[:], m1[:], ALU.mult))
            then(dve.tensor_tensor(m3[:], siota[:], m1[:], ALU.mult))
            dve.tensor_reduce(red[:, 0:1], m2[:], AX.X, ALU.add)
            dve.tensor_reduce(red[:, 1:2], m3[:], AX.X, ALU.add)
            then(dve.tensor_reduce(red[:, 2:3], m1[:], AX.X, ALU.add))
            then(dve.tensor_scalar(tmp[:], red[:, 2:3], -float(NODES), float(NODES), ALU.mult, ALU.add))
            dve.tensor_copy(res[:, 1:2], red[:, 1:2])
            then(dve.tensor_tensor(res[:, 0:1], red[:, 0:1], tmp[:], ALU.add))
            then(dve.tensor_copy(resi[:], res[:]))
            then(dve.tensor_copy(tmp[:], res[:, 0:1]))


def edges(nc, att, xl_d, xr_d, src_pad, dst_pad, st_d, tabf_d, tabi_d):
    with ExitStack() as ctx:
        sb = lambda n, s, d=F32: ctx.enter_context(nc.sbuf_tensor(n, s, d))
        ps = lambda n, s, d=F32: ctx.enter_context(nc.psum_tensor(n, s, d))
        sem = lambda n: ctx.enter_context(nc.semaphore(n))
        ring = lambda n: [sem(f"{n}{r}") for r in range(RING)]
        idx = sb("idx", [P, RING, C], I32); dsti = sb("dsti", [P, RING, C], I32); base = sb("base", [P, RING, 1])
        xrw = sb("xrw", [P, RING, XW]); xl = sb("xl", [P, RING, C, XW]); px = sb("px", [P, RING, C, HEADS, HS])
        dst8 = sb("dst8", [P, RING, C, HEADS]); rel = sb("rel", [P, RING, C])
        hot = sb("hot", [P, RING, C, P]); hotT = sb("hotT", [P, RING, C * P])
        s = sb("s", [P, 2, 512 * 3])
        att_sb = sb("att_sb", [P, 2, HEADS])
        e_sb = sb("e_sb", [P, RING, C, HEADS])
        dts = sb("dts", [C * HEADS, P]); reset = sb("reset", [C * HEADS, P + 1]); runmax = sb("runmax", [C * HEADS, P]); lastmax = sb("lastmax", [C * HEADS, P])
        rh = sb("rh", [P, C, HEADS + 1]); pen = sb("pen", [P, C]); vs = sb("vs", [P, C, HEADS])
        mraw = sb("mraw", [P, HEADS]); m = sb("m", [P, RING, 2 * HEADS]); de = sb("de", [P, C, HEADS]); d = sb("d", [P, C, HEADS]); dm = sb("dm", [P, C, HEADS])
        st = sb("st", [P, RING, SW]); new = sb("new", [P, RING, SW]); mn = sb("mn", [P, HEADS]); dd = sb("dd", [P, 2, HEADS]); ab = sb("ab", [P, 2, HEADS])
        t2 = sb("t2", [P, HEADS * HS])
        ident = sb("ident2", [P, P]); ones = sb("ones2", [P, P]); iota = sb("iota2", [P, P])
        tab = sb("tab", [1, 2, BLOCKS + EXTRA + 1], I32)
        psz = ps("psz", [P, 3, 512]); psot = ps("psot", [P, 512]); pss = ps("pss", [P, 512]); psv = ps("psv", [P, 512]); psa = ps("psa", [P, 512])
        ps_e = pss[:, 0:96]
        ps_et = psv[0:96, 0:128]; ps_dt = psv[0:96, 128:256]; ps_fm = psv[:, 256:352]
        ps_v = psv[:, 0:108].rearrange("p (c h) -> p c h", h=9); ps_m = psv[:, 128:320].rearrange("p (c h) -> p c h", h=16)
        idx_in = ring("idx_in"); win_in = ring("win_in"); st_in = ring("st_in"); xl_in = ring("xl_in"); stored = ring("stored")
        sp_passed = sem("sp_passed"); pool_passed = sem("pool_passed")
        consts = sem("consts2"); cz = sem("cz2"); attin = sem("attin")
        hot_made = sem("hot_made"); ot_tr = sem("ot_tr"); ot_copied = sem("ot_copied"); z_made = sem("z_made"); s_made = sem("s_made"); e_made = sem("e_made"); e_copied = sem("e_copied")
        rel_made = sem("rel_made")
        et_made = sem("et_made"); dts_made = sem("dts_made"); reset_made = sem("reset_made"); run_made = sem("run_made"); fm_made = sem("fm_made"); fmt_made = sem("fmt_made"); rh_made = sem("rh_made")
        v_made = sem("v_made"); pen_made = sem("pen_made"); vs_made = sem("vs_made"); m_made = sem("m_made"); mraw_made = sem("mraw_made"); de_made = sem("de_made"); me_made = sem("me_made"); d_made = sem("d_made"); dm_made = sem("dm_made"); p_made = sem("p_made"); px_made = sem("px_made")
        a_made = sem("a_made"); mn_made = sem("mn_made"); dd_made = sem("dd_made"); ab_made = sem("ab_made"); new_part = sem("new_part"); t2_made = sem("t2_made"); new_made = sem("new_made")
        block = ctx.enter_context(nc.Block())

        def pipeline(eng, slot, k0, n):
            for k in range(3):
                slot(k0 + k, k, (k0 + k) // RING, a=True, b=k >= 1, c=k >= 2)
            with eng.Fori(1, n // RING) as i:
                for r in range(RING):
                    slot(k0 + RING * i + r, r, i + k0 // RING, a=True, b=True, c=True)
            slot(k0 + n, 0, (k0 + n) // RING, a=False, b=True, c=True)
            slot(k0 + n + 1, 1, (k0 + n) // RING, a=False, b=False, c=True)

        @block.sync
        def _(sp):
            sp.wait_ge(consts, 4)
            sp.dma_start(tab[:, 0, 0:BLOCKS + EXTRA], tabi_d[None, 0, 0:BLOCKS + EXTRA]).then_inc(attin, 16)
            sp.dma_start(tab[:, 1, BLOCKS:], tabi_d[None, 1, BLOCKS:]).then_inc(attin, 16)
            with nc.allow_non_contiguous_dma(reason="attention weights by feature"):
                for h in range(HEADS):
                    p0 = h % 4 * HD
                    sp.dma_start(att_sb[p0:p0 + HD, h // 4, h:h + 1], att[h, :, None]).then_inc(attin, 16)
            sp.wait_ge(attin, 16 * 10)
            W = tab[0:1, 0, :]
            B = tab[0:1, 1, :]
            srcv = src_pad.rearrange("(s p j) -> s p j", p=P, j=C)
            dstv = dst_pad.rearrange("(s p j) -> s p j", p=P, j=C)
            one = lambda x: slice(x, x + 1) if isinstance(x, int) else bass.ds(x, 1)
            rows = lambda w: bass.ds(w, P)

            def which(k, extra):
                if not extra:
                    return k
                return sp.value_load(B[:, one(k)], min_val=0, max_val=BLOCKS - 1)

            def window(k):
                return sp.value_load(W[:, one(k)], min_val=0, max_val=NODES)

            def load_idx(k, r, extra):
                sp.dma_start(idx[:, r, :], srcv[one(which(k, extra)), :, :].rearrange("o p j -> p (o j)")).then_inc(idx_in[r], 16)

            def load_window(k, r, extra):
                sp.dma_start(dsti[:, r, :], dstv[one(which(k, extra)), :, :].rearrange("o p j -> p (o j)")).then_inc(win_in[r], 16)
                sp.dma_start(base[:, r, :], tabf_d[one(k)].rearrange("(o k) -> o k", o=1).to_broadcast([P, 1])).then_inc(win_in[r], 16)
                sp.dma_start(xrw[:, r, :], xr_d[rows(window(k)), :]).then_inc(win_in[r], 16)

            def load_state(k, r):
                sp.dma_start(st[:, r, :], st_d[rows(window(k)), :]).then_inc(st_in[r], 16)

            def settle():
                sp.sem_inc(sp_passed, 1)

            def run(k0, n, extra):
                for k in range(3):
                    load_idx(k0 + k, k, extra)
                for k in range(2):
                    load_window(k0 + k, k, extra)
                load_state(k0, 0)

                def slot(k, r, u, a, b, c, ahead_idx=True, ahead_win=True):
                    if ahead_idx:
                        sp.wait_ge(xl_in[r], 16 * C * (u + 1))
                        settle()
                        load_idx(k + 3, r, extra)
                    if ahead_win:
                        q = (r + 2) % RING
                        if not (isinstance(k, int) and k == k0):
                            sp.wait_ge(z_made, 6 * k)
                            settle()
                            sp.wait_ge(rel_made, 2 * k)
                            settle()
                        load_window(k + 2, q, extra)
                    if c:
                        q = (r + 1) % RING
                        sp.wait_ge(new_made, k - 1)
                        settle()
                        sp.dma_start(st_d[rows(window(k - 2)), :], new[:, q, :]).then_inc(stored[q], 16)
                        sp.wait_ge(stored[q], 16 * (u + 1 if r >= 2 else u))
                        settle()
                    if b:
                        q = (r + 2) % RING
                        if not (isinstance(k, int) and k - 1 == k0):
                            pass
                        load_state(k - 1, q) if not (isinstance(k, int) and k - 1 == k0) else None
                for k in range(3):
                    slot(k0 + k, k, (k0 + k) // RING, True, k >= 1, k >= 2)
                with sp.Fori(1, n // RING - 1) as i:
                    for r in range(RING):
                        slot(k0 + RING * i + r, r, i + k0 // RING, True, True, True)
                kk = k0 + n - RING
                for r in range(RING):
                    slot(kk + r, r, kk // RING, True, True, True, ahead_idx=False, ahead_win=r == 0)
                slot(k0 + n, 0, (k0 + n) // RING, False, True, True, False, False)
                slot(k0 + n + 1, 1, (k0 + n) // RING, False, False, True, False, False)
            run(0, BLOCKS, False)
            if GENERAL:
                more = sp.value_load(B[:, BLOCKS + EXTRA:BLOCKS + EXTRA + 1], min_val=0, max_val=EXTRA)
                with sp.If(more > 0):
                    run(BLOCKS, EXTRA, True)

        @block.gpsimd
        def _(pool):
            pool.memset(ones[:], 1.0).then_inc(cz, 1)
            pool.wait_ge(cz, 1)
            pool.affine_select(out=ident[:], in_=ones[:], compare_op=ALU.is_equal, fill=0.0, base=0, pattern=[[-1, P]], channel_multiplier=1).then_inc(consts, 1)
            pool.iota(iota[:], [[1, P]], base=0, channel_multiplier=0, allow_small_or_imprecise_dtypes=True).then_inc(consts, 1)

            def gathers(k, r, u, free=True):
                pool.wait_ge(idx_in[r], 16 * (u + 1))
                if free:
                    pool.sem_inc(pool_passed, 1)
                    pool.wait_ge(px_made, 2 * (k - 2))
                pool.sem_inc(pool_passed, 1)
                for j in range(C):
                    pool.indirect_dma_start(xl[:, r, j, :], None, xl_d[:, :], bass.IndirectOffsetOnAxis(idx[:, r, j:j + 1], 0),
                                            bounds_check=NODES - 1, oob_is_err=False).then_inc(xl_in[r], 16)

            def run(k0, n):
                for r in range(RING):
                    gathers(k0 + r, r, k0 // RING, free=k0 > 0)
                with pool.Fori(1, n // RING) as i:
                    for r in range(RING):
                        gathers(k0 + RING * i + r, r, i + k0 // RING)
            run(0, BLOCKS)
            if GENERAL:
                pool.wait_ge(attin, 16 * 10)
                more = pool.value_load(tab[0:1, 1, BLOCKS + EXTRA:BLOCKS + EXTRA + 1], min_val=0, max_val=EXTRA)
                with pool.If(more > 0):
                    run(BLOCKS, EXTRA)

        @block.vector
        def _(dve):
            dve.memset(reset[:, 0:1], 0.0)
            dve.memset(reset[:, P:P + 1], -1.0)
            dve.memset(att_sb[:], 0.0).then_inc(consts, 1)
            dve.memset(rh[:], 1.0).then_inc(consts, 1)
            dve.wait_ge(consts, 4)

            def make_hot(k, r, u):
                dve.wait_ge(win_in[r], 48 * (u + 1))
                if not (isinstance(k, int) and k < 3):
                    dve.wait_ge(et_made, k - 2)
                dve.tensor_copy(m[:, r, HEADS:2 * HEADS], xrw[:, r, D:XW])
                dve.tensor_copy(dst8[:, r, :, :], dsti[:, r, :].unsqueeze(2).to_broadcast([P, C, HEADS])).then_inc(rel_made, 1)
                dve.tensor_scalar(rel[:, r, :], dsti[:, r, :], base[:, r, 0:1], None, ALU.subtract).then_inc(rel_made, 1)
                dve.wait_ge(rel_made, 2 * k + 2)
                if not (isinstance(k, int) and k < 3):
                    dve.wait_ge(a_made, k - 2)
                for g in range(G):
                    dve.tensor_tensor(hot[:, r, 4 * g:4 * g + 4, :], iota[:].unsqueeze(1).to_broadcast([P, 4, P]),
                                      rel[:, r, 4 * g:4 * g + 4].unsqueeze(2).to_broadcast([P, 4, P]), ALU.is_equal).then_inc(hot_made, 1)

            def slot(k, r, u, a, b, c, ahead=True):
                qb = (r + 2) % RING
                qc = (r + 1) % RING
                if b:
                    dve.wait_ge(e_made, 3 * k)
                    dve.tensor_tensor(e_sb[:, qb, :, :], xl[:, qb, :, D:XW], ps_e.rearrange("p (c h) -> p c h", h=HEADS), ALU.add).then_inc(e_copied, 1)
                if c:
                    uc = u + 1 if r >= 2 else u
                    dve.wait_ge(st_in[qc], 16 * uc)
                    dve.tensor_tensor(mn[:], st[:, qc, HEADS * HS:SW], m[:, qc, 0:HEADS], ALU.max).then_inc(mn_made, 1)
                    dve.wait_ge(mn_made, k - 1)
                    dve.tensor_tensor(dd[:, 0, :], st[:, qc, HEADS * HS:SW], mn[:], ALU.subtract)
                    dve.tensor_tensor(dd[:, 1, :], m[:, qc, 0:HEADS], mn[:], ALU.subtract).then_inc(dd_made, 1)
                if b:
                    dve.wait_ge(et_made, k)
                    dve.tensor_scalar(dts[:], ps_dt, -NEG, None, ALU.mult).then_inc(dts_made, 1)
                    dve.wait_ge(dts_made, k)
                    dve.tensor_tensor(reset[:, 1:P], dts[:, 0:P - 1], dts[:, 1:P], ALU.subtract).then_inc(reset_made, 1)
                    dve.wait_ge(reset_made, k)
                    dve.tensor_tensor_scan(runmax[:], reset[:, 0:P], ps_et, NEG, ALU.add, ALU.max).then_inc(run_made, 1)
                    dve.wait_ge(run_made, k)
                    dve.scalar_tensor_tensor(out=lastmax[:], in0=reset[:, 1:P + 1], scalar=0.0, in1=runmax[:], op0=ALU.is_lt, op1=ALU.mult).then_inc(fm_made, 1)
                if c:
                    dve.wait_ge(ab_made, k - 1)
                    bro = lambda i: ab[:, i, :].unsqueeze(2).to_broadcast([P, HEADS, HS])
                    hv = lambda x: x.rearrange("p (h f) -> p h f", f=HS)
                    dve.tensor_tensor(hv(new[:, qc, 0:HEADS * HS]), hv(st[:, qc, 0:HEADS * HS]), bro(0), ALU.mult).then_inc(new_part, 1)
                    dve.tensor_copy(new[:, qc, HEADS * HS:SW], mn[:])
                    dve.wait_ge(a_made, k - 1)
                    dve.tensor_tensor(hv(t2[:]), hv(psa[:, 0:HEADS * HS]), bro(1), ALU.mult).then_inc(t2_made, 1)
                    dve.wait_ge(t2_made, k - 1)
                    dve.wait_ge(new_part, k - 1)
                    dve.tensor_tensor(new[:, qc, 0:HEADS * HS], new[:, qc, 0:HEADS * HS], t2[:], ALU.add).then_inc(new_made, 1)
                if b:
                    dve.wait_ge(v_made, k)
                    dve.tensor_scalar(pen[:], ps_v[:, :, HEADS], 0.0, NEG, ALU.is_equal, ALU.mult).then_inc(pen_made, 1)
                    dve.wait_ge(pen_made, k)
                    dve.tensor_tensor(vs[:], ps_v[:, :, 0:HEADS], pen[:].unsqueeze(2).to_broadcast([P, C, HEADS]), ALU.add).then_inc(vs_made, 1)
                    dve.wait_ge(vs_made, k)
                    dve.tensor_reduce(mraw[:], vs[:].rearrange("p c h -> p h c"), AX.X, ALU.max).then_inc(mraw_made, 1)
                    dve.wait_ge(mraw_made, k)
                    dve.tensor_tensor(m[:, qb, 0:HEADS], mraw[:], m[:, qb, HEADS:2 * HEADS], ALU.add).then_inc(m_made, 1)
                if a and ahead:
                    make_hot(k + 1, (r + 1) % RING, u + 1 if r == 2 else u)
                if b:
                    dve.wait_ge(me_made, k)
                    dve.tensor_tensor(de[:], e_sb[:, qb, :, :], ps_m[:, :, HEADS:], ALU.add).then_inc(de_made, 1)
                    dve.wait_ge(de_made, k)
                    dve.tensor_tensor(d[:], de[:], ps_m[:, :, 0:HEADS], ALU.subtract).then_inc(d_made, 1)
                    dve.wait_ge(d_made, k)
                    dve.tensor_scalar(dm[:], d[:], 0.0, None, ALU.min).then_inc(dm_made, 1)
                    dve.wait_ge(p_made, k)
                    dve.wait_ge(xl_in[qb], 16 * C * (u if r == 0 else u + 1))
                    for g in range(2):
                        cs = slice(g * C // 2, (g + 1) * C // 2)
                        xv = xl[:, qb, cs, 0:D].rearrange("p c (h f) -> p c h f", f=HD)
                        pv = px[:, qb, cs, :, :]
                        dve.tensor_tensor(pv[:, :, :, 0:HD], xv, pv[:, :, :, HD:HS].to_broadcast([P, C // 2, HEADS, HD]), ALU.mult).then_inc(px_made, 1)

            def run(k0, n):
                make_hot(k0, 0, k0 // RING)
                for k in range(3):
                    slot(k0 + k, k, (k0 + k) // RING, a=True, b=k >= 1, c=k >= 2)
                with dve.Fori(1, n // RING - 1) as i:
                    for r in range(RING):
                        slot(k0 + RING * i + r, r, i + k0 // RING, a=True, b=True, c=True)
                kk = k0 + n - RING
                for r in range(RING):
                    slot(kk + r, r, kk // RING, a=True, b=True, c=True, ahead=r < 2)
                slot(k0 + n, 0, (k0 + n) // RING, a=False, b=True, c=True)
                slot(k0 + n + 1, 1, (k0 + n) // RING, a=False, b=False, c=True)
            run(0, BLOCKS)
            if GENERAL:
                dve.wait_ge(attin, 16 * 10)
                more = dve.value_load(tab[0:1, 1, BLOCKS + EXTRA:BLOCKS + EXTRA + 1], min_val=0, max_val=EXTRA)
                with dve.If(more > 0):
                    run(BLOCKS, EXTRA)

        @block.scalar
        def _(act):
            def slot(k, r, u, a, b, c):
                qb = (r + 2) % RING
                late = not (isinstance(k, int) and k < 3)

                def copy_hotT(g):
                    act.wait_ge(ot_tr, 3 * k + g + 1)
                    if late:
                        act.wait_ge(me_made, k - 2)
                    act.copy(hotT[:, r, 512 * g:512 * g + 512], psot[:]).then_inc(ot_copied, 1)

                def leaky(g):
                    for h in range(2):
                        act.wait_ge(z_made, 6 * k + 2 * g + h + 1)
                        if not (isinstance(k, int) and k == 0):
                            act.wait_ge(e_made, 3 * (k - 1) + g + 1)
                        act.activation(s[:, h, 512 * g:512 * g + 512], psz[:, (2 * g + h) % 3, :], ACT.Relu, scale=0.8).then_inc(s_made, 1)
                if a:
                    copy_hotT(0)
                if c:
                    act.wait_ge(dd_made, k - 1)
                    if not (isinstance(k, int) and k < 3):
                        act.wait_ge(t2_made, k - 2)
                    act.activation(ab[:], dd[:], ACT.Exp).then_inc(ab_made, 1)
                if a:
                    leaky(0)
                    copy_hotT(1)
                    leaky(1)
                if b:
                    act.wait_ge(fmt_made, k)
                    act.copy(rh[:, :, 0:HEADS], ps_fm.rearrange("p (c h) -> p c h", h=HEADS)).then_inc(rh_made, 1)
                if a:
                    copy_hotT(2)
                    leaky(2)
                if b:
                    act.wait_ge(dm_made, k)
                    act.activation(px[:, qb, :, :, HD], dm[:], ACT.Exp).then_inc(p_made, 1)
            act.wait_ge(consts, 4)
            pipeline(act, slot, 0, BLOCKS)
            if GENERAL:
                act.wait_ge(attin, 16 * 10)
                more = act.value_load(tab[0:1, 1, BLOCKS + EXTRA:BLOCKS + EXTRA + 1], min_val=0, max_val=EXTRA)
                with act.If(more > 0):
                    pipeline(act, slot, BLOCKS, EXTRA)

        @block.tensor
        def _(pe):
            pe.wait_ge(consts, 4)
            pe.wait_ge(attin, 16 * 10)

            def slot(k, r, u, a, b, c):
                qb = (r + 2) % RING
                qc = (r + 1) % RING
                first = isinstance(k, int) and k == 0

                def hot_columns(g):
                    pe.wait_ge(hot_made, 3 * k + g + 1)
                    if not (first and g == 0):
                        pe.wait_ge(ot_copied, 3 * k + g)
                    for c_ in range(4):
                        last = pe.transpose(psot[:, P * c_:P * c_ + P], hot[:, r, 4 * g + c_, :], ident[:])
                    last.then_inc(ot_tr, 1)

                def z(g):
                    pe.wait_ge(ot_copied, 3 * k + g + 1)
                    if g == 0:
                        pe.wait_ge(xl_in[r], 16 * C * (u + 1))
                        pe.wait_ge(win_in[r], 48 * (u + 1))
                    for h in range(2):
                        bank = (2 * g + h) % 3
                        if not (first and 2 * g + h < 3):
                            pe.wait_ge(s_made, 6 * k + 2 * g + h - 2)
                        pe.matmul(psz[:, bank, :], xrw[:, r, P * h:P * h + P], hotT[:, r, 512 * g:512 * g + 512], start=True, stop=False)
                        for c_ in range(4):
                            last = pe.matmul(psz[:, bank, P * c_:P * c_ + P], xl[:, r, 4 * g + c_, P * h:P * h + P], ident[:],
                                             is_transpose=True, start=False, stop=c_ == 3)
                        last.then_inc(z_made, 1)

                def scores(k, g, wait_copy):
                    pe.wait_ge(s_made, 6 * k + 2 * g + 2)
                    if wait_copy:
                        pe.wait_ge(e_copied, k)
                    for c_ in range(4):
                        j = 4 * g + c_
                        for h in range(2):
                            last = pe.matmul(ps_e[:, HEADS * j:HEADS * j + HEADS], s[:, h, P * j:P * j + P], att_sb[:, h, :], start=h == 0, stop=h == 1)
                    last.then_inc(e_made, 1)
                if a:
                    hot_columns(0)
                if b:
                    scores(k - 1, 2, False)
                if a:
                    z(0)
                if b:
                    pe.wait_ge(e_copied, k)
                    if not (isinstance(k, int) and k < 2):
                        pe.wait_ge(d_made, k - 1)
                    pe.transpose(ps_et, e_sb[:, qb, :, :].rearrange("p c h -> p (c h)"), ident[:])
                    pe.transpose(ps_dt, dst8[:, qb, :, :].rearrange("p c h -> p (c h)"), ident[:]).then_inc(et_made, 1)
                if a:
                    hot_columns(1)
                if c:
                    pe.wait_ge(px_made, 2 * (k - 1))
                    if not (isinstance(k, int) and k < 3):
                        pe.wait_ge(t2_made, k - 2)
                    for j in range(C):
                        last = pe.matmul(psa[:, 0:HEADS * HS], hot[:, qc, j, :], px[:, qc, j, :, :].rearrange("p h f -> p (h f)"), start=j == 0, stop=j == C - 1)
                    last.then_inc(a_made, 1)
                if a:
                    z(1)
                    scores(k, 0, not first)
                if b:
                    pe.wait_ge(fm_made, k)
                    pe.transpose(ps_fm, lastmax[:], ident[0:C * HEADS, 0:C * HEADS]).then_inc(fmt_made, 1)
                if a:
                    hot_columns(2)
                    z(2)
                if b:
                    pe.wait_ge(rh_made, k)
                    for j in range(C):
                        last = pe.matmul(ps_v[:, j, :], hot[:, qb, j, :], rh[:, j, :], start=True, stop=True)
                    last.then_inc(v_made, 1)
                if a:
                    scores(k, 1, False)
                if b:
                    pe.wait_ge(m_made, k)
                    for j in range(C):
                        last = pe.matmul(ps_m[:, j, :], hotT[:, qb, P * j:P * j + P], m[:, qb, :], start=True, stop=True)
                    last.then_inc(me_made, 1)
            pipeline(pe, slot, 0, BLOCKS)
            if GENERAL:
                more = pe.value_load(tab[0:1, 1, BLOCKS + EXTRA:BLOCKS + EXTRA + 1], min_val=0, max_val=EXTRA)
                with pe.If(more > 0):
                    pipeline(pe, slot, BLOCKS, EXTRA)

GENERAL = True
def project(nc, x, Wl, Wr, bl, br, att, xn_d, xl_d, xr_d):
    N, D = x.shape
    TILES = (N + P - 1) // P
    LAST = N - P
    with ExitStack() as ctx:
        sb = lambda n, s, d=F32: ctx.enter_context(nc.sbuf_tensor(n, s, d))
        ps = lambda n, s, d=F32: ctx.enter_context(nc.psum_tensor(n, s, d))
        sem = lambda n: ctx.enter_context(nc.semaphore(n))
        xb = sb("xb", [P, 2, D]); xnb = sb("xnb", [P, 2, D]); xT = sb("xT", [P, 2, 2, P])
        W = sb("W", [P, 2, 2 * D]); bias = sb("bias", [P, 2 * D]); lr = sb("lr", [P, 2, 2, XW]); att_row = sb("att_row", [P, 2, D]); att_02 = sb("att_02", [P, 2, D]); la = sb("la", [P, 2, D]); la_made = sem("la_made"); y_made = sem("y_made"); a02 = sem("a02")
        stats = sb("stats", [P, 6]); mv = sb("mv", [P, 2]); ve = sb("ve", [P, 1]); half = sb("half", [P, 1]); rstd = sb("rstd", [P, 1])
        ident = sb("ident", [P, P]); ones = sb("ones", [P, P])
        psT = ps("psT", [P, 2, 512]); psY = ps("psY", [P, 2, 512])
        consts = sem("consts"); idz = sem("idz"); wload = sem("wload")
        xl_ = [sem("x_loaded0"), sem("x_loaded1")]
        stat = sem("stat"); aggr = sem("aggr"); vped = sem("vped"); rst = sem("rst"); xnd = sem("xnd")
        tr = sem("tr"); xTd = sem("xTd"); mm = sem("mm"); lrd = sem("lrd")
        st = [sem("stored0"), sem("stored1")]
        block = ctx.enter_context(nc.Block())

        def rows(t):
            return bass.ds(t * P, P) if not isinstance(t, int) or t < TILES - 1 else slice(LAST, LAST + P)

        def loop(eng, step):
            with eng.Fori(0, TILES // 2 - 1) as i:
                step(i, 0, False); step(i, 1, False)
            step(TILES // 2 - 1, 0, True); step(TILES // 2 - 1, 1, True)

        @block.sync
        def _(sp):
            sp.dma_start(W[:, 0, 0:D], Wl[0:P, :]).then_inc(wload, 16)
            sp.dma_start(W[:, 1, 0:D], Wl[P:2 * P, :]).then_inc(wload, 16)
            sp.dma_start(W[:, 0, D:2 * D], Wr[0:P, :]).then_inc(wload, 16)
            sp.dma_start(W[:, 1, D:2 * D], Wr[P:2 * P, :]).then_inc(wload, 16)
            sp.dma_start(bias[:, 0:D], bl[None, :].to_broadcast([P, D])).then_inc(wload, 16)
            sp.dma_start(bias[:, D:2 * D], br[None, :].to_broadcast([P, D])).then_inc(wload, 16)
            for side in range(2):
                sp.dma_start(att_row[:, side, :], att.rearrange("(o h) f -> o (h f)", o=1).to_broadcast([P, D])).then_inc(wload, 16)
            sp.dma_start(xb[:, 0, :], x[0:P, :]).then_inc(xl_[0], 16)
            sp.dma_start(xb[:, 1, :], x[P:2 * P, :]).then_inc(xl_[1], 16)

            def step(i, b, last):
                t = 2 * i + b
                sp.wait_ge(xnd, t + 1)
                if not (last):
                    sp.dma_start(xb[:, b, :], x[rows(t + 2) , :]).then_inc(xl_[b], 16)
                sp.wait_ge(lrd, t + 1)
                sp.dma_start(xn_d[rows(t), :], xnb[:, b, :]).then_inc(st[b], 16)
                sp.dma_start(xl_d[rows(t), :], lr[:, b, 0, :]).then_inc(st[b], 16)
                sp.dma_start(xr_d[rows(t), :], lr[:, b, 1, :]).then_inc(st[b], 16)
            with sp.Fori(0, TILES // 2 - 2) as i:
                step(i, 0, False); step(i, 1, False)
            k = TILES // 2 - 2
            step(k, 0, False); step(k, 1, False)
            sp.wait_ge(st[0], 48 * (k + 1)); sp.wait_ge(st[1], 48 * (k + 1))
            step(k + 1, 0, True)
            sp.wait_ge(st[0], 48 * (k + 2))
            step(k + 1, 1, True)
            sp.wait_ge(st[1], 48 * (k + 2))

        @block.gpsimd
        def _(pool):
            pool.memset(ones[:], 1.0).then_inc(idz, 1)
            pool.memset(half[:], -0.5).then_inc(consts, 1)
            pool.wait_ge(idz, 1)
            pool.affine_select(out=ident[:], in_=ones[:], compare_op=ALU.is_equal, fill=0.0, base=0, pattern=[[-1, P]], channel_multiplier=1).then_inc(consts, 1)
            pool.wait_ge(consts, 1)
            def step(i, b, last):
                t = 2 * i + b
                pool.wait_ge(vped, t + 1)
                pool.tensor_tensor(rstd[:], ve[:], half[:], ALU.pow).then_inc(rst, 1)
            loop(pool, step)

        @block.vector
        def _(dve):
            dve.wait_ge(wload, 128)
            dve.tensor_scalar(att_02[:], att_row[:], 0.2, None, ALU.mult).then_inc(a02, 1)
            dve.wait_ge(a02, 1)
            def add_bias(t, b):
                dve.wait_ge(mm, t + 1)
                dve.tensor_tensor(lr[:, b, :, 0:D], psY[:, b, :].rearrange("p (s f) -> p s f", s=2), bias[:].rearrange("p (s f) -> p s f", s=2), ALU.add).then_inc(y_made, 1)
                dve.wait_ge(y_made, t + 1)
                dve.tensor_tensor(la[:], lr[:, b, :, 0:D], att_02[:], ALU.mult).then_inc(la_made, 1)
                dve.wait_ge(la_made, t + 1)
                dve.tensor_reduce(lr[:, b, :, D:XW], la[:].rearrange("p s (h f) -> p s h f", f=HD), AX.X, ALU.add).then_inc(lrd, 1)
            def step(t, b, uses, first=False):
                dve.wait_ge(xl_[b], 16 * (uses + 1))
                dve.bn_stats(stats[:], xb[:, b, :]).then_inc(stat, 1)
                dve.wait_ge(stat, t + 1)
                if not first:
                    add_bias(t - 1, 1 - b)
                dve.bn_aggr(mv[:], stats[:]).then_inc(aggr, 1)
                dve.wait_ge(aggr, t + 1)
                dve.tensor_scalar(ve[:], mv[:, 1:2], EPS, None, ALU.add).then_inc(vped, 1)
                dve.wait_ge(rst, t + 1)
                if not (isinstance(uses, int) and uses == 0):
                    dve.wait_ge(st[b], 48 * uses)
                dve.tensor_scalar(xnb[:, b, :], xb[:, b, :], mv[:, 0:1], rstd[:, 0:1], ALU.subtract, ALU.mult).then_inc(xnd, 1)
            step(0, 0, 0, True)
            step(1, 1, 0)
            step(2, 0, 1)
            with dve.Fori(1, TILES // 2 - 1) as i:
                step(2 * i + 1, 1, i)
                step(2 * i + 2, 0, i + 1)
            step(TILES - 1, 1, TILES // 2 - 1)
            add_bias(TILES - 1, 1)

        @block.scalar
        def _(act):
            def step(i, b, last):
                t = 2 * i + b
                act.wait_ge(tr, t + 1)
                act.copy(xT[:, b, :, :], psT[:, b, 0:2 * P].rearrange("p (h n) -> p h n", h=2)).then_inc(xTd, 1)
            loop(act, step)

        @block.tensor
        def _(pe):
            pe.wait_ge(wload, 128)
            pe.wait_ge(consts, 2)
            def step(i, b, last):
                t = 2 * i + b
                pe.wait_ge(xnd, t + 1)
                pe.transpose(psT[:, b, 0:P], xnb[:, b, 0:P], ident[:])
                pe.transpose(psT[:, b, P:2 * P], xnb[:, b, P:2 * P], ident[:]).then_inc(tr, 1)
                pe.wait_ge(xTd, t + 1)
                pe.matmul(psY[:, b, :], xT[:, b, 0, :], W[:, 0, :], start=True, stop=False)
                pe.matmul(psY[:, b, :], xT[:, b, 1, :], W[:, 1, :], start=False, stop=True).then_inc(mm, 1)
            loop(pe, step)


HID, EXPERTS = 1024, 8
HC = HID // P
T4 = 4
GROUP = T4 * P
GROUPS = -(-NODES // GROUP)
LAST0 = NODES - GROUP
REPEATED = (GROUPS - 1) * GROUP - LAST0
CAP = (NODES // P + 2) * P
RW = D + 4
ETILES = (NODES + EXPERTS * (P - 1)) // P
ROUTED = EXPERTS * CAP + P
NOWHERE = float(1 << 20)


def nodes(nc, x, bias, gamma, beta, W1, b1, Wg, bg, xn_d, st_d, routed_d, etab_d):
    with ExitStack() as ctx:
        sb = lambda n, s, d=F32: ctx.enter_context(nc.sbuf_tensor(n, s, d))
        ps = lambda n, s, d=F32: ctx.enter_context(nc.psum_tensor(n, s, d))
        sem = lambda n: ctx.enter_context(nc.semaphore(n))
        stb = sb("n_st", [P, 2, T4, SW]); xnb = sb("n_xn", [P, 2, T4, D]); xb = sb("n_x", [P, 2, T4, D])
        rden = sb("rden", [P, T4, HEADS]); z = sb("z", [P, T4, D]); neg = sb("neg", [P, T4, D]); eneg = sb("eneg", [P, T4, D])
        stats = sb("n_stats", [P, T4, 6]); mv = sb("n_mv", [P, T4, 2]); ve = sb("n_ve", [P, T4]); rstd = sb("n_rstd", [P, T4])
        row = sb("row", [P, 2, T4, RW]); x2n = sb("x2n", [P, T4, D]); x2T = sb("x2T", [P, 2, GROUP]); H = sb("H", [P, HC, GROUP])
        bias_r = sb("bias_r", [P, D]); gamma_r = sb("gamma_r", [P, D]); beta_r = sb("beta_r", [P, D]); bg_r = sb("bg_r", [P, EXPERTS])
        w1 = sb("w1", [P, 2, HID]); b1c = sb("b1c", [P, HC]); wg = sb("wg", [P, HC, EXPERTS])
        lg = sb("lg", [P, T4, EXPERTS]); lmax = sb("lmax", [P, T4]); ex = sb("ex", [P, T4, EXPERTS]); pr = sb("pr", [P, T4, EXPERTS])
        one = sb("one_hot", [P, T4, EXPERTS]); before = sb("before", [P, T4 + 1, EXPERTS]); cnt = sb("cnt", [P, EXPERTS]); cap0 = sb("cap0", [P, EXPERTS])
        prio = sb("prio", [P, EXPERTS]); top = sb("top", [P, T4]); rk = sb("rk", [P, T4, EXPERTS]); posf = sb("posf", [P, T4]); posi = sb("posi", [P, 2, T4], I32)
        valid = sb("valid", [P, T4]); invalid = sb("invalid", [P, T4]); half = sb("n_half", [P, T4]); ident = sb("n_ident", [P, P]); ones = sb("n_ones", [P, P]); tri = sb("tri", [P, P])
        pid = sb("pid", [P, 1]); nodei = sb("nodei", [P, T4])
        j128 = sb("n_j128", [P, 1]); nti = sb("nti", [P, EXPERTS], I32); ntf = sb("ntf", [P, EXPERTS]); w = sb("n_w", [P, 6, EXPERTS]); red = sb("n_red", [P, 4]); et = sb("et", [P, 2]); eti = sb("eti", [P, 2], I32)
        pad = sb("pad", [P, RW]); padpos = sb("padpos", [P, EXPERTS], I32)
        psx = ps("psx", [P, 2, GROUP]); psh = ps("psh", [P, 2, GROUP]); psl_ = ps("psl", [P, 512]); psr_ = ps("psr", [P, 512])
        psl = psl_[:, 0:T4 * EXPERTS].rearrange("p (t e) -> p t e", e=EXPERTS); psr = psr_[:, 0:(T4 + 1) * EXPERTS].rearrange("p (t e) -> p t e", e=EXPERTS)
        cz = sem("n_cz"); consts = sem("n_consts"); wload = sem("n_wload"); loaded = [sem("n_loaded0"), sem("n_loaded1")]
        x1_done = sem("x1_done"); z_done = sem("z_done"); vp = sem("n_vp"); rst = sem("n_rst"); neg_done = sem("neg_done"); eneg_done = sem("eneg_done"); x2_done = sem("x2_done")
        xT = sem("n_xT"); xT_copied = sem("xT_copied"); h_made = sem("h_made"); gelu_done = sem("gelu_done"); l_made = sem("l_made"); lm_done = sem("lm_done"); ex_done = sem("ex_done")
        hot_done = sem("n_hot_done"); r_made = sem("r_made"); pos_done = sem("pos_done"); scattered = [sem("scattered0"), sem("scattered1")]; passed = sem("n_passed"); dpassed = sem("n_dpassed")
        rowbase = sb("rowbase", [P, 1]); dpassed2 = sem("n_dpassed2"); top_done = sem("top_done"); masked = sem("masked"); masked2 = sem("masked2"); rk_s = sem("rk_step"); pf_done = sem("pf_done")
        link_s = sem("node_step"); route_s = sem("route_step"); tabs = sem("n_tabs"); padded = sem("padded"); tstep = sem("tstep"); tstored = sem("tstored")
        block = ctx.enter_context(nc.Block())
        bro = lambda v, s: v.to_broadcast(s)

        def rows(g):
            return LAST0 if isinstance(g, int) and g == GROUPS - 1 else g * GROUP

        def grouped(a, g):
            r0 = rows(g)
            return a[bass.ds(r0, GROUP), :].rearrange("(t p) c -> p t c", p=P)

        @block.sync
        def _(sp):
            rb = lambda a, n: a.rearrange("(o c) -> o c", o=1).to_broadcast([P, n])
            sp.dma_start(bias_r[:], rb(bias, D)).then_inc(wload, 16)
            sp.dma_start(gamma_r[:], rb(gamma, D)).then_inc(wload, 16)
            sp.dma_start(beta_r[:], rb(beta, D)).then_inc(wload, 16)
            sp.dma_start(bg_r[:], rb(bg, EXPERTS)).then_inc(wload, 16)
            sp.dma_start(w1[:], W1.rearrange("(k p) c -> p k c", p=P)).then_inc(wload, 16)
            sp.dma_start(wg[:], Wg.rearrange("(k p) c -> p k c", p=P)).then_inc(wload, 16)
            with nc.allow_non_contiguous_dma(reason="bias by hidden unit"):
                sp.dma_start(b1c[:], b1.rearrange("(k p) -> p k", p=P)).then_inc(wload, 16)

            def load(g, b):
                sp.dma_start(stb[:, b, :, :], grouped(st_d, g)).then_inc(loaded[b], 16)
                sp.dma_start(xnb[:, b, :, :], grouped(xn_d, g)).then_inc(loaded[b], 16)
                sp.dma_start(xb[:, b, :, :], grouped(x, g)).then_inc(loaded[b], 16)
            load(0, 0)
            load(1, 1)
            with sp.Fori(0, (GROUPS - 3) // 2) as i:
                for b in range(2):
                    g = 2 * i + b
                    sp.wait_ge(x1_done, g + 1)
                    sp.sem_inc(passed, 1)
                    load(g + 2, b)
            for g in range((GROUPS - 3) // 2 * 2, GROUPS - 2):
                sp.wait_ge(x1_done, g + 1)
                load(g + 2, g % 2)
            sp.wait_ge(tabs, 1)
            with nc.allow_non_contiguous_dma(reason="a table row"):
                sp.dma_start(etab_d[0, :, None], eti[0:ETILES, 0:1]).then_inc(tstored, 16)
                sp.dma_start(etab_d[1, :, None], eti[0:ETILES, 1:2]).then_inc(tstored, 16)
            sp.dma_start(routed_d[EXPERTS * CAP:ROUTED, :], pad[:]).then_inc(tstored, 16)
            sp.wait_ge(tstored, 48)

        @block.gpsimd
        def _(pool):
            pool.memset(ones[:], 1.0).then_inc(cz, 1)
            pool.memset(half[:], -0.5).then_inc(consts, 1)
            pool.memset(valid[:], 1.0).then_inc(cz, 1)
            pool.iota(pid[:], [[0, 1]], base=0, channel_multiplier=1, allow_small_or_imprecise_dtypes=True).then_inc(consts, 1)
            pool.iota(nodei[:], [[P, T4]], base=0, channel_multiplier=1, allow_small_or_imprecise_dtypes=True).then_inc(consts, 1)
            pool.iota(cap0[:], [[CAP, EXPERTS]], base=0, channel_multiplier=0, allow_small_or_imprecise_dtypes=True).then_inc(consts, 1)
            pool.iota(prio[:], [[-1, EXPERTS]], base=EXPERTS, channel_multiplier=0, allow_small_or_imprecise_dtypes=True).then_inc(consts, 1)
            pool.iota(j128[:], [[0, 1]], base=0, channel_multiplier=P, allow_small_or_imprecise_dtypes=True).then_inc(consts, 1)
            pool.wait_ge(cz, 2)
            pool.affine_select(out=ident[:], in_=ones[:], compare_op=ALU.is_equal, fill=0.0, base=0, pattern=[[-1, P]], channel_multiplier=1).then_inc(consts, 1)
            pool.affine_select(out=tri[:], in_=ones[:], compare_op=ALU.is_gt, fill=0.0, base=0, pattern=[[1, P]], channel_multiplier=-1).then_inc(consts, 1)
            pool.affine_select(out=valid[:], in_=ones[:, 0:T4], compare_op=ALU.is_ge, fill=0.0, base=-REPEATED, pattern=[[P, T4]], channel_multiplier=1).then_inc(consts, 1)

            def rsqrt(g, n):
                pool.wait_ge(vp, 2 * g + n + 1)
                pool.tensor_tensor(rstd[:], ve[:], half[:], ALU.pow).then_inc(rst, 1)

            def scatter(g, b):
                pool.wait_ge(pos_done, g + 1)
                pool.sem_inc(dpassed, 1)
                for t in range(T4):
                    pool.indirect_dma_start(routed_d[:, :], bass.IndirectOffsetOnAxis(posi[:, b, t:t + 1], 0), row[:, b, t, :], None,
                                            bounds_check=ROUTED - 1, oob_is_err=False).then_inc(scattered[b], 16)
            rsqrt(0, 0)
            rsqrt(0, 1)
            with pool.Fori(0, (GROUPS - 1) // 2) as i:
                for b in range(2):
                    rsqrt(2 * i + b + 1, 0)
                    rsqrt(2 * i + b + 1, 1)
                    scatter(2 * i + b, b)
            scatter(GROUPS - 1, 0)
            pool.wait_ge(tabs, 1)
            pool.wait_ge(scattered[0], 16 * T4 * ((GROUPS + 1) // 2))
            pool.wait_ge(scattered[1], 16 * T4 * (GROUPS // 2))
            for e in range(EXPERTS):
                pool.indirect_dma_start(routed_d[:, :], bass.IndirectOffsetOnAxis(padpos[:, e:e + 1], 0), pad[:, :], None,
                                        bounds_check=ROUTED - 1, oob_is_err=False).then_inc(padded, 16)
            pool.wait_ge(padded, 16 * EXPERTS)

        @block.vector
        def _(dve):
            dve.memset(cnt[:], 0.0)
            dve.memset(before[:, 0, :], 0.0)
            dve.memset(pad[:, 0:RW - 1], 0.0)
            dve.memset(pad[:, RW - 1:RW], NOWHERE)
            dve.wait_ge(consts, 9)
            dve.wait_ge(wload, 7 * 16)
            dve.tensor_scalar(invalid[:], valid[:], -NOWHERE, NOWHERE, ALU.mult, ALU.add)

            N_STEPS, R_STEPS = [None], [None]

            def chain(s, g, total):
                n = [0]

                def then(ins, wait=True):
                    n[0] += 1
                    ins.then_inc(s, 1)
                    if wait:
                        dve.wait_ge(s, total * g + n[0])
                return then, n

            NT = 11
            def node(g, b, u):
                then, n = chain(link_s, g, NT)
                heads = lambda v: v.rearrange("p t (h f) -> p t h f", f=HS)
                acc = heads(stb[:, b, :, 0:HEADS * HS])
                f3 = lambda v: v.unsqueeze(1).to_broadcast([P, T4, D])
                dve.wait_ge(loaded[b], 48 * (u + 1))
                then(dve.tensor_scalar(rden[:], acc[:, :, :, HD], 0.0, None, ALU.is_equal))
                then(dve.tensor_tensor(rden[:], rden[:], acc[:, :, :, HD], ALU.add))
                then(dve.reciprocal(rden[:], rden[:]))
                then(dve.tensor_tensor(z[:].rearrange("p t (h f) -> p t h f", f=HD), acc[:, :, :, 0:HD], rden[:].unsqueeze(3).to_broadcast([P, T4, HEADS, HD]), ALU.mult))
                then(dve.tensor_tensor(z[:], z[:], f3(bias_r[:]), ALU.add))
                then(dve.tensor_tensor(z[:], z[:], xnb[:, b, :, :], ALU.add))

                def moments(src, k):
                    for t in range(T4):
                        ins = dve.bn_stats(stats[:, t, :], src[:, t, :])
                    ins.then_inc(z_done, 1)
                    dve.wait_ge(z_done, 4 * g + 2 * k + 1)
                    dve.sem_inc(dpassed2, 1)
                    for t in range(T4):
                        ins = dve.bn_aggr(mv[:, t, :], stats[:, t, :])
                    ins.then_inc(z_done, 1)
                    dve.wait_ge(z_done, 4 * g + 2 * k + 2)
                    dve.tensor_scalar(ve[:], mv[:, :, 1], EPS, None, ALU.add).then_inc(vp, 1)
                    dve.wait_ge(rst, 2 * g + k + 1)
                moments(z, 0)
                for t in range(T4):
                    ins = dve.tensor_scalar(z[:, t, :], z[:, t, :], mv[:, t, 0:1], rstd[:, t:t + 1], ALU.subtract, ALU.mult)
                then(ins)
                then(dve.tensor_tensor(z[:], z[:], f3(gamma_r[:]), ALU.mult))
                then(dve.tensor_tensor(z[:], z[:], f3(beta_r[:]), ALU.add))
                dve.tensor_scalar(neg[:], z[:], 0.0, None, ALU.min).then_inc(neg_done, 1)
                if not (isinstance(u, int) and u == 0):
                    dve.wait_ge(scattered[b], 16 * T4 * u)
                then(dve.scalar_tensor_tensor(out=row[:, b, :, 0:D], in0=z[:], scalar=0.0, in1=xb[:, b, :, :], op0=ALU.max, op1=ALU.add))
                dve.wait_ge(eneg_done, g + 1)
                dve.scalar_tensor_tensor(out=row[:, b, :, 0:D], in0=eneg[:], scalar=-1.0, in1=row[:, b, :, 0:D], op0=ALU.add, op1=ALU.add).then_inc(x1_done, 1)
                dve.wait_ge(x1_done, g + 1)
                moments(row[:, b, :, 0:D], 1)
                dve.tensor_copy(row[:, b, :, D], mv[:, :, 0])
                then(dve.tensor_copy(row[:, b, :, D + 1], rstd[:]))
                if not (isinstance(g, int) and g == 0):
                    dve.wait_ge(xT, g)
                for t in range(T4):
                    ins = dve.tensor_scalar(x2n[:, t, :], row[:, b, t, 0:D], mv[:, t, 0:1], rstd[:, t:t + 1], ALU.subtract, ALU.mult)
                ins.then_inc(x2_done, 1)
                assert n[0] == NT, n

            RT = 10
            def route(g, b, last=False):
                then, n = chain(route_s, g, RT)
                e3 = lambda v: v.unsqueeze(2).to_broadcast([P, T4, EXPERTS])
                dve.wait_ge(l_made, g + 1)
                then(dve.tensor_tensor(lg[:], psl, bg_r[:].unsqueeze(1).to_broadcast([P, T4, EXPERTS]), ALU.add))
                then(dve.tensor_reduce(lmax[:], lg[:], AX.X, ALU.max))
                dve.tensor_tensor(lg[:], lg[:], e3(lmax[:]), ALU.subtract).then_inc(lm_done, 1)
                dve.wait_ge(ex_done, g + 1)
                then(dve.tensor_reduce(lmax[:], ex[:], AX.X, ALU.add))
                then(dve.reciprocal(lmax[:], lmax[:]))
                then(dve.tensor_tensor(pr[:], ex[:], e3(lmax[:]), ALU.mult))
                dve.tensor_reduce(top[:], pr[:], AX.X, ALU.max).then_inc(top_done, 1)
                dve.wait_ge(top_done, g + 1)
                dve.tensor_copy(row[:, b, :, D + 2], top[:])
                dve.tensor_scalar(row[:, b, :, D + 3], nodei[:], rowbase[:, 0:1], None, ALU.add)
                then(dve.tensor_tensor(one[:], pr[:], e3(top[:]), ALU.is_equal))
                then(dve.tensor_tensor(one[:], one[:], prio[:].unsqueeze(1).to_broadcast([P, T4, EXPERTS]), ALU.mult))
                then(dve.tensor_reduce(top[:], one[:], AX.X, ALU.max))
                then(dve.tensor_tensor(one[:], prio[:].unsqueeze(1).to_broadcast([P, T4, EXPERTS]), e3(top[:]), ALU.is_equal))
                if last:
                    dve.tensor_tensor(one[:], one[:], e3(valid[:]), ALU.mult).then_inc(masked, 1)
                    dve.wait_ge(masked, 1)
                for t in range(T4):
                    dve.tensor_tensor(before[:, t + 1, :], before[:, t, :], one[:, t, :], ALU.add).then_inc(hot_done, 1)
                    dve.wait_ge(hot_done, 4 * g + t + 1)
                dve.wait_ge(r_made, g + 1)
                then(dve.tensor_tensor(rk[:], psr[:, 0:T4, :], cnt[:].unsqueeze(1).to_broadcast([P, T4, EXPERTS]), ALU.add))
                dve.tensor_tensor(rk[:], rk[:], cap0[:].unsqueeze(1).to_broadcast([P, T4, EXPERTS]), ALU.add).then_inc(rk_s, 1)
                dve.wait_ge(rk_s, 2 * g + 1)
                dve.tensor_tensor(rk[:], rk[:], one[:], ALU.mult).then_inc(rk_s, 1)
                dve.tensor_tensor(cnt[:], cnt[:], psr[:, T4, :], ALU.add)
                dve.wait_ge(rk_s, 2 * g + 2)
                dve.tensor_reduce(posf[:], rk[:], AX.X, ALU.add).then_inc(pf_done, 1)
                dve.tensor_scalar(rowbase[:], rowbase[:], float(GROUP), None, ALU.add)
                dve.wait_ge(pf_done, g + 1)
                if last:
                    dve.tensor_tensor(posf[:], posf[:], invalid[:], ALU.add).then_inc(masked, 1)
                    dve.wait_ge(masked, 2)
                dve.tensor_copy(posi[:, b, :], posf[:]).then_inc(pos_done, 1)
                assert n[0] == RT, n

            dve.memset(rowbase[:], 0.0)
            node(0, 0, 0)
            node(1, 1, 0)
            route(0, 0)
            with dve.Fori(1, (GROUPS - 1) // 2) as i:
                node(2 * i, 0, i)
                route(2 * i - 1, 1)
                node(2 * i + 1, 1, i)
                route(2 * i, 0)
            k = (GROUPS - 1) // 2
            node(2 * k, 0, k)
            route(2 * k - 1, 1)
            dve.wait_ge(pos_done, GROUPS - 1)
            dve.memset(rowbase[:], float(LAST0)).then_inc(masked2, 1)
            dve.wait_ge(masked2, 1)
            route(2 * k, 0, last=True)
            q = [0]

            def then(ins):
                q[0] += 1
                ins.then_inc(tstep, 1)
                dve.wait_ge(tstep, q[0])
            then(dve.tensor_scalar(nti[:], cnt[:], float(P - 1), None, ALU.add))
            then(dve.tensor_scalar(nti[:], nti[:], 7, None, ALU.arith_shift_right))
            then(dve.tensor_copy(ntf[:], nti[:]))
            then(dve.memset(w[:, 0, :], 1.0))
            then(dve.tensor_tensor_scan(w[:, 1, :], w[:, 0, :], ntf[:], 0.0, ALU.mult, ALU.add))
            then(dve.tensor_tensor(w[:, 2, :], w[:, 1, :], ntf[:], ALU.subtract))
            then(dve.tensor_scalar(w[:, 3, :], w[:, 1, :], pid[:, 0:1], None, ALU.is_gt))
            then(dve.tensor_scalar(w[:, 4, :], w[:, 2, :], pid[:, 0:1], None, ALU.is_le))
            then(dve.tensor_tensor(w[:, 3, :], w[:, 3, :], w[:, 4, :], ALU.mult))
            then(dve.tensor_scalar(w[:, 4, :], w[:, 2, :], -float(P), j128[:, 0:1], ALU.mult, ALU.add))
            then(dve.tensor_tensor(w[:, 4, :], w[:, 4, :], cap0[:], ALU.add))
            then(dve.tensor_tensor(w[:, 4, :], w[:, 4, :], w[:, 3, :], ALU.mult))
            then(dve.tensor_scalar(w[:, 5, :], prio[:], -1.0, float(EXPERTS), ALU.mult, ALU.add))
            then(dve.tensor_tensor(w[:, 5, :], w[:, 5, :], w[:, 3, :], ALU.mult))
            then(dve.tensor_reduce(red[:, 0:1], w[:, 3, :], AX.X, ALU.add))
            then(dve.tensor_reduce(red[:, 1:2], w[:, 4, :], AX.X, ALU.add))
            then(dve.tensor_reduce(et[:, 1:2], w[:, 5, :], AX.X, ALU.add))
            then(dve.tensor_scalar(red[:, 2:3], red[:, 0:1], -float(EXPERTS * CAP), float(EXPERTS * CAP), ALU.mult, ALU.add))
            then(dve.tensor_tensor(et[:, 0:1], red[:, 1:2], red[:, 2:3], ALU.add))
            then(dve.tensor_copy(eti[:], et[:]))
            then(dve.tensor_tensor(w[:, 0, :], cnt[:], cap0[:], ALU.add))
            then(dve.tensor_scalar(padpos[:], w[:, 0, :], pid[:, 0:1], None, ALU.add))
            dve.tensor_copy(red[:, 3:4], red[:, 0:1]).then_inc(tabs, 1)

        @block.scalar
        def _(act):
            act.wait_ge(wload, 7 * 16)

            def elu(g):
                act.wait_ge(neg_done, g + 1)
                act.activation(eneg[:], neg[:], ACT.Exp).then_inc(eneg_done, 1)

            def softmax(g):
                act.wait_ge(lm_done, g + 1)
                act.activation(ex[:], lg[:], ACT.Exp).then_inc(ex_done, 1)

            def hidden(g):
                act.wait_ge(xT, g + 1)
                act.copy(x2T[:], psx[:]).then_inc(xT_copied, 1)
                for c in range(HC):
                    act.wait_ge(h_made, HC * g + c + 1)
                    act.activation(H[:, c, :], psh[:, c % 2, :], ACT.Gelu, bias=b1c[:, c:c + 1]).then_inc(gelu_done, 1)
            elu(0)
            with act.Fori(0, (GROUPS - 1) // 2) as i:
                for b in range(2):
                    hidden(2 * i + b)
                    elu(2 * i + b + 1)
                    softmax(2 * i + b)
            hidden(GROUPS - 1)
            softmax(GROUPS - 1)

        @block.tensor
        def _(pe):
            pe.wait_ge(consts, 9)
            pe.wait_ge(wload, 7 * 16)

            def step(g):
                pe.wait_ge(x2_done, g + 1)
                for h in range(2):
                    for t in range(T4):
                        last = pe.transpose(psx[:, h, P * t:P * t + P], x2n[:, t, P * h:P * h + P], ident[:])
                last.then_inc(xT, 1)
                pe.wait_ge(xT_copied, g + 1)
                for c in range(HC):
                    if not (isinstance(g, int) and g == 0 and c < 2):
                        pe.wait_ge(gelu_done, HC * g + c - 1)
                    pe.matmul(psh[:, c % 2, :], w1[:, 0, P * c:P * c + P], x2T[:, 0, :], start=True, stop=False)
                    pe.matmul(psh[:, c % 2, :], w1[:, 1, P * c:P * c + P], x2T[:, 1, :], start=False, stop=True).then_inc(h_made, 1)
                pe.wait_ge(gelu_done, HC * g + HC)
                for t in range(T4):
                    for c in range(HC):
                        last = pe.matmul(psl[:, t, :], H[:, c, P * t:P * t + P], wg[:, c, :], start=c == 0, stop=c == HC - 1)
                last.then_inc(l_made, 1)
                pe.wait_ge(hot_done, 4 * g + 4)
                flat = lambda v: v.rearrange("p t e -> p (t e)")
                pe.matmul(flat(psr[:, 0:T4, :]), tri[:], flat(one[:]), start=True, stop=False, skip_group_check=True)
                pe.matmul(flat(psr[:, 0:T4, :]), ones[:], flat(before[:, 0:T4, :]), start=False, stop=True, skip_group_check=True)
                pe.matmul(psr[:, T4, :], ones[:], before[:, T4, :], start=True, stop=True, skip_group_check=True).then_inc(r_made, 1)
            step(0)
            with pe.Fori(0, (GROUPS - 1) // 2) as i:
                step(2 * i + 1)
                step(2 * i + 2)


def experts(nc, W1, b1, Wd, bd, routed_d, etab_d, out):
    with ExitStack() as ctx:
        sb = lambda n, s, d=F32: ctx.enter_context(nc.sbuf_tensor(n, s, d))
        ps = lambda n, s, d=F32: ctx.enter_context(nc.psum_tensor(n, s, d))
        sem = lambda n: ctx.enter_context(nc.semaphore(n))
        ring = lambda n: [sem(f"{n}{r}") for r in range(RING)]
        wd = sb("wd", [P, EXPERTS, HC, D]); bdr = sb("bdr", [P, EXPERTS, D]); w1 = sb("x_w1", [P, 2, HID]); b1c = sb("x_b1c", [P, HC])
        row = sb("x_row", [P, RING, RW]); x2 = sb("x_x2", [P, D]); x2T = sb("x_x2T", [P, 2, P]); H = sb("x_H", [P, RING, HC, P])
        y = sb("x_y", [P, RING, D]); res = sb("x_res", [P, RING, D]); node = sb("x_node", [P, RING, 1], I32)
        ident = sb("x_ident", [P, P]); ones = sb("x_ones", [P, P]); tab = sb("x_tab", [1, 2, ETILES], I32)
        psx = ps("x_psx", [P, 2, 256]); psh = ps("x_psh", [P, 2, 512]); psy = ps("x_psy", [P, 3, 512])
        cz = sem("x_cz"); consts = sem("x_consts"); wload = sem("x_wload"); row_in = ring("row_in"); x2_done = sem("x_x2_done"); xT = sem("x_xT"); xT_copied = sem("x_xT_copied")
        h_made = sem("x_h_made"); gelu = sem("x_gelu"); y_made = sem("x_y_made"); y1 = sem("x_y1"); res_done = sem("x_res"); stored = ring("x_stored"); passed = sem("x_passed")
        block = ctx.enter_context(nc.Block())
        one = lambda t: slice(t, t + 1) if isinstance(t, int) else bass.ds(t, 1)

        def run(eng, step):
            for t in range(RING):
                step(t, t, 0)
            with eng.Fori(1, ETILES // RING) as i:
                for r in range(RING):
                    step(RING * i + r, r, i)

        @block.sync
        def _(sp):
            sp.dma_start(tab[:], etab_d[None, :, :]).then_inc(wload, 16)
            sp.dma_start(w1[:], W1.rearrange("(k p) c -> p k c", p=P)).then_inc(wload, 16)
            with nc.allow_non_contiguous_dma(reason="bias by hidden unit"):
                sp.dma_start(b1c[:], b1.rearrange("(k p) -> p k", p=P)).then_inc(wload, 16)
            sp.dma_start(bdr[:], bd.rearrange("(o e) d -> o e d", o=1).to_broadcast([P, EXPERTS, D])).then_inc(wload, 16)
            for e in range(EXPERTS):
                sp.dma_start(wd[:, e, :, :], Wd[e, :, :].rearrange("(k p) c -> p k c", p=P)).then_inc(wload, 16)
            sp.wait_ge(wload, 16 * 12)

            def step(t, r, u):
                first = sp.value_load(tab[0:1, 0, one(t)], min_val=0, max_val=ROUTED - P)
                if not (isinstance(u, int) and u == 0):
                    sp.wait_ge(res_done, t - 2)
                    sp.sem_inc(passed, 1)
                sp.dma_start(row[:, r, :], routed_d[bass.ds(first, P), :]).then_inc(row_in[r], 16)
            run(sp, step)

        @block.gpsimd
        def _(pool):
            pool.memset(ones[:], 1.0).then_inc(cz, 1)
            pool.wait_ge(cz, 1)
            pool.affine_select(out=ident[:], in_=ones[:], compare_op=ALU.is_equal, fill=0.0, base=0, pattern=[[-1, P]], channel_multiplier=1).then_inc(consts, 1)

            def step(t, r, u):
                pool.wait_ge(res_done, t + 1)
                pool.sem_inc(passed, 1)
                pool.indirect_dma_start(out[:, :], bass.IndirectOffsetOnAxis(node[:, r, :], 0), res[:, r, :], None, bounds_check=NODES - 1, oob_is_err=False).then_inc(stored[r], 16)
            run(pool, step)
            for r in range(RING):
                pool.wait_ge(stored[r], 16 * (ETILES // RING))

        @block.vector
        def _(dve):
            def normal(t, r, u):
                dve.wait_ge(row_in[r], 16 * (u + 1))
                if not (isinstance(t, int) and t == 0):
                    dve.wait_ge(xT, t)
                dve.tensor_scalar(x2[:], row[:, r, 0:D], row[:, r, D:D + 1], row[:, r, D + 1:D + 2], ALU.subtract, ALU.mult).then_inc(x2_done, 1)

            def finish(t, r, u):
                e = dve.value_load(tab[0:1, 1, one(t)], min_val=0, max_val=EXPERTS - 1)
                dve.wait_ge(y_made, t + 1)
                dve.sem_inc(passed, 1)
                dve.tensor_tensor(y[:, r, :], psy[:, r, 0:D], bdr[:, one2(e), :].rearrange("p o d -> p (o d)"), ALU.add).then_inc(y1, 1)
                if not (isinstance(u, int) and u == 0):
                    dve.wait_ge(stored[r], 16 * u)
                dve.tensor_copy(node[:, r, :], row[:, r, D + 3:D + 4])
                dve.wait_ge(y1, t + 1)
                dve.scalar_tensor_tensor(out=res[:, r, :], in0=y[:, r, :], scalar=row[:, r, D + 2:D + 3], in1=row[:, r, 0:D], op0=ALU.mult, op1=ALU.add).then_inc(res_done, 1)
            one2 = lambda e: bass.ds(e, 1)
            dve.wait_ge(wload, 16 * 12)
            normal(0, 0, 0)
            for t in range(RING):
                normal(t + 1, (t + 1) % RING, (t + 1) // RING)
                finish(t, t, 0)
            with dve.Fori(1, ETILES // RING - 1) as i:
                for r in range(RING):
                    normal(RING * i + r + 1, (r + 1) % RING, i + (r + 1) // RING)
                    finish(RING * i + r, r, i)
            for t in range(ETILES - RING, ETILES):
                if t + 1 < ETILES:
                    normal(t + 1, (t + 1) % RING, (t + 1) // RING)
                finish(t, t % RING, t // RING)

        @block.scalar
        def _(act):
            act.wait_ge(wload, 16 * 12)

            def step(t, r, u):
                act.wait_ge(xT, t + 1)
                act.copy(x2T[:], psx[:, :, 0:P]).then_inc(xT_copied, 1)
                for c in range(HC):
                    act.wait_ge(h_made, HC * t + c + 1)
                    act.activation(H[:, r, c, :], psh[:, c % 2, 0:P], ACT.Gelu, bias=b1c[:, c:c + 1]).then_inc(gelu, 1)
            run(act, step)

        @block.tensor
        def _(pe):
            pe.wait_ge(wload, 16 * 12)
            pe.wait_ge(consts, 1)

            def down(t, r):
                e = pe.value_load(tab[0:1, 1, one(t)], min_val=0, max_val=EXPERTS - 1)
                pe.wait_ge(gelu, HC * t + HC)
                if not (isinstance(t, int) and t < 3):
                    pe.wait_ge(y1, t - 2)
                pe.sem_inc(passed, 1)
                for c in range(HC):
                    last = pe.matmul(psy[:, r, 0:D], H[:, r, c, :], wd[:, bass.ds(e, 1), c, :].rearrange("p o d -> p (o d)"), start=c == 0, stop=c == HC - 1)
                last.then_inc(y_made, 1)

            def up(t, r, first=False):
                pe.wait_ge(x2_done, t + 1)
                for h in range(2):
                    last = pe.transpose(psx[:, h, 0:P], x2[:, P * h:P * h + P], ident[:])
                last.then_inc(xT, 1)
                pe.wait_ge(xT_copied, t + 1)
                for c in range(HC):
                    if not (first and c < 2):
                        pe.wait_ge(gelu, HC * t + c - 1)
                    pe.matmul(psh[:, c % 2, 0:P], w1[:, 0, P * c:P * c + P], x2T[:, 0, :], start=True, stop=False)
                    pe.matmul(psh[:, c % 2, 0:P], w1[:, 1, P * c:P * c + P], x2T[:, 1, :], start=False, stop=True).then_inc(h_made, 1)
            up(0, 0, True)
            up(1, 1); down(0, 0)
            up(2, 2); down(1, 1)
            with pe.Fori(1, ETILES // RING) as i:
                for r in range(RING):
                    up(RING * i + r, r)
                    down(RING * i + r - 1, (r + 2) % RING)
            down(ETILES - 1, 2)


_INS = ['x', 'src', 'dst', 'L0_gnn_Wl', 'L0_gnn_bl', 'L0_gnn_Wr', 'L0_gnn_br', 'L0_gnn_att', 'L0_gnn_bias', 'L0_gnn_gamma',
        'L0_gnn_beta', 'L0_ffn_W1', 'L0_ffn_b1', 'L0_ffn_Wg', 'L0_ffn_bg', 'L0_ffn_Wd', 'L0_ffn_bd']


def program(nc, i, out):
    scratch = lambda name, shape, dt=F32: nc.dram_tensor(name, shape, dt).ap()
    xn_d = scratch("xn_d", (NODES, D))
    xl_d = scratch("xl_d", (NODES, XW))
    xr_d = scratch("xr_d", (NODES_UP, XW))
    st_d = scratch("st_d", (NODES_UP, SW))
    src_pad = scratch("src_pad", (PADDED,), I32)
    dst_pad = scratch("dst_pad", (PADDED,), I32)
    rows_d = scratch("rows_d", (3, BLOCKS))
    tabf_d = scratch("tabf_d", (BLOCKS + EXTRA,))
    tabi_d = scratch("tabi_d", (2, BLOCKS + EXTRA + 1), I32)
    routed_d = scratch("routed_d", (ROUTED, RW))
    etab_d = scratch("etab_d", (2, ETILES), I32)
    project(nc, i['x'], i['L0_gnn_Wl'], i['L0_gnn_Wr'], i['L0_gnn_bl'], i['L0_gnn_br'], i['L0_gnn_att'], xn_d, xl_d, xr_d)
    setup(nc, i['src'], i['dst'], src_pad, dst_pad, xr_d, st_d, rows_d, tabf_d, tabi_d)
    edges(nc, i['L0_gnn_att'], xl_d, xr_d, src_pad, dst_pad, st_d, tabf_d, tabi_d)
    nodes(nc, i['x'], i['L0_gnn_bias'], i['L0_gnn_gamma'], i['L0_gnn_beta'], i['L0_ffn_W1'], i['L0_ffn_b1'], i['L0_ffn_Wg'],
          i['L0_ffn_bg'], xn_d, st_d, routed_d, etab_d)
    experts(nc, i['L0_ffn_W1'], i['L0_ffn_b1'], i['L0_ffn_Wd'], i['L0_ffn_bd'], routed_d, etab_d, out)


def kernel(**inputs):
    import numpy as _np
    import concourse.bacc as _bacc
    from concourse.bass_utils import run_bass_kernel_spmd as _run

    nc = _bacc.Bacc("TRN2", target_bir_lowering=False, num_devices=1)
    arrays, aps = {}, {}
    for name in _INS:
        a = _np.ascontiguousarray(inputs[name])
        arrays[f"in_{name}_dram"] = a
        aps[name] = nc.dram_tensor(f"in_{name}_dram", a.shape, mybir.dt.from_np(a.dtype), kind="ExternalInput").ap()
    out = nc.dram_tensor("out_0_dram", (NODES, D), F32, kind="ExternalOutput").ap()
    program(nc, aps, out)
    r = _run(nc, [arrays], core_ids=[0])
    return r.results[0]["out_0_dram"]
```

```python
from contextlib import ExitStack
import concourse.bass as bass
from concourse import mybir

P = 128
F32 = mybir.dt.float32
F32R = mybir.dt.float32r
BF16 = mybir.dt.bfloat16
I32 = mybir.dt.int32
ALU = mybir.AluOpType
ACT = mybir.ActivationFunctionType
AX = mybir.AxisListType
EPS = 1e-5
NEG = -1e30
NODES, EDGES, D = 12500, 200000, 256
HEADS, HD = 8, 32
HS = HD + 1
C = 12
BLOCK = P * C
RING = 3
BLOCKS = -(-(-(-EDGES // BLOCK)) // RING) * RING
PADDED = BLOCKS * BLOCK
NODES_UP = (NODES // P + 2) * P
EXTRA = -(-(NODES // P) // RING) * RING
FAR = 20000
G = 3
SW = HEADS * HS + HEADS
XW = D + HEADS


def setup(nc, src, dst, src_pad, dst_pad, xr_d, st_d, rows_d, tabf_d, tabi_d):
    with ExitStack() as ctx:
        sb = lambda n, s, d=F32: ctx.enter_context(nc.sbuf_tensor(n, s, d))
        sem = lambda n: ctx.enter_context(nc.semaphore(n))
        tail = PADDED - EDGES
        tp = 64
        far = sb("far", [tp, tail // tp], I32); nil = sb("nil", [tp, tail // tp], I32)
        zx = sb("zx", [P, XW]); st0 = sb("st0", [P, SW])
        fi = sb("fi", [1, 2, BLOCKS], I32); ff = sb("ff", [1, 2, BLOCKS])
        sp_f = sb("sp_f", [1, BLOCKS]); sp_i = sb("sp_i", [1, BLOCKS], I32); sh_i = sb("sh_i", [1, BLOCKS], I32)
        rows = sb("rows", [1, 3, BLOCKS]); inc = sb("inc", [1, BLOCKS]); one = sb("one", [1, BLOCKS])
        bc = sb("bc", [EXTRA, 3, BLOCKS]); m1 = sb("m1", [EXTRA, BLOCKS]); m2 = sb("m2", [EXTRA, BLOCKS]); m3 = sb("m3", [EXTRA, BLOCKS])
        siota = sb("siota", [EXTRA, BLOCKS]); j = sb("j", [EXTRA, 1]); j128 = sb("j128", [EXTRA, 1])
        red = sb("red", [EXTRA, 3]); res = sb("res", [EXTRA, 2]); resi = sb("resi", [EXTRA, 2], I32)
        firsti = sb("firsti", [1, BLOCKS], I32); tot = sb("tot", [1, 1]); toti = sb("toti", [1, 1], I32); tmp = sb("tmp", [EXTRA, 1])
        made = sem("setup_made"); filled = sem("filled"); loaded = sem("loaded"); v = sem("table_step"); wrote = sem("table_rows"); back = sem("rows_back"); done = sem("tables_stored"); io = sem("setup_iota")
        block = ctx.enter_context(nc.Block())

        @block.gpsimd
        def _(pool):
            pool.iota(siota[:], [[1, BLOCKS]], base=0, channel_multiplier=0, allow_small_or_imprecise_dtypes=True).then_inc(io, 1)
            pool.iota(j[:], [[0, 1]], base=0, channel_multiplier=1, allow_small_or_imprecise_dtypes=True).then_inc(io, 1)
            pool.iota(j128[:], [[0, 1]], base=P, channel_multiplier=P, allow_small_or_imprecise_dtypes=True).then_inc(io, 1)

        @block.sync
        def _(sp):
            sp.dma_start(dst_pad[0:EDGES].rearrange("(a b) -> a b", a=125), dst.rearrange("(a b) -> a b", a=125)).then_inc(filled, 16)
            sp.dma_start(src_pad[0:EDGES].rearrange("(a b) -> a b", a=125), src.rearrange("(a b) -> a b", a=125)).then_inc(filled, 16)
            sp.wait_ge(made, 4)
            sp.dma_start(dst_pad[EDGES:PADDED].rearrange("(a b) -> a b", a=tp), far[:]).then_inc(filled, 16)
            sp.dma_start(src_pad[EDGES:PADDED].rearrange("(a b) -> a b", a=tp), nil[:]).then_inc(filled, 16)
            sp.dma_start(xr_d[NODES:NODES + P, :], zx[:]).then_inc(filled, 16)
            sp.dma_start(xr_d[NODES + P:NODES_UP, :], zx[0:NODES_UP - NODES - P, :]).then_inc(filled, 16)
            sp.dma_start(st_d.rearrange("(t p) c -> p t c", p=P), st0[:].rearrange("p (o c) -> p o c", o=1).to_broadcast([P, NODES_UP // P, SW])).then_inc(filled, 16)
            sp.wait_ge(filled, 7 * 16)
            ends = dst_pad.rearrange("(o s e) -> o s e", o=1, e=BLOCK)
            with nc.allow_non_contiguous_dma(reason="one destination of each block"):
                sp.dma_start(fi[:, 0, :], ends[:, :, 0]).then_inc(loaded, 16)
                sp.dma_start(fi[:, 1, :], ends[:, :, BLOCK - 1]).then_inc(loaded, 16)
            sp.wait_ge(v, 8)
            sp.dma_start(rows_d[None, :, :], rows[:]).then_inc(wrote, 16)
            sp.dma_start(tabf_d[None, 0:BLOCKS], rows[:, 2, :]).then_inc(done, 16)
            sp.dma_start(tabi_d[None, 0, 0:BLOCKS], firsti[:]).then_inc(done, 16)
            sp.dma_start(tabi_d[None, 1, BLOCKS + EXTRA:BLOCKS + EXTRA + 1], toti[:]).then_inc(done, 16)
            sp.wait_ge(wrote, 16)
            sp.dma_start(bc[:], rows_d[None, :, :].to_broadcast([EXTRA, 3, BLOCKS])).then_inc(back, 16)
            sp.wait_ge(v, 21)
            with nc.allow_non_contiguous_dma(reason="a table row"):
                sp.dma_start(tabf_d[BLOCKS:BLOCKS + EXTRA, None], res[:, 0:1]).then_inc(done, 16)
                sp.dma_start(tabi_d[0, BLOCKS:BLOCKS + EXTRA, None], resi[:, 0:1]).then_inc(done, 16)
                sp.dma_start(tabi_d[1, BLOCKS:BLOCKS + EXTRA, None], resi[:, 1:2]).then_inc(done, 16)
            sp.wait_ge(done, 6 * 16)

        @block.vector
        def _(dve):
            dve.memset(far[:], FAR).then_inc(made, 1)
            dve.memset(nil[:], 0).then_inc(made, 1)
            dve.memset(zx[:], 0.0).then_inc(made, 1)
            dve.memset(one[:], 1.0)
            dve.memset(st0[:, 0:HEADS * HS], 0.0)
            dve.memset(st0[:, HEADS * HS:SW], NEG).then_inc(made, 1)
            dve.wait_ge(loaded, 32)
            n = [0]

            def then(ins):
                n[0] += 1
                ins.then_inc(v, 1)
                dve.wait_ge(v, n[0])
            then(dve.tensor_scalar(ff[:, 0, :], fi[:, 0, :], float(NODES), None, ALU.min))
            then(dve.tensor_scalar(ff[:, 1, :], fi[:, 1, :], float(NODES - 1), None, ALU.min))
            then(dve.tensor_tensor(sp_f[:], ff[:, 1, :], ff[:, 0, :], ALU.subtract))
            then(dve.tensor_scalar(sp_i[:], sp_f[:], 0.0, None, ALU.max))
            then(dve.tensor_scalar(sh_i[:], sp_i[:], 7, None, ALU.arith_shift_right))
            dve.tensor_copy(firsti[:], ff[:, 0, :])
            dve.tensor_copy(rows[:, 2, :], ff[:, 0, :])
            then(dve.tensor_copy(rows[:, 1, :], sh_i[:]))
            then(dve.tensor_tensor_scan(inc[:], one[:], rows[:, 1, :], 0.0, ALU.mult, ALU.add))
            dve.tensor_copy(toti[:], inc[:, BLOCKS - 1:BLOCKS])
            then(dve.tensor_tensor(rows[:, 0, :], inc[:], rows[:, 1, :], ALU.subtract))
            dve.wait_ge(back, 16)
            dve.wait_ge(io, 3)
            then(dve.tensor_scalar(m1[:], bc[:, 0, :], j[:, 0:1], None, ALU.is_le))
            then(dve.tensor_tensor(m2[:], bc[:, 0, :], bc[:, 1, :], ALU.add))
            then(dve.tensor_scalar(m3[:], m2[:], j[:, 0:1], None, ALU.is_gt))
            then(dve.tensor_tensor(m1[:], m1[:], m3[:], ALU.mult))
            then(dve.tensor_scalar(m2[:], bc[:, 0, :], -float(P), j128[:, 0:1], ALU.mult, ALU.add))
            then(dve.tensor_tensor(m2[:], m2[:], bc[:, 2, :], ALU.add))
            then(dve.tensor_tensor(m2[:], m2[:], m1[:], ALU.mult))
            then(dve.tensor_tensor(m3[:], siota[:], m1[:], ALU.mult))
            dve.tensor_reduce(red[:, 0:1], m2[:], AX.X, ALU.add)
            dve.tensor_reduce(red[:, 1:2], m3[:], AX.X, ALU.add)
            then(dve.tensor_reduce(red[:, 2:3], m1[:], AX.X, ALU.add))
            then(dve.tensor_scalar(tmp[:], red[:, 2:3], -float(NODES), float(NODES), ALU.mult, ALU.add))
            dve.tensor_copy(res[:, 1:2], red[:, 1:2])
            then(dve.tensor_tensor(res[:, 0:1], red[:, 0:1], tmp[:], ALU.add))
            then(dve.tensor_copy(resi[:], res[:]))
            then(dve.tensor_copy(tmp[:], res[:, 0:1]))


def edges(nc, att, xl_d, xr_d, src_pad, dst_pad, st_d, tabf_d, tabi_d):
    with ExitStack() as ctx:
        sb = lambda n, s, d=F32: ctx.enter_context(nc.sbuf_tensor(n, s, d))
        ps = lambda n, s, d=F32: ctx.enter_context(nc.psum_tensor(n, s, d))
        sem = lambda n: ctx.enter_context(nc.semaphore(n))
        ring = lambda n: [sem(f"{n}{r}") for r in range(RING)]
        idx = sb("idx", [P, RING, C], I32); dsti = sb("dsti", [P, RING, C], I32); base = sb("base", [P, RING, 1])
        xrw = sb("xrw", [P, RING, XW]); xrp = sb("xrp", [P, RING, 2, D], F32R); xl = sb("xl", [P, RING, C, XW]); px = sb("px", [P, RING, C, HEADS, HS])
        dst8 = sb("dst8", [P, RING, C, HEADS]); rel = sb("rel", [P, RING, C])
        hot = sb("hot", [P, RING, C, P], F32R); hotT = sb("hotT", [P, RING, C * P], F32R)
        s = sb("s", [P, 2, 512 * 3])
        att_sb = sb("att_sb", [P, 2, HEADS])
        e_sb = sb("e_sb", [P, RING, C, HEADS])
        dts = sb("dts", [C * HEADS, P]); reset = sb("reset", [C * HEADS, P + 1]); runmax = sb("runmax", [C * HEADS, P]); lastmax = sb("lastmax", [C * HEADS, P])
        rh = sb("rh", [P, C, 2, HEADS + 1], F32R); mh = sb("mh", [P, 3, HEADS], BF16); mrest = sb("mrest", [P, HEADS]); hotTb = sb("hotTb", [P, RING, C * P], BF16); vsum = sb("vsum", [P, C, HEADS]); mback = sb("mback", [P, C * HEADS]); pen = sb("pen", [P, C]); vs = sb("vs", [P, C, HEADS])
        mraw = sb("mraw", [P, HEADS]); m = sb("m", [P, RING, 2 * HEADS]); d = sb("d", [P, C, HEADS]); dm = sb("dm", [P, C, HEADS])
        st = sb("st", [P, RING, SW]); new = sb("new", [P, RING, SW]); mn = sb("mn", [P, HEADS]); dd = sb("dd", [P, 2, HEADS]); ab = sb("ab", [P, 2, HEADS])
        t2 = sb("t2", [P, HEADS * HS]); one_zero = sb("one_zero", [P, C, 2])
        ident = sb("ident2", [P, P]); identr = sb("identr", [P, P], F32R); ones = sb("ones2", [P, P]); iota = sb("iota2", [P, P])
        tab = sb("tab", [1, 2, BLOCKS + EXTRA + 1], I32)
        psz = ps("psz", [P, 2, 512]); psot = ps("psot", [P, G, 512], F32R); pss = ps("pss", [P, 512]); psv = ps("psv", [P, 512]); psa = ps("psa", [P, 512])
        ps_e = pss[:, 0:96]
        ps_et = psv[0:96, 0:128]; ps_dt = psv[0:96, 128:256]; ps_fm = psv[:, 256:352]
        ps_v = psv[:, 0:C * 2 * (HEADS + 1)].rearrange("p (c s h) -> p c s h", c=C, s=2); ps_m = psv[:, 0:C * 3 * HEADS].rearrange("p (c s h) -> p c s h", c=C, s=3)
        idx_in = ring("idx_in"); win_in = ring("win_in"); st_in = ring("st_in"); xl_in = ring("xl_in"); stored = ring("stored")
        sp_passed = sem("sp_passed"); pool_passed = sem("pool_passed")
        consts = sem("consts2"); cz = sem("cz2"); oz = sem("oz"); attin = sem("attin")
        hot_made = sem("hot_made"); ot_tr = sem("ot_tr"); ot_copied = sem("ot_copied"); z_made = sem("z_made"); s_made = sem("s_made"); e_made = sem("e_made"); e_copied = sem("e_copied")
        rel_made = sem("rel_made"); xh_made = sem("xh_made"); xrp_made = sem("xrp_made")
        et_made = sem("et_made"); dts_made = sem("dts_made"); reset_made = sem("reset_made"); run_made = sem("run_made"); fm_made = sem("fm_made"); fmt_made = sem("fmt_made"); rh_made = sem("rh_made"); rl_made = sem("rl_made"); mh_made = sem("mh_made"); mrest_made = sem("mrest_made"); mm_made = sem("mm_made"); ml_made = sem("ml_made"); mback_made = sem("mback_made"); vsum_made = sem("vsum_made"); otb_copied = sem("otb_copied")
        v_made = sem("v_made"); pen_made = sem("pen_made"); vs_made = sem("vs_made"); m_made = sem("m_made"); mraw_made = sem("mraw_made"); me_made = sem("me_made"); d_made = sem("d_made"); dm_made = sem("dm_made"); p_made = sem("p_made"); px_made = sem("px_made")
        a_made = sem("a_made"); mn_made = sem("mn_made"); dd_made = sem("dd_made"); ab_made = sem("ab_made"); new_part = sem("new_part"); t2_made = sem("t2_made"); new_made = sem("new_made")
        block = ctx.enter_context(nc.Block())

        def pipeline(eng, slot, first_hot, k0, n):
            first_hot(k0, 0, k0 // RING)
            for k in range(3):
                slot(k0 + k, k, (k0 + k) // RING, a=True, b=k >= 1, c=k >= 2)
            with eng.Fori(1, n // RING - 1) as i:
                for r in range(RING):
                    slot(k0 + RING * i + r, r, i + k0 // RING, a=True, b=True, c=True)
            kk = k0 + n - RING
            for r in range(RING):
                slot(kk + r, r, kk // RING, a=True, b=True, c=True, ahead=r < 2)
            slot(k0 + n, 0, (k0 + n) // RING, a=False, b=True, c=True)
            slot(k0 + n + 1, 1, (k0 + n) // RING, a=False, b=False, c=True)

        @block.sync
        def _(sp):
            sp.wait_ge(consts, 4)
            sp.dma_start(tab[:, 0, 0:BLOCKS + EXTRA], tabi_d[None, 0, 0:BLOCKS + EXTRA]).then_inc(attin, 16)
            sp.dma_start(tab[:, 1, BLOCKS:], tabi_d[None, 1, BLOCKS:]).then_inc(attin, 16)
            with nc.allow_non_contiguous_dma(reason="attention weights by feature"):
                for h in range(HEADS):
                    p0 = h % 4 * HD
                    sp.dma_start(att_sb[p0:p0 + HD, h // 4, h:h + 1], att[h, :, None]).then_inc(attin, 16)
            sp.wait_ge(attin, 16 * 10)
            W = tab[0:1, 0, :]
            B = tab[0:1, 1, :]
            srcv = src_pad.rearrange("(s p j) -> s p j", p=P, j=C)
            dstv = dst_pad.rearrange("(s p j) -> s p j", p=P, j=C)
            one = lambda x: slice(x, x + 1) if isinstance(x, int) else bass.ds(x, 1)
            rows = lambda w: bass.ds(w, P)

            def which(k, extra):
                if not extra:
                    return k
                return sp.value_load(B[:, one(k)], min_val=0, max_val=BLOCKS - 1)

            def window(k):
                return sp.value_load(W[:, one(k)], min_val=0, max_val=NODES)

            def load_idx(k, r, extra):
                sp.dma_start(idx[:, r, :], srcv[one(which(k, extra)), :, :].rearrange("o p j -> p (o j)")).then_inc(idx_in[r], 16)

            def load_window(k, r, extra):
                sp.dma_start(dsti[:, r, :], dstv[one(which(k, extra)), :, :].rearrange("o p j -> p (o j)")).then_inc(win_in[r], 16)
                sp.dma_start(base[:, r, :], tabf_d[one(k)].rearrange("(o k) -> o k", o=1).to_broadcast([P, 1])).then_inc(win_in[r], 16)
                sp.dma_start(xrw[:, r, :], xr_d[rows(window(k)), :]).then_inc(win_in[r], 16)

            def load_state(k, r):
                sp.dma_start(st[:, r, :], st_d[rows(window(k)), :]).then_inc(st_in[r], 16)

            def settle():
                sp.sem_inc(sp_passed, 1)

            def run(k0, n, extra):
                for k in range(3):
                    load_idx(k0 + k, k, extra)
                for k in range(2):
                    load_window(k0 + k, k, extra)
                load_state(k0, 0)

                def slot(k, r, u, a, b, c, ahead_idx=True, ahead_win=True):
                    if ahead_idx:
                        sp.wait_ge(xl_in[r], 16 * C * (u + 1))
                        settle()
                        load_idx(k + 3, r, extra)
                    if ahead_win:
                        q = (r + 2) % RING
                        if not (isinstance(k, int) and k == k0):
                            sp.wait_ge(xrp_made, k)
                            settle()
                            sp.wait_ge(rel_made, 2 * k)
                            settle()
                        load_window(k + 2, q, extra)
                    if c:
                        q = (r + 1) % RING
                        sp.wait_ge(new_made, k - 1)
                        settle()
                        sp.dma_start(st_d[rows(window(k - 2)), :], new[:, q, :]).then_inc(stored[q], 16)
                        sp.wait_ge(stored[q], 16 * (u + 1 if r >= 2 else u))
                        settle()
                    if b:
                        q = (r + 2) % RING
                        if not (isinstance(k, int) and k - 1 == k0):
                            pass
                        load_state(k - 1, q) if not (isinstance(k, int) and k - 1 == k0) else None
                for k in range(3):
                    slot(k0 + k, k, (k0 + k) // RING, True, k >= 1, k >= 2)
                with sp.Fori(1, n // RING - 1) as i:
                    for r in range(RING):
                        slot(k0 + RING * i + r, r, i + k0 // RING, True, True, True)
                kk = k0 + n - RING
                for r in range(RING):
                    slot(kk + r, r, kk // RING, True, True, True, ahead_idx=False, ahead_win=r == 0)
                slot(k0 + n, 0, (k0 + n) // RING, False, True, True, False, False)
                slot(k0 + n + 1, 1, (k0 + n) // RING, False, False, True, False, False)
            run(0, BLOCKS, False)
            if GENERAL:
                more = sp.value_load(B[:, BLOCKS + EXTRA:BLOCKS + EXTRA + 1], min_val=0, max_val=EXTRA)
                with sp.If(more > 0):
                    run(BLOCKS, EXTRA, True)

        @block.gpsimd
        def _(pool):
            pool.memset(ones[:], 1.0).then_inc(cz, 1)
            pool.wait_ge(cz, 1)
            pool.affine_select(out=ident[:], in_=ones[:], compare_op=ALU.is_equal, fill=0.0, base=0, pattern=[[-1, P]], channel_multiplier=1).then_inc(cz, 1)
            pool.iota(iota[:], [[1, P]], base=0, channel_multiplier=0, allow_small_or_imprecise_dtypes=True).then_inc(consts, 1)

            def gathers(k, r, u, free=True):
                pool.wait_ge(idx_in[r], 16 * (u + 1))
                if free:
                    pool.sem_inc(pool_passed, 1)
                    pool.wait_ge(px_made, 2 * (k - 2))
                pool.sem_inc(pool_passed, 1)
                for j in range(C):
                    pool.indirect_dma_start(xl[:, r, j, :], None, xl_d[:, :], bass.IndirectOffsetOnAxis(idx[:, r, j:j + 1], 0),
                                            bounds_check=NODES - 1, oob_is_err=False).then_inc(xl_in[r], 16)

            def run(k0, n):
                for r in range(RING):
                    gathers(k0 + r, r, k0 // RING, free=k0 > 0)
                with pool.Fori(1, n // RING) as i:
                    for r in range(RING):
                        gathers(k0 + RING * i + r, r, i + k0 // RING)
            run(0, BLOCKS)
            if GENERAL:
                pool.wait_ge(attin, 16 * 10)
                more = pool.value_load(tab[0:1, 1, BLOCKS + EXTRA:BLOCKS + EXTRA + 1], min_val=0, max_val=EXTRA)
                with pool.If(more > 0):
                    run(BLOCKS, EXTRA)

        @block.vector
        def _(dve):
            dve.memset(one_zero[:, :, 0:1], 1.0)
            dve.memset(one_zero[:, :, 1:2], 0.0).then_inc(oz, 1)
            dve.wait_ge(oz, 1)
            dve.memset(reset[:, 0:1], 0.0)
            dve.memset(reset[:, P:P + 1], -1.0)
            dve.memset(att_sb[:], 0.0).then_inc(consts, 1)
            dve.tensor_copy(rh[:, :, :, HEADS], one_zero[:]).then_inc(consts, 1)
            dve.wait_ge(cz, 2)
            dve.tensor_copy(identr[:], ident[:]).then_inc(consts, 1)
            dve.wait_ge(consts, 4)

            def make_hot(k, r, u):
                dve.wait_ge(win_in[r], 48 * (u + 1))
                if not (isinstance(k, int) and k < 3):
                    dve.wait_ge(et_made, k - 2)
                if not (isinstance(k, int) and k < 3):
                    dve.wait_ge(z_made, 6 * (k - 2))
                dve.tensor_copy(m[:, r, HEADS:2 * HEADS], xrw[:, r, D:XW])
                dve.tensor_copy(xrp[:, r, 0, :], xrw[:, r, 0:D]).then_inc(xh_made, 1)
                dve.tensor_copy(dst8[:, r, :, :], dsti[:, r, :].unsqueeze(2).to_broadcast([P, C, HEADS])).then_inc(rel_made, 1)
                dve.tensor_scalar(rel[:, r, :], dsti[:, r, :], base[:, r, 0:1], None, ALU.subtract).then_inc(rel_made, 1)
                dve.wait_ge(rel_made, 2 * k + 2)
                dve.wait_ge(xh_made, k + 1)
                dve.tensor_tensor(xrp[:, r, 1, :], xrw[:, r, 0:D], xrp[:, r, 0, :], ALU.subtract).then_inc(xrp_made, 1)
                if not (isinstance(k, int) and k < 3):
                    dve.wait_ge(a_made, k - 2)
                for g in range(G):
                    dve.tensor_tensor(hot[:, r, 4 * g:4 * g + 4, :], iota[:].unsqueeze(1).to_broadcast([P, 4, P]),
                                      rel[:, r, 4 * g:4 * g + 4].unsqueeze(2).to_broadcast([P, 4, P]), ALU.is_equal).then_inc(hot_made, 1)

            def slot(k, r, u, a, b, c, ahead=True):
                qb = (r + 2) % RING
                qc = (r + 1) % RING
                if b:
                    dve.wait_ge(e_made, 3 * k)
                    dve.tensor_tensor(e_sb[:, qb, :, :], xl[:, qb, :, D:XW], ps_e.rearrange("p (c h) -> p c h", h=HEADS), ALU.add).then_inc(e_copied, 1)
                if c:
                    uc = u + 1 if r >= 2 else u
                    dve.wait_ge(st_in[qc], 16 * uc)
                    dve.tensor_tensor(mn[:], st[:, qc, HEADS * HS:SW], m[:, qc, 0:HEADS], ALU.max).then_inc(mn_made, 1)
                    dve.wait_ge(mn_made, k - 1)
                    dve.tensor_tensor(dd[:, 0, :], st[:, qc, HEADS * HS:SW], mn[:], ALU.subtract)
                    dve.tensor_tensor(dd[:, 1, :], m[:, qc, 0:HEADS], mn[:], ALU.subtract).then_inc(dd_made, 1)
                if b:
                    dve.wait_ge(et_made, k)
                    dve.tensor_scalar(dts[:], ps_dt, -NEG, None, ALU.mult).then_inc(dts_made, 1)
                    dve.wait_ge(dts_made, k)
                    dve.tensor_tensor(reset[:, 1:P], dts[:, 0:P - 1], dts[:, 1:P], ALU.subtract).then_inc(reset_made, 1)
                    dve.wait_ge(reset_made, k)
                    dve.tensor_tensor_scan(runmax[:], reset[:, 0:P], ps_et, NEG, ALU.add, ALU.max).then_inc(run_made, 1)
                    dve.wait_ge(run_made, k)
                    dve.scalar_tensor_tensor(out=lastmax[:], in0=reset[:, 1:P + 1], scalar=0.0, in1=runmax[:], op0=ALU.is_lt, op1=ALU.mult).then_inc(fm_made, 1)
                if c:
                    dve.wait_ge(ab_made, k - 1)
                    bro = lambda i: ab[:, i, :].unsqueeze(2).to_broadcast([P, HEADS, HS])
                    hv = lambda x: x.rearrange("p (h f) -> p h f", f=HS)
                    dve.tensor_tensor(hv(new[:, qc, 0:HEADS * HS]), hv(st[:, qc, 0:HEADS * HS]), bro(0), ALU.mult).then_inc(new_part, 1)
                    dve.tensor_copy(new[:, qc, HEADS * HS:SW], mn[:])
                if b:
                    dve.wait_ge(rh_made, k)
                    dve.tensor_tensor(rh[:, :, 1, 0:HEADS], ps_fm.rearrange("p (c h) -> p c h", h=HEADS), rh[:, :, 0, 0:HEADS], ALU.subtract).then_inc(rl_made, 1)
                    dve.wait_ge(v_made, k)
                    dve.tensor_scalar(pen[:], ps_v[:, :, 0, HEADS], 0.0, NEG, ALU.is_equal, ALU.mult).then_inc(pen_made, 1)
                    dve.tensor_reduce(vsum[:], ps_v[:, :, :, 0:HEADS].rearrange("p c s h -> p c h s"), AX.X, ALU.add).then_inc(vsum_made, 1)
                    dve.wait_ge(pen_made, k)
                    dve.wait_ge(vsum_made, k)
                    dve.tensor_tensor(vs[:], vsum[:], pen[:].unsqueeze(2).to_broadcast([P, C, HEADS]), ALU.add).then_inc(vs_made, 1)
                    dve.wait_ge(vs_made, k)
                    dve.tensor_reduce(mraw[:], vs[:].rearrange("p c h -> p h c"), AX.X, ALU.max).then_inc(mraw_made, 1)
                    dve.wait_ge(mraw_made, k)
                    dve.tensor_copy(mh[:, 0, :], mraw[:]).then_inc(mh_made, 1)
                    dve.wait_ge(mh_made, k)
                    dve.tensor_tensor(mrest[:], mraw[:], mh[:, 0, :], ALU.subtract).then_inc(mrest_made, 1)
                    dve.wait_ge(mrest_made, k)
                    dve.tensor_copy(mh[:, 1, :], mrest[:]).then_inc(mm_made, 1)
                    dve.wait_ge(mm_made, k)
                    dve.tensor_tensor(mh[:, 2, :], mrest[:], mh[:, 1, :], ALU.subtract).then_inc(ml_made, 1)
                    dve.tensor_tensor(m[:, qb, 0:HEADS], mraw[:], m[:, qb, HEADS:2 * HEADS], ALU.add).then_inc(m_made, 1)
                if c:
                    dve.wait_ge(a_made, k - 1)
                    dve.tensor_tensor(hv(t2[:]), hv(psa[:, 0:HEADS * HS]), bro(1), ALU.mult).then_inc(t2_made, 1)
                    dve.wait_ge(t2_made, k - 1)
                    dve.wait_ge(new_part, k - 1)
                    dve.tensor_tensor(new[:, qc, 0:HEADS * HS], new[:, qc, 0:HEADS * HS], t2[:], ALU.add).then_inc(new_made, 1)
                if b:
                    dve.wait_ge(me_made, k)
                    dve.tensor_reduce(mback[:].rearrange("p (c h) -> p c h", c=C), ps_m.rearrange("p c s h -> p c h s"), AX.X, ALU.add).then_inc(mback_made, 1)
                    dve.wait_ge(mback_made, k)
                    dve.tensor_tensor(d[:], e_sb[:, qb, :, :], mback[:].rearrange("p (c h) -> p c h", c=C), ALU.subtract).then_inc(d_made, 1)
                    dve.wait_ge(d_made, k)
                    dve.tensor_scalar(dm[:], d[:], 0.0, None, ALU.min).then_inc(dm_made, 1)
                if a and ahead:
                    make_hot(k + 1, (r + 1) % RING, u + 1 if r == 2 else u)
                if b:
                    dve.wait_ge(p_made, k)
                    dve.wait_ge(xl_in[qb], 16 * C * (u if r == 0 else u + 1))
                    for g in range(2):
                        cs = slice(g * C // 2, (g + 1) * C // 2)
                        xv = xl[:, qb, cs, 0:D].rearrange("p c (h f) -> p c h f", f=HD)
                        pv = px[:, qb, cs, :, :]
                        dve.tensor_tensor(pv[:, :, :, 0:HD], xv, pv[:, :, :, HD:HS].to_broadcast([P, C // 2, HEADS, HD]), ALU.mult).then_inc(px_made, 1)

            pipeline(dve, slot, make_hot, 0, BLOCKS)
            if GENERAL:
                dve.wait_ge(attin, 16 * 10)
                more = dve.value_load(tab[0:1, 1, BLOCKS + EXTRA:BLOCKS + EXTRA + 1], min_val=0, max_val=EXTRA)
                with dve.If(more > 0):
                    pipeline(dve, slot, make_hot, BLOCKS, EXTRA)

        @block.scalar
        def _(act):
            def copy_hotT(k, r, u):
                for g in range(G):
                    act.wait_ge(ot_tr, 3 * k + g + 1)
                    if not (isinstance(k, int) and k < 3):
                        act.wait_ge(z_made, 6 * (k - 2))
                    act.copy(hotT[:, r, 512 * g:512 * g + 512], psot[:, g, :]).then_inc(ot_copied, 1)

            def slot(k, r, u, a, b, c, ahead=True):
                qb = (r + 2) % RING

                def leaky(g, h):
                    act.wait_ge(z_made, 6 * k + 2 * g + h + 1)
                    if not (isinstance(k, int) and k == 0):
                        act.wait_ge(e_made, 3 * (k - 1) + g + 1)
                    act.activation(s[:, h, 512 * g:512 * g + 512], psz[:, h, :], ACT.Relu, scale=0.8).then_inc(s_made, 1)
                if a:
                    leaky(0, 0)
                    leaky(0, 1)
                if c:
                    act.wait_ge(dd_made, k - 1)
                    if not (isinstance(k, int) and k < 3):
                        act.wait_ge(t2_made, k - 2)
                    act.activation(ab[:], dd[:], ACT.Exp).then_inc(ab_made, 1)
                if a:
                    if not (isinstance(k, int) and k < 3):
                        act.wait_ge(me_made, k - 2)
                    for g in range(G):
                        act.copy(hotTb[:, r, 512 * g:512 * g + 512], psot[:, g, :]).then_inc(otb_copied, 1)
                if b:
                    act.wait_ge(fmt_made, k)
                    act.copy(rh[:, :, 0, 0:HEADS], ps_fm.rearrange("p (c h) -> p c h", h=HEADS)).then_inc(rh_made, 1)
                if a:
                    leaky(1, 0)
                    leaky(1, 1)
                    leaky(2, 0)
                if b:
                    act.wait_ge(dm_made, k)
                    act.activation(px[:, qb, :, :, HD], dm[:], ACT.Exp).then_inc(p_made, 1)
                if a:
                    leaky(2, 1)
                if a and ahead:
                    copy_hotT(k + 1, (r + 1) % RING, u + 1 if r == 2 else u)
            act.wait_ge(consts, 4)
            pipeline(act, slot, copy_hotT, 0, BLOCKS)
            if GENERAL:
                act.wait_ge(attin, 16 * 10)
                more = act.value_load(tab[0:1, 1, BLOCKS + EXTRA:BLOCKS + EXTRA + 1], min_val=0, max_val=EXTRA)
                with act.If(more > 0):
                    pipeline(act, slot, copy_hotT, BLOCKS, EXTRA)

        @block.tensor
        def _(pe):
            pe.wait_ge(consts, 4)
            pe.wait_ge(attin, 16 * 10)

            def turn_hot(k, r, u):
                for g in range(G):
                    pe.wait_ge(hot_made, 3 * k + g + 1)
                    if not (isinstance(k, int) and k == 0):
                        pe.wait_ge(otb_copied, 3 * (k - 1) + g + 1)
                    for c_ in range(4):
                        last = pe.transpose(psot[:, g, P * c_:P * c_ + P], hot[:, r, 4 * g + c_, :], identr[:])
                    last.then_inc(ot_tr, 1)

            def slot(k, r, u, a, b, c, ahead=True):
                qb = (r + 2) % RING
                qc = (r + 1) % RING
                first = isinstance(k, int) and k == 0

                def z(g, h):
                    if h == 0:
                        pe.wait_ge(ot_copied, 3 * k + g + 1)
                    if g == 0 and h == 0:
                        pe.wait_ge(xl_in[r], 16 * C * (u + 1))
                        pe.wait_ge(xrp_made, k + 1)
                    if not (first and g == 0):
                        pe.wait_ge(s_made, 6 * k + 2 * g + h - 1)
                    for part in range(2):
                        pe.matmul(psz[:, h, :], xrp[:, r, part, P * h:P * h + P], hotT[:, r, 512 * g:512 * g + 512], start=part == 0, stop=False)
                    for c_ in range(4):
                        last = pe.matmul(psz[:, h, P * c_:P * c_ + P], xl[:, r, 4 * g + c_, P * h:P * h + P], ident[:],
                                         is_transpose=True, start=False, stop=c_ == 3)
                    last.then_inc(z_made, 1)

                def scores(k, g, half):
                    if half == 0:
                        pe.wait_ge(s_made, 6 * k + 2 * g + 2)
                    for c_ in range(2 * half, 2 * half + 2):
                        j = 4 * g + c_
                        for h in range(2):
                            last = pe.matmul(ps_e[:, HEADS * j:HEADS * j + HEADS], s[:, h, P * j:P * j + P], att_sb[:, h, :], start=h == 0, stop=h == 1)
                    if half == 1:
                        last.then_inc(e_made, 1)

                def sums(j0, j1):
                    for j in range(j0, j1):
                        last = pe.matmul(psa[:, 0:HEADS * HS], hot[:, qc, j, :].bitcast(F32), px[:, qc, j, :, :].rearrange("p h f -> p (h f)"), start=j == 0, stop=j == C - 1)
                    if j1 == C:
                        last.then_inc(a_made, 1)
                if a:
                    z(0, 0)
                if b:
                    scores(k - 1, 2, 0)
                if a:
                    z(0, 1)
                if b:
                    scores(k - 1, 2, 1)
                if c:
                    pe.wait_ge(px_made, 2 * (k - 1))
                    if not (isinstance(k, int) and k < 3):
                        pe.wait_ge(t2_made, k - 2)
                    sums(0, 2)
                if b:
                    pe.wait_ge(e_copied, k)
                    if not (isinstance(k, int) and k < 2):
                        pe.wait_ge(mback_made, k - 1)
                    pe.transpose(ps_et, e_sb[:, qb, :, :].rearrange("p c h -> p (c h)"), ident[:])
                    pe.transpose(ps_dt, dst8[:, qb, :, :].rearrange("p c h -> p (c h)"), ident[:]).then_inc(et_made, 1)
                if a:
                    scores(k, 0, 0)
                if c:
                    sums(2, 5)
                if b:
                    pe.wait_ge(fm_made, k)
                    pe.transpose(ps_fm, lastmax[:], ident[0:C * HEADS, 0:C * HEADS]).then_inc(fmt_made, 1)
                if a:
                    scores(k, 0, 1)
                if c:
                    sums(5, 9)
                if b:
                    pe.wait_ge(rl_made, k)
                    for j in range(C):
                        last = pe.matmul(ps_v[:, j, :, :], hot[:, qb, j, :], rh[:, j, :, :], start=True, stop=True)
                    last.then_inc(v_made, 1)
                if c:
                    sums(9, C)
                if a:
                    z(1, 0)
                    z(1, 1)
                if b:
                    pe.wait_ge(ml_made, k)
                    for j in range(C):
                        last = pe.matmul(ps_m[:, j, :, :], hotTb[:, qb, P * j:P * j + P], mh[:], start=True, stop=True)
                    last.then_inc(me_made, 1)
                if a:
                    z(2, 0)
                    scores(k, 1, 0)
                    z(2, 1)
                    scores(k, 1, 1)
                if a and ahead:
                    turn_hot(k + 1, (r + 1) % RING, u + 1 if r == 2 else u)
            pipeline(pe, slot, turn_hot, 0, BLOCKS)
            if GENERAL:
                more = pe.value_load(tab[0:1, 1, BLOCKS + EXTRA:BLOCKS + EXTRA + 1], min_val=0, max_val=EXTRA)
                with pe.If(more > 0):
                    pipeline(pe, slot, turn_hot, BLOCKS, EXTRA)

GENERAL = True
def project(nc, x, Wl, Wr, bl, br, att, xn_d, xl_d, xr_d):
    T = 4
    ROWS = T * P
    GROUPS = -(-NODES // ROWS)
    with ExitStack() as ctx:
        sb = lambda n, s, d=F32: ctx.enter_context(nc.sbuf_tensor(n, s, d))
        ps = lambda n, s, d=F32: ctx.enter_context(nc.psum_tensor(n, s, d))
        sem = lambda n: ctx.enter_context(nc.semaphore(n))
        xb = sb("xb", [P, 2, T, D]); xnb = sb("xnb", [P, 2, T, D]); xT = sb("xT", [P, 2, 2, ROWS])
        W = sb("W", [P, 2, 2 * D]); bias = sb("bias", [P, 2, D]); att_row = sb("att_row", [P, 2, D]); att_02 = sb("att_02", [P, 2, D])
        lr = sb("lr", [P, 2, T, 2, XW]); weighted = sb("weighted", [P, T, 2, D])
        stats = sb("stats", [P, T, 6]); mv = sb("mv", [P, 2, T, 2]); ve = sb("ve", [P, 2, T]); half = sb("half", [P, T]); rstd = sb("rstd", [P, 2, T])
        ident = sb("ident", [P, P]); ones = sb("ones", [P, P])
        psT = ps("psT", [P, 2, 2, 512]); psY = ps("psY", [P, T, 512])
        consts = sem("consts"); cones = sem("cones"); wload = sem("wload"); att_made = sem("att_made")
        x_in = [sem("x_in0"), sem("x_in1")]
        xn_out = [sem("xn_out0"), sem("xn_out1")]
        lr_out = [sem("lr_out0"), sem("lr_out1")]
        stats_made = sem("stats_made"); mv_made = sem("mv_made"); ve_made = sem("ve_made"); rstd_made = sem("rstd_made"); xn_made = sem("xn_made")
        aggr_passed = sem("aggr_passed"); turned = sem("turned"); xT_made = sem("xT_made"); y_made = sem("y_made"); biased = sem("biased"); weighted_made = sem("weighted_made"); lr_made = sem("lr_made")
        block = ctx.enter_context(nc.Block())

        def rows(a, g):
            at = slice(NODES - ROWS, NODES) if isinstance(g, int) and g == GROUPS - 1 else bass.ds(g * ROWS, ROWS)
            return a[at, :].rearrange("(q p) c -> p q c", p=P)

        def groups(eng, slot):
            slot(0, 0, 0)
            with eng.Fori(1, GROUPS // 2 - 1) as i:
                slot(2 * i - 1, 1, i - 1)
                slot(2 * i, 0, i)
            for g in range(GROUPS - 4, GROUPS):
                slot(g, g % 2, g // 2)

        is_last = lambda g, n: isinstance(g, int) and g + n >= GROUPS

        @block.sync
        def _(sp):
            for h in range(2):
                sp.dma_start(W[:, h, 0:D], Wl[h * P:h * P + P, :]).then_inc(wload, 16)
                sp.dma_start(W[:, h, D:2 * D], Wr[h * P:h * P + P, :]).then_inc(wload, 16)
            sp.dma_start(xb[:, 0, :, :], rows(x, 0)).then_inc(x_in[0], 16)
            sp.dma_start(xb[:, 1, :, :], rows(x, 1)).then_inc(x_in[1], 16)
            for side, b in ((0, bl), (1, br)):
                sp.dma_start(bias[:, side, :], b[None, :].to_broadcast([P, D])).then_inc(wload, 16)
                sp.dma_start(att_row[:, side, :], att.rearrange("(o h) f -> o (h f)", o=1).to_broadcast([P, D])).then_inc(wload, 16)

            def normed(g, b, u):
                sp.wait_ge(xn_made, g + 1)
                if is_last(g, 1):
                    sp.wait_ge(xn_out[1 - b], 16 * u)
                sp.dma_start(rows(xn_d, g), xnb[:, b, :, :]).then_inc(xn_out[b], 16)
                if not is_last(g, 2):
                    sp.dma_start(xb[:, b, :, :], rows(x, g + 2)).then_inc(x_in[b], 16)
            normed(0, 0, 0)

            def slot(g, b, u):
                if not is_last(g, 1):
                    normed(g + 1, 1 - b, u + b)
                sp.wait_ge(lr_made, g + 1)
                if is_last(g, 1):
                    sp.wait_ge(lr_out[1 - b], 32 * u)
                sp.dma_start(rows(xl_d, g), lr[:, b, :, 0, :]).then_inc(lr_out[b], 16)
                sp.dma_start(rows(xr_d, g), lr[:, b, :, 1, :]).then_inc(lr_out[b], 16)
            groups(sp, slot)
            sp.wait_ge(xn_out[0], 16 * (GROUPS // 2 + 1))
            sp.wait_ge(xn_out[1], 16 * (GROUPS // 2))
            sp.wait_ge(lr_out[0], 32 * (GROUPS // 2 + 1))
            sp.wait_ge(lr_out[1], 32 * (GROUPS // 2))

        @block.gpsimd
        def _(pool):
            pool.memset(ones[:], 1.0).then_inc(cones, 1)
            pool.memset(half[:], -0.5).then_inc(consts, 1)
            pool.wait_ge(cones, 1)
            pool.affine_select(out=ident[:], in_=ones[:], compare_op=ALU.is_equal, fill=0.0, base=0, pattern=[[-1, P]], channel_multiplier=1).then_inc(consts, 1)
            pool.wait_ge(consts, 2)

            def inverse_deviation(g, b):
                pool.wait_ge(ve_made, g + 1)
                pool.tensor_tensor(rstd[:, b, :], ve[:, b, :], half[:], ALU.pow).then_inc(rstd_made, 1)
            inverse_deviation(0, 0)
            inverse_deviation(1, 1)
            pool.wait_ge(att_made, 1)

            def slot(g, b, u):
                for q in range(T):
                    if q == 3 and not is_last(g, 2):
                        inverse_deviation(g + 2, b)
                    pool.wait_ge(biased, T * g + q + 1)
                    if not (isinstance(g, int) and g == 0):
                        pool.wait_ge(lr_made, g)
                    pool.tensor_tensor(weighted[:, q, :, :], lr[:, b, q, :, 0:D], att_02[:], ALU.mult).then_inc(weighted_made, 1)
            groups(pool, slot)

        @block.vector
        def _(dve):
            def statistics(g, b, u):
                dve.wait_ge(x_in[b], 16 * (u + 1))
                if not (isinstance(g, int) and g == 0):
                    dve.wait_ge(mv_made, g)
                for q in range(T):
                    dve.bn_stats(stats[:, q, :], xb[:, b, q, :]).then_inc(stats_made, 1)
                if not (isinstance(g, int) and g < 2):
                    dve.wait_ge(xn_made, g - 1)
                dve.wait_ge(stats_made, T * (g + 1))
                dve.sem_inc(aggr_passed, 1)
                for q in range(T):
                    last = dve.bn_aggr(mv[:, b, q, :], stats[:, q, :])
                last.then_inc(mv_made, 1)
                dve.wait_ge(mv_made, g + 1)
                dve.tensor_scalar(ve[:, b, :], mv[:, b, :, 1], EPS, None, ALU.add).then_inc(ve_made, 1)

            def normalise(g, b, u):
                dve.wait_ge(rstd_made, g + 1)
                if not (isinstance(g, int) and g < 2):
                    dve.wait_ge(xn_out[b], 16 * u)
                    dve.wait_ge(turned, g - 1)
                for q in range(T):
                    last = dve.tensor_scalar(xnb[:, b, q, :], xb[:, b, q, :], mv[:, b, q, 0:1], rstd[:, b, q:q + 1], ALU.subtract, ALU.mult)
                last.then_inc(xn_made, 1)

            def add_bias(g, b, q):
                dve.wait_ge(y_made, T * g + q + 1)
                dve.tensor_tensor(lr[:, b, q, :, 0:D], psY[:, q, :].rearrange("p (s f) -> p s f", s=2), bias[:], ALU.add).then_inc(biased, 1)

            def head_sums(g, b, q):
                dve.wait_ge(weighted_made, T * g + q + 1)
                return dve.tensor_reduce(lr[:, b, q, :, D:XW], weighted[:, q, :, :].rearrange("p s (h f) -> p s h f", f=HD), AX.X, ALU.add)
            statistics(0, 0, 0)
            normalise(0, 0, 0)
            statistics(1, 1, 0)
            dve.wait_ge(wload, 8 * 16)
            dve.tensor_scalar(att_02[:], att_row[:], 0.2, None, ALU.mult).then_inc(att_made, 1)

            def slot(g, b, u):
                if not (isinstance(g, int) and g < 2):
                    dve.wait_ge(lr_out[b], 32 * u)
                add_bias(g, b, 0)
                if not is_last(g, 1):
                    normalise(g + 1, 1 - b, u + b)
                add_bias(g, b, 1)
                head_sums(g, b, 0)
                add_bias(g, b, 2)
                if not is_last(g, 2):
                    statistics(g + 2, b, u + 1)
                add_bias(g, b, 3)
                head_sums(g, b, 1)
                head_sums(g, b, 2)
                head_sums(g, b, 3).then_inc(lr_made, 1)
            groups(dve, slot)

        @block.scalar
        def _(act):
            def copy_turned(g, b):
                act.wait_ge(turned, g + 1)
                if not (isinstance(g, int) and g < 2):
                    act.wait_ge(y_made, T * (g - 1))
                for h in range(2):
                    act.copy(xT[:, b, h, :], psT[:, b, h, :]).then_inc(xT_made, 1)
            copy_turned(0, 0)

            def slot(g, b, u):
                if not is_last(g, 1):
                    copy_turned(g + 1, 1 - b)
            groups(act, slot)

        @block.tensor
        def _(pe):
            pe.wait_ge(consts, 2)

            def turn(g, b):
                pe.wait_ge(xn_made, g + 1)
                if not (isinstance(g, int) and g < 2):
                    pe.wait_ge(xT_made, 2 * (g - 1))
                for q in range(T):
                    for h in range(2):
                        last = pe.transpose(psT[:, b, h, P * q:P * q + P], xnb[:, b, q, P * h:P * h + P], ident[:])
                last.then_inc(turned, 1)
            turn(0, 0)
            pe.wait_ge(wload, 8 * 16)

            def slot(g, b, u):
                pe.wait_ge(xT_made, 2 * (g + 1))
                for q in range(T):
                    if q == 2 and not is_last(g, 1):
                        turn(g + 1, 1 - b)
                    if not (isinstance(g, int) and g == 0):
                        pe.wait_ge(biased, T * (g - 1) + q + 1)
                    for h in range(2):
                        last = pe.matmul(psY[:, q, :], xT[:, b, h, P * q:P * q + P], W[:, h, :], start=h == 0, stop=h == 1)
                    last.then_inc(y_made, 1)
            groups(pe, slot)


HID, EXPERTS = 1024, 8
HC = HID // P
T4 = 4
GROUP = T4 * P
GROUPS = -(-NODES // GROUP)
LAST0 = NODES - GROUP
REPEATED = (GROUPS - 1) * GROUP - LAST0
CAP = (NODES // P + 2) * P
RW = D + 4
ETILES = (NODES + EXPERTS * (P - 1)) // P
ROUTED = EXPERTS * CAP + P
NOWHERE = float(1 << 20)


def nodes(nc, x, bias, gamma, beta, W1, b1, Wg, bg, xn_d, st_d, routed_d, etab_d):
    with ExitStack() as ctx:
        sb = lambda n, s, d=F32: ctx.enter_context(nc.sbuf_tensor(n, s, d))
        ps = lambda n, s, d=F32: ctx.enter_context(nc.psum_tensor(n, s, d))
        sem = lambda n: ctx.enter_context(nc.semaphore(n))
        stb = sb("n_st", [P, 2, T4, SW]); xnb = sb("n_xn", [P, 2, T4, D]); xb = sb("n_x", [P, 2, T4, D])
        rden = sb("rden", [P, T4, HEADS]); z = sb("z", [P, T4, D]); neg = sb("neg", [P, T4, D]); eneg = sb("eneg", [P, T4, D])
        stats = sb("n_stats", [P, T4, 6]); mv = sb("n_mv", [P, T4, 2]); ve = sb("n_ve", [P, T4]); rstd = sb("n_rstd", [P, T4])
        row = sb("row", [P, 2, T4, RW]); x2n = sb("x2n", [P, T4, D]); x2T = sb("x2T", [P, 2, GROUP]); H = sb("H", [P, HC, GROUP])
        bias_r = sb("bias_r", [P, D]); gamma_r = sb("gamma_r", [P, D]); beta_r = sb("beta_r", [P, D]); bg_r = sb("bg_r", [P, EXPERTS])
        w1 = sb("w1", [P, 2, HID]); b1c = sb("b1c", [P, HC]); wg = sb("wg", [P, HC, EXPERTS])
        lg = sb("lg", [P, T4, EXPERTS]); lmax = sb("lmax", [P, T4]); ex = sb("ex", [P, T4, EXPERTS]); pr = sb("pr", [P, T4, EXPERTS])
        one = sb("one_hot", [P, T4, EXPERTS]); before = sb("before", [P, T4 + 1, EXPERTS]); cnt = sb("cnt", [P, EXPERTS]); cap0 = sb("cap0", [P, EXPERTS])
        prio = sb("prio", [P, EXPERTS]); top = sb("top", [P, T4]); rk = sb("rk", [P, T4, EXPERTS]); posf = sb("posf", [P, T4]); posi = sb("posi", [P, 2, T4], I32)
        valid = sb("valid", [P, T4]); invalid = sb("invalid", [P, T4]); half = sb("n_half", [P, T4]); ident = sb("n_ident", [P, P]); ones = sb("n_ones", [P, P]); tri = sb("tri", [P, P])
        pid = sb("pid", [P, 1]); nodei = sb("nodei", [P, T4])
        j128 = sb("n_j128", [P, 1]); nti = sb("nti", [P, EXPERTS], I32); ntf = sb("ntf", [P, EXPERTS]); w = sb("n_w", [P, 6, EXPERTS]); red = sb("n_red", [P, 4]); et = sb("et", [P, 2]); eti = sb("eti", [P, 2], I32)
        pad = sb("pad", [P, RW]); padpos = sb("padpos", [P, EXPERTS], I32)
        psx = ps("psx", [P, 2, GROUP]); psh = ps("psh", [P, 2, GROUP]); psl_ = ps("psl", [P, 512]); psr_ = ps("psr", [P, 512])
        psl = psl_[:, 0:T4 * EXPERTS].rearrange("p (t e) -> p t e", e=EXPERTS); psr = psr_[:, 0:(T4 + 1) * EXPERTS].rearrange("p (t e) -> p t e", e=EXPERTS)
        cz = sem("n_cz"); consts = sem("n_consts"); wload = sem("n_wload"); loaded = [sem("n_loaded0"), sem("n_loaded1")]
        x1_done = sem("x1_done"); z_done = sem("z_done"); vp = sem("n_vp"); rst = sem("n_rst"); neg_done = sem("neg_done"); eneg_done = sem("eneg_done"); x2_done = sem("x2_done")
        xT = sem("n_xT"); xT_copied = sem("xT_copied"); h_made = sem("h_made"); gelu_done = sem("gelu_done"); l_made = sem("l_made"); lm_done = sem("lm_done"); ex_done = sem("ex_done")
        hot_done = sem("n_hot_done"); r_made = sem("r_made"); pos_done = sem("pos_done"); scattered = [sem("scattered0"), sem("scattered1")]; passed = sem("n_passed"); dpassed = sem("n_dpassed")
        rowbase = sb("rowbase", [P, 1]); dpassed2 = sem("n_dpassed2"); top_done = sem("top_done"); masked = sem("masked"); masked2 = sem("masked2"); rk_s = sem("rk_step"); pf_done = sem("pf_done")
        link_s = sem("node_step"); route_s = sem("route_step"); tabs = sem("n_tabs"); padded = sem("padded"); tstep = sem("tstep"); tstored = sem("tstored")
        block = ctx.enter_context(nc.Block())
        bro = lambda v, s: v.to_broadcast(s)

        def rows(g):
            return LAST0 if isinstance(g, int) and g == GROUPS - 1 else g * GROUP

        def grouped(a, g):
            r0 = rows(g)
            return a[bass.ds(r0, GROUP), :].rearrange("(t p) c -> p t c", p=P)

        @block.sync
        def _(sp):
            rb = lambda a, n: a.rearrange("(o c) -> o c", o=1).to_broadcast([P, n])
            sp.dma_start(bias_r[:], rb(bias, D)).then_inc(wload, 16)
            sp.dma_start(gamma_r[:], rb(gamma, D)).then_inc(wload, 16)
            sp.dma_start(beta_r[:], rb(beta, D)).then_inc(wload, 16)
            sp.dma_start(bg_r[:], rb(bg, EXPERTS)).then_inc(wload, 16)
            sp.dma_start(w1[:], W1.rearrange("(k p) c -> p k c", p=P)).then_inc(wload, 16)
            sp.dma_start(wg[:], Wg.rearrange("(k p) c -> p k c", p=P)).then_inc(wload, 16)
            with nc.allow_non_contiguous_dma(reason="bias by hidden unit"):
                sp.dma_start(b1c[:], b1.rearrange("(k p) -> p k", p=P)).then_inc(wload, 16)

            def load(g, b):
                sp.dma_start(stb[:, b, :, :], grouped(st_d, g)).then_inc(loaded[b], 16)
                sp.dma_start(xnb[:, b, :, :], grouped(xn_d, g)).then_inc(loaded[b], 16)
                sp.dma_start(xb[:, b, :, :], grouped(x, g)).then_inc(loaded[b], 16)
            load(0, 0)
            load(1, 1)
            with sp.Fori(0, (GROUPS - 3) // 2) as i:
                for b in range(2):
                    g = 2 * i + b
                    sp.wait_ge(x1_done, g + 1)
                    sp.sem_inc(passed, 1)
                    load(g + 2, b)
            for g in range((GROUPS - 3) // 2 * 2, GROUPS - 2):
                sp.wait_ge(x1_done, g + 1)
                load(g + 2, g % 2)
            sp.wait_ge(tabs, 1)
            with nc.allow_non_contiguous_dma(reason="a table row"):
                sp.dma_start(etab_d[0, :, None], eti[0:ETILES, 0:1]).then_inc(tstored, 16)
                sp.dma_start(etab_d[1, :, None], eti[0:ETILES, 1:2]).then_inc(tstored, 16)
            sp.dma_start(routed_d[EXPERTS * CAP:ROUTED, :], pad[:]).then_inc(tstored, 16)
            sp.wait_ge(tstored, 48)

        @block.gpsimd
        def _(pool):
            pool.memset(ones[:], 1.0).then_inc(cz, 1)
            pool.memset(half[:], -0.5).then_inc(consts, 1)
            pool.memset(valid[:], 1.0).then_inc(cz, 1)
            pool.iota(pid[:], [[0, 1]], base=0, channel_multiplier=1, allow_small_or_imprecise_dtypes=True).then_inc(consts, 1)
            pool.iota(nodei[:], [[P, T4]], base=0, channel_multiplier=1, allow_small_or_imprecise_dtypes=True).then_inc(consts, 1)
            pool.iota(cap0[:], [[CAP, EXPERTS]], base=0, channel_multiplier=0, allow_small_or_imprecise_dtypes=True).then_inc(consts, 1)
            pool.iota(prio[:], [[-1, EXPERTS]], base=EXPERTS, channel_multiplier=0, allow_small_or_imprecise_dtypes=True).then_inc(consts, 1)
            pool.iota(j128[:], [[0, 1]], base=0, channel_multiplier=P, allow_small_or_imprecise_dtypes=True).then_inc(consts, 1)
            pool.wait_ge(cz, 2)
            pool.affine_select(out=ident[:], in_=ones[:], compare_op=ALU.is_equal, fill=0.0, base=0, pattern=[[-1, P]], channel_multiplier=1).then_inc(consts, 1)
            pool.affine_select(out=tri[:], in_=ones[:], compare_op=ALU.is_gt, fill=0.0, base=0, pattern=[[1, P]], channel_multiplier=-1).then_inc(consts, 1)
            pool.affine_select(out=valid[:], in_=ones[:, 0:T4], compare_op=ALU.is_ge, fill=0.0, base=-REPEATED, pattern=[[P, T4]], channel_multiplier=1).then_inc(consts, 1)

            def rsqrt(g, n):
                pool.wait_ge(vp, 2 * g + n + 1)
                pool.tensor_tensor(rstd[:], ve[:], half[:], ALU.pow).then_inc(rst, 1)

            def scatter(g, b):
                pool.wait_ge(pos_done, g + 1)
                pool.sem_inc(dpassed, 1)
                for t in range(T4):
                    pool.indirect_dma_start(routed_d[:, :], bass.IndirectOffsetOnAxis(posi[:, b, t:t + 1], 0), row[:, b, t, :], None,
                                            bounds_check=ROUTED - 1, oob_is_err=False).then_inc(scattered[b], 16)
            rsqrt(0, 0)
            rsqrt(0, 1)
            with pool.Fori(0, (GROUPS - 1) // 2) as i:
                for b in range(2):
                    rsqrt(2 * i + b + 1, 0)
                    rsqrt(2 * i + b + 1, 1)
                    scatter(2 * i + b, b)
            scatter(GROUPS - 1, 0)
            pool.wait_ge(tabs, 1)
            pool.wait_ge(scattered[0], 16 * T4 * ((GROUPS + 1) // 2))
            pool.wait_ge(scattered[1], 16 * T4 * (GROUPS // 2))
            for e in range(EXPERTS):
                pool.indirect_dma_start(routed_d[:, :], bass.IndirectOffsetOnAxis(padpos[:, e:e + 1], 0), pad[:, :], None,
                                        bounds_check=ROUTED - 1, oob_is_err=False).then_inc(padded, 16)
            pool.wait_ge(padded, 16 * EXPERTS)

        @block.vector
        def _(dve):
            dve.memset(cnt[:], 0.0)
            dve.memset(before[:, 0, :], 0.0)
            dve.memset(pad[:, 0:RW - 1], 0.0)
            dve.memset(pad[:, RW - 1:RW], NOWHERE)
            dve.wait_ge(consts, 9)
            dve.wait_ge(wload, 7 * 16)
            dve.tensor_scalar(invalid[:], valid[:], -NOWHERE, NOWHERE, ALU.mult, ALU.add)

            N_STEPS, R_STEPS = [None], [None]

            def chain(s, g, total):
                n = [0]

                def then(ins, wait=True):
                    n[0] += 1
                    ins.then_inc(s, 1)
                    if wait:
                        dve.wait_ge(s, total * g + n[0])
                return then, n

            NT = 11
            def node(g, b, u):
                then, n = chain(link_s, g, NT)
                heads = lambda v: v.rearrange("p t (h f) -> p t h f", f=HS)
                acc = heads(stb[:, b, :, 0:HEADS * HS])
                f3 = lambda v: v.unsqueeze(1).to_broadcast([P, T4, D])
                dve.wait_ge(loaded[b], 48 * (u + 1))
                then(dve.tensor_scalar(rden[:], acc[:, :, :, HD], 0.0, None, ALU.is_equal))
                then(dve.tensor_tensor(rden[:], rden[:], acc[:, :, :, HD], ALU.add))
                then(dve.reciprocal(rden[:], rden[:]))
                then(dve.tensor_tensor(z[:].rearrange("p t (h f) -> p t h f", f=HD), acc[:, :, :, 0:HD], rden[:].unsqueeze(3).to_broadcast([P, T4, HEADS, HD]), ALU.mult))
                then(dve.tensor_tensor(z[:], z[:], f3(bias_r[:]), ALU.add))
                then(dve.tensor_tensor(z[:], z[:], xnb[:, b, :, :], ALU.add))

                def moments(src, k):
                    for t in range(T4):
                        ins = dve.bn_stats(stats[:, t, :], src[:, t, :])
                    ins.then_inc(z_done, 1)
                    dve.wait_ge(z_done, 4 * g + 2 * k + 1)
                    dve.sem_inc(dpassed2, 1)
                    for t in range(T4):
                        ins = dve.bn_aggr(mv[:, t, :], stats[:, t, :])
                    ins.then_inc(z_done, 1)
                    dve.wait_ge(z_done, 4 * g + 2 * k + 2)
                    dve.tensor_scalar(ve[:], mv[:, :, 1], EPS, None, ALU.add).then_inc(vp, 1)
                    dve.wait_ge(rst, 2 * g + k + 1)
                moments(z, 0)
                for t in range(T4):
                    ins = dve.tensor_scalar(z[:, t, :], z[:, t, :], mv[:, t, 0:1], rstd[:, t:t + 1], ALU.subtract, ALU.mult)
                then(ins)
                then(dve.tensor_tensor(z[:], z[:], f3(gamma_r[:]), ALU.mult))
                then(dve.tensor_tensor(z[:], z[:], f3(beta_r[:]), ALU.add))
                dve.tensor_scalar(neg[:], z[:], 0.0, None, ALU.min).then_inc(neg_done, 1)
                if not (isinstance(u, int) and u == 0):
                    dve.wait_ge(scattered[b], 16 * T4 * u)
                then(dve.scalar_tensor_tensor(out=row[:, b, :, 0:D], in0=z[:], scalar=0.0, in1=xb[:, b, :, :], op0=ALU.max, op1=ALU.add))
                dve.wait_ge(eneg_done, g + 1)
                dve.scalar_tensor_tensor(out=row[:, b, :, 0:D], in0=eneg[:], scalar=-1.0, in1=row[:, b, :, 0:D], op0=ALU.add, op1=ALU.add).then_inc(x1_done, 1)
                dve.wait_ge(x1_done, g + 1)
                moments(row[:, b, :, 0:D], 1)
                dve.tensor_copy(row[:, b, :, D], mv[:, :, 0])
                then(dve.tensor_copy(row[:, b, :, D + 1], rstd[:]))
                if not (isinstance(g, int) and g == 0):
                    dve.wait_ge(xT, g)
                for t in range(T4):
                    ins = dve.tensor_scalar(x2n[:, t, :], row[:, b, t, 0:D], mv[:, t, 0:1], rstd[:, t:t + 1], ALU.subtract, ALU.mult)
                ins.then_inc(x2_done, 1)
                assert n[0] == NT, n

            RT = 10
            def route(g, b, last=False):
                then, n = chain(route_s, g, RT)
                e3 = lambda v: v.unsqueeze(2).to_broadcast([P, T4, EXPERTS])
                dve.wait_ge(l_made, g + 1)
                then(dve.tensor_tensor(lg[:], psl, bg_r[:].unsqueeze(1).to_broadcast([P, T4, EXPERTS]), ALU.add))
                then(dve.tensor_reduce(lmax[:], lg[:], AX.X, ALU.max))
                dve.tensor_tensor(lg[:], lg[:], e3(lmax[:]), ALU.subtract).then_inc(lm_done, 1)
                dve.wait_ge(ex_done, g + 1)
                then(dve.tensor_reduce(lmax[:], ex[:], AX.X, ALU.add))
                then(dve.reciprocal(lmax[:], lmax[:]))
                then(dve.tensor_tensor(pr[:], ex[:], e3(lmax[:]), ALU.mult))
                dve.tensor_reduce(top[:], pr[:], AX.X, ALU.max).then_inc(top_done, 1)
                dve.wait_ge(top_done, g + 1)
                dve.tensor_copy(row[:, b, :, D + 2], top[:])
                dve.tensor_scalar(row[:, b, :, D + 3], nodei[:], rowbase[:, 0:1], None, ALU.add)
                then(dve.tensor_tensor(one[:], pr[:], e3(top[:]), ALU.is_equal))
                then(dve.tensor_tensor(one[:], one[:], prio[:].unsqueeze(1).to_broadcast([P, T4, EXPERTS]), ALU.mult))
                then(dve.tensor_reduce(top[:], one[:], AX.X, ALU.max))
                then(dve.tensor_tensor(one[:], prio[:].unsqueeze(1).to_broadcast([P, T4, EXPERTS]), e3(top[:]), ALU.is_equal))
                if last:
                    dve.tensor_tensor(one[:], one[:], e3(valid[:]), ALU.mult).then_inc(masked, 1)
                    dve.wait_ge(masked, 1)
                for t in range(T4):
                    dve.tensor_tensor(before[:, t + 1, :], before[:, t, :], one[:, t, :], ALU.add).then_inc(hot_done, 1)
                    dve.wait_ge(hot_done, 4 * g + t + 1)
                dve.wait_ge(r_made, g + 1)
                then(dve.tensor_tensor(rk[:], psr[:, 0:T4, :], cnt[:].unsqueeze(1).to_broadcast([P, T4, EXPERTS]), ALU.add))
                dve.tensor_tensor(rk[:], rk[:], cap0[:].unsqueeze(1).to_broadcast([P, T4, EXPERTS]), ALU.add).then_inc(rk_s, 1)
                dve.wait_ge(rk_s, 2 * g + 1)
                dve.tensor_tensor(rk[:], rk[:], one[:], ALU.mult).then_inc(rk_s, 1)
                dve.tensor_tensor(cnt[:], cnt[:], psr[:, T4, :], ALU.add)
                dve.wait_ge(rk_s, 2 * g + 2)
                dve.tensor_reduce(posf[:], rk[:], AX.X, ALU.add).then_inc(pf_done, 1)
                dve.tensor_scalar(rowbase[:], rowbase[:], float(GROUP), None, ALU.add)
                dve.wait_ge(pf_done, g + 1)
                if last:
                    dve.tensor_tensor(posf[:], posf[:], invalid[:], ALU.add).then_inc(masked, 1)
                    dve.wait_ge(masked, 2)
                dve.tensor_copy(posi[:, b, :], posf[:]).then_inc(pos_done, 1)
                assert n[0] == RT, n

            dve.memset(rowbase[:], 0.0)
            node(0, 0, 0)
            node(1, 1, 0)
            route(0, 0)
            with dve.Fori(1, (GROUPS - 1) // 2) as i:
                node(2 * i, 0, i)
                route(2 * i - 1, 1)
                node(2 * i + 1, 1, i)
                route(2 * i, 0)
            k = (GROUPS - 1) // 2
            node(2 * k, 0, k)
            route(2 * k - 1, 1)
            dve.wait_ge(pos_done, GROUPS - 1)
            dve.memset(rowbase[:], float(LAST0)).then_inc(masked2, 1)
            dve.wait_ge(masked2, 1)
            route(2 * k, 0, last=True)
            q = [0]

            def then(ins):
                q[0] += 1
                ins.then_inc(tstep, 1)
                dve.wait_ge(tstep, q[0])
            then(dve.tensor_scalar(nti[:], cnt[:], float(P - 1), None, ALU.add))
            then(dve.tensor_scalar(nti[:], nti[:], 7, None, ALU.arith_shift_right))
            then(dve.tensor_copy(ntf[:], nti[:]))
            then(dve.memset(w[:, 0, :], 1.0))
            then(dve.tensor_tensor_scan(w[:, 1, :], w[:, 0, :], ntf[:], 0.0, ALU.mult, ALU.add))
            then(dve.tensor_tensor(w[:, 2, :], w[:, 1, :], ntf[:], ALU.subtract))
            then(dve.tensor_scalar(w[:, 3, :], w[:, 1, :], pid[:, 0:1], None, ALU.is_gt))
            then(dve.tensor_scalar(w[:, 4, :], w[:, 2, :], pid[:, 0:1], None, ALU.is_le))
            then(dve.tensor_tensor(w[:, 3, :], w[:, 3, :], w[:, 4, :], ALU.mult))
            then(dve.tensor_scalar(w[:, 4, :], w[:, 2, :], -float(P), j128[:, 0:1], ALU.mult, ALU.add))
            then(dve.tensor_tensor(w[:, 4, :], w[:, 4, :], cap0[:], ALU.add))
            then(dve.tensor_tensor(w[:, 4, :], w[:, 4, :], w[:, 3, :], ALU.mult))
            then(dve.tensor_scalar(w[:, 5, :], prio[:], -1.0, float(EXPERTS), ALU.mult, ALU.add))
            then(dve.tensor_tensor(w[:, 5, :], w[:, 5, :], w[:, 3, :], ALU.mult))
            then(dve.tensor_reduce(red[:, 0:1], w[:, 3, :], AX.X, ALU.add))
            then(dve.tensor_reduce(red[:, 1:2], w[:, 4, :], AX.X, ALU.add))
            then(dve.tensor_reduce(et[:, 1:2], w[:, 5, :], AX.X, ALU.add))
            then(dve.tensor_scalar(red[:, 2:3], red[:, 0:1], -float(EXPERTS * CAP), float(EXPERTS * CAP), ALU.mult, ALU.add))
            then(dve.tensor_tensor(et[:, 0:1], red[:, 1:2], red[:, 2:3], ALU.add))
            then(dve.tensor_copy(eti[:], et[:]))
            then(dve.tensor_tensor(w[:, 0, :], cnt[:], cap0[:], ALU.add))
            then(dve.tensor_scalar(padpos[:], w[:, 0, :], pid[:, 0:1], None, ALU.add))
            dve.tensor_copy(red[:, 3:4], red[:, 0:1]).then_inc(tabs, 1)

        @block.scalar
        def _(act):
            act.wait_ge(wload, 7 * 16)

            def elu(g):
                act.wait_ge(neg_done, g + 1)
                act.activation(eneg[:], neg[:], ACT.Exp).then_inc(eneg_done, 1)

            def softmax(g):
                act.wait_ge(lm_done, g + 1)
                act.activation(ex[:], lg[:], ACT.Exp).then_inc(ex_done, 1)

            def hidden(g):
                act.wait_ge(xT, g + 1)
                act.copy(x2T[:], psx[:]).then_inc(xT_copied, 1)
                for c in range(HC):
                    act.wait_ge(h_made, HC * g + c + 1)
                    act.activation(H[:, c, :], psh[:, c % 2, :], ACT.Gelu, bias=b1c[:, c:c + 1]).then_inc(gelu_done, 1)
            elu(0)
            with act.Fori(0, (GROUPS - 1) // 2) as i:
                for b in range(2):
                    hidden(2 * i + b)
                    elu(2 * i + b + 1)
                    softmax(2 * i + b)
            hidden(GROUPS - 1)
            softmax(GROUPS - 1)

        @block.tensor
        def _(pe):
            pe.wait_ge(consts, 9)
            pe.wait_ge(wload, 7 * 16)

            def step(g):
                pe.wait_ge(x2_done, g + 1)
                for h in range(2):
                    for t in range(T4):
                        last = pe.transpose(psx[:, h, P * t:P * t + P], x2n[:, t, P * h:P * h + P], ident[:])
                last.then_inc(xT, 1)
                pe.wait_ge(xT_copied, g + 1)
                for c in range(HC):
                    if not (isinstance(g, int) and g == 0 and c < 2):
                        pe.wait_ge(gelu_done, HC * g + c - 1)
                    pe.matmul(psh[:, c % 2, :], w1[:, 0, P * c:P * c + P], x2T[:, 0, :], start=True, stop=False)
                    pe.matmul(psh[:, c % 2, :], w1[:, 1, P * c:P * c + P], x2T[:, 1, :], start=False, stop=True).then_inc(h_made, 1)
                pe.wait_ge(gelu_done, HC * g + HC)
                for t in range(T4):
                    for c in range(HC):
                        last = pe.matmul(psl[:, t, :], H[:, c, P * t:P * t + P], wg[:, c, :], start=c == 0, stop=c == HC - 1)
                last.then_inc(l_made, 1)
                pe.wait_ge(hot_done, 4 * g + 4)
                flat = lambda v: v.rearrange("p t e -> p (t e)")
                pe.matmul(flat(psr[:, 0:T4, :]), tri[:], flat(one[:]), start=True, stop=False, skip_group_check=True)
                pe.matmul(flat(psr[:, 0:T4, :]), ones[:], flat(before[:, 0:T4, :]), start=False, stop=True, skip_group_check=True)
                pe.matmul(psr[:, T4, :], ones[:], before[:, T4, :], start=True, stop=True, skip_group_check=True).then_inc(r_made, 1)
            step(0)
            with pe.Fori(0, (GROUPS - 1) // 2) as i:
                step(2 * i + 1)
                step(2 * i + 2)


def experts(nc, W1, b1, Wd, bd, routed_d, etab_d, out):
    with ExitStack() as ctx:
        sb = lambda n, s, d=F32: ctx.enter_context(nc.sbuf_tensor(n, s, d))
        ps = lambda n, s, d=F32: ctx.enter_context(nc.psum_tensor(n, s, d))
        sem = lambda n: ctx.enter_context(nc.semaphore(n))
        ring = lambda n: [sem(f"{n}{r}") for r in range(RING)]
        wd = sb("wd", [P, EXPERTS, HC, D]); bdr = sb("bdr", [P, EXPERTS, D]); w1 = sb("x_w1", [P, 2, HID]); b1c = sb("x_b1c", [P, HC])
        row = sb("x_row", [P, RING, RW]); x2 = sb("x_x2", [P, D]); x2T = sb("x_x2T", [P, RING, 2, P]); H = sb("x_H", [P, RING, HC, P])
        y = sb("x_y", [P, RING, D]); res = sb("x_res", [P, RING, D]); node = sb("x_node", [P, RING, 1], I32)
        ident = sb("x_ident", [P, P]); ones = sb("x_ones", [P, P]); tab = sb("x_tab", [1, 2, ETILES], I32)
        psx = ps("x_psx", [P, 2, 256]); psh = ps("x_psh", [P, 2, 512]); psy = ps("x_psy", [P, 3, 512])
        cz = sem("x_cz"); consts = sem("x_consts"); wload = sem("x_wload"); row_in = ring("row_in"); x2_done = sem("x_x2_done"); xT = sem("x_xT"); xT_copied = sem("x_xT_copied")
        h_made = sem("x_h_made"); gelu = sem("x_gelu"); y_made = sem("x_y_made"); y1 = sem("x_y1"); res_done = sem("x_res"); stored = ring("x_stored"); passed = sem("x_passed")
        block = ctx.enter_context(nc.Block())
        one = lambda t: slice(t, t + 1) if isinstance(t, int) else bass.ds(t, 1)

        def slots(eng, slot):
            slot(0, 0, 0, down=False)
            slot(1, 1, 0)
            slot(2, 2, 0)
            with eng.Fori(1, ETILES // RING - 1) as i:
                for r in range(RING):
                    slot(RING * i + r, r, i)
            for t in range(ETILES - RING, ETILES):
                slot(t, t % RING, t // RING, turn=t + 1 < ETILES)
            slot(ETILES, 0, ETILES // RING, up=False, turn=False)

        def run(eng, step):
            for t in range(RING):
                step(t, t, 0)
            with eng.Fori(1, ETILES // RING) as i:
                for r in range(RING):
                    step(RING * i + r, r, i)

        @block.sync
        def _(sp):
            sp.dma_start(tab[:], etab_d[None, :, :]).then_inc(wload, 16)
            sp.dma_start(w1[:], W1.rearrange("(k p) c -> p k c", p=P)).then_inc(wload, 16)
            with nc.allow_non_contiguous_dma(reason="bias by hidden unit"):
                sp.dma_start(b1c[:], b1.rearrange("(k p) -> p k", p=P)).then_inc(wload, 16)
            sp.dma_start(bdr[:], bd.rearrange("(o e) d -> o e d", o=1).to_broadcast([P, EXPERTS, D])).then_inc(wload, 16)
            for e in range(EXPERTS):
                sp.dma_start(wd[:, e, :, :], Wd[e, :, :].rearrange("(k p) c -> p k c", p=P)).then_inc(wload, 16)
            sp.wait_ge(wload, 16 * 12)

            def step(t, r, u):
                first = sp.value_load(tab[0:1, 0, one(t)], min_val=0, max_val=ROUTED - P)
                if not (isinstance(u, int) and u == 0):
                    sp.wait_ge(res_done, t - 2)
                    sp.sem_inc(passed, 1)
                sp.dma_start(row[:, r, :], routed_d[bass.ds(first, P), :]).then_inc(row_in[r], 16)
            run(sp, step)

        @block.gpsimd
        def _(pool):
            pool.memset(ones[:], 1.0).then_inc(cz, 1)
            pool.wait_ge(cz, 1)
            pool.affine_select(out=ident[:], in_=ones[:], compare_op=ALU.is_equal, fill=0.0, base=0, pattern=[[-1, P]], channel_multiplier=1).then_inc(consts, 1)

            def step(t, r, u):
                pool.wait_ge(res_done, t + 1)
                pool.sem_inc(passed, 1)
                pool.indirect_dma_start(out[:, :], bass.IndirectOffsetOnAxis(node[:, r, :], 0), res[:, r, :], None, bounds_check=NODES - 1, oob_is_err=False).then_inc(stored[r], 16)
            run(pool, step)
            for r in range(RING):
                pool.wait_ge(stored[r], 16 * (ETILES // RING))

        @block.vector
        def _(dve):
            def normal(t, r, u):
                dve.wait_ge(row_in[r], 16 * (u + 1))
                if not (isinstance(t, int) and t == 0):
                    dve.wait_ge(xT, t)
                dve.tensor_scalar(x2[:], row[:, r, 0:D], row[:, r, D:D + 1], row[:, r, D + 1:D + 2], ALU.subtract, ALU.mult).then_inc(x2_done, 1)

            def finish(t, r, u):
                e = dve.value_load(tab[0:1, 1, one(t)], min_val=0, max_val=EXPERTS - 1)
                dve.wait_ge(y_made, t + 1)
                dve.sem_inc(passed, 1)
                dve.tensor_tensor(y[:, r, :], psy[:, r, 0:D], bdr[:, one2(e), :].rearrange("p o d -> p (o d)"), ALU.add).then_inc(y1, 1)
                if not (isinstance(u, int) and u == 0):
                    dve.wait_ge(stored[r], 16 * u)
                dve.tensor_copy(node[:, r, :], row[:, r, D + 3:D + 4])
                dve.wait_ge(y1, t + 1)
                dve.scalar_tensor_tensor(out=res[:, r, :], in0=y[:, r, :], scalar=row[:, r, D + 2:D + 3], in1=row[:, r, 0:D], op0=ALU.mult, op1=ALU.add).then_inc(res_done, 1)
            one2 = lambda e: bass.ds(e, 1)
            dve.wait_ge(wload, 16 * 12)
            normal(0, 0, 0)

            def slot(t, r, u, up=True, turn=True, down=True):
                if turn:
                    normal(t + 1, (r + 1) % RING, u + 1 if r == 2 else u)
                if down:
                    finish(t - 1, (r + 2) % RING, u - 1 if r == 0 else u)
            slots(dve, slot)

        @block.scalar
        def _(act):
            act.wait_ge(wload, 16 * 12)

            def copy_turned(t, r):
                act.wait_ge(xT, t + 1)
                act.copy(x2T[:, r, :, :], psx[:, :, 0:P]).then_inc(xT_copied, 1)
            copy_turned(0, 0)

            def slot(t, r, u, up=True, turn=True, down=True):
                if up:
                    for half in range(2):
                        act.wait_ge(h_made, 2 * t + half + 1)
                        for c in range(HC // 2):
                            last = act.activation(H[:, r, HC // 2 * half + c, :], psh[:, half, P * c:P * c + P], ACT.Gelu, bias=b1c[:, HC // 2 * half + c:HC // 2 * half + c + 1])
                        last.then_inc(gelu, 1)
                if turn:
                    copy_turned(t + 1, (r + 1) % RING)
            slots(act, slot)

        @block.tensor
        def _(pe):
            pe.wait_ge(wload, 16 * 12)
            pe.wait_ge(consts, 1)

            def project_down(t, r, e, c0, c1):
                if c0 == 0:
                    pe.wait_ge(gelu, 2 * t + 2)
                    if not (isinstance(t, int) and t < 3):
                        pe.wait_ge(y1, t - 2)
                    pe.sem_inc(passed, 1)
                for c in range(c0, c1):
                    last = pe.matmul(psy[:, r, 0:D], H[:, r, c, :], wd[:, bass.ds(e, 1), c, :].rearrange("p o d -> p (o d)"), start=c == 0, stop=c == HC - 1)
                if c1 == HC:
                    last.then_inc(y_made, 1)

            def turn_rows(t, r):
                pe.wait_ge(x2_done, t + 1)
                if not (isinstance(t, int) and t == 0):
                    pe.wait_ge(xT_copied, t)
                for h in range(2):
                    last = pe.transpose(psx[:, h, 0:P], x2[:, P * h:P * h + P], ident[:])
                last.then_inc(xT, 1)

            def hidden(t, r, half):
                if not (isinstance(t, int) and t == 0):
                    pe.wait_ge(gelu, 2 * t + half - 1)
                for c in range(HC // 2):
                    for h in range(2):
                        at = P * (HC // 2 * half + c)
                        last = pe.matmul(psh[:, half, P * c:P * c + P], w1[:, h, at:at + P], x2T[:, r, h, :], start=h == 0, stop=h == 1)
                last.then_inc(h_made, 1)
            turn_rows(0, 0)

            def slot(t, r, u, up=True, turn=True, down=True):
                if down:
                    e = pe.value_load(tab[0:1, 1, one(t - 1)], min_val=0, max_val=EXPERTS - 1)
                if up:
                    pe.wait_ge(xT_copied, t + 1)
                    hidden(t, r, 0)
                    hidden(t, r, 1)
                if down:
                    project_down(t - 1, (r + 2) % RING, e, 0, HC // 2)
                if turn:
                    turn_rows(t + 1, (r + 1) % RING)
                if down:
                    project_down(t - 1, (r + 2) % RING, e, HC // 2, HC)
            slots(pe, slot)



_INS = ['x', 'src', 'dst', 'L0_gnn_Wl', 'L0_gnn_bl', 'L0_gnn_Wr', 'L0_gnn_br', 'L0_gnn_att', 'L0_gnn_bias', 'L0_gnn_gamma',
        'L0_gnn_beta', 'L0_ffn_W1', 'L0_ffn_b1', 'L0_ffn_Wg', 'L0_ffn_bg', 'L0_ffn_Wd', 'L0_ffn_bd']


def program(nc, i, out):
    scratch = lambda name, shape, dt=F32: nc.dram_tensor(name, shape, dt).ap()
    xn_d = scratch("xn_d", (NODES, D))
    xl_d = scratch("xl_d", (NODES, XW))
    xr_d = scratch("xr_d", (NODES_UP, XW))
    st_d = scratch("st_d", (NODES_UP, SW))
    src_pad = scratch("src_pad", (PADDED,), I32)
    dst_pad = scratch("dst_pad", (PADDED,), I32)
    rows_d = scratch("rows_d", (3, BLOCKS))
    tabf_d = scratch("tabf_d", (BLOCKS + EXTRA,))
    tabi_d = scratch("tabi_d", (2, BLOCKS + EXTRA + 1), I32)
    routed_d = scratch("routed_d", (ROUTED, RW))
    etab_d = scratch("etab_d", (2, ETILES), I32)
    project(nc, i['x'], i['L0_gnn_Wl'], i['L0_gnn_Wr'], i['L0_gnn_bl'], i['L0_gnn_br'], i['L0_gnn_att'], xn_d, xl_d, xr_d)
    setup(nc, i['src'], i['dst'], src_pad, dst_pad, xr_d, st_d, rows_d, tabf_d, tabi_d)
    edges(nc, i['L0_gnn_att'], xl_d, xr_d, src_pad, dst_pad, st_d, tabf_d, tabi_d)
    nodes(nc, i['x'], i['L0_gnn_bias'], i['L0_gnn_gamma'], i['L0_gnn_beta'], i['L0_ffn_W1'], i['L0_ffn_b1'], i['L0_ffn_Wg'],
          i['L0_ffn_bg'], xn_d, st_d, routed_d, etab_d)
    experts(nc, i['L0_ffn_W1'], i['L0_ffn_b1'], i['L0_ffn_Wd'], i['L0_ffn_bd'], routed_d, etab_d, out)


def kernel(**inputs):
    import numpy as _np
    import concourse.bacc as _bacc
    from concourse.bass_utils import run_bass_kernel_spmd as _run

    nc = _bacc.Bacc("TRN2", target_bir_lowering=False, num_devices=1)
    arrays, aps = {}, {}
    for name in _INS:
        a = _np.ascontiguousarray(inputs[name])
        arrays[f"in_{name}_dram"] = a
        aps[name] = nc.dram_tensor(f"in_{name}_dram", a.shape, mybir.dt.from_np(a.dtype), kind="ExternalInput").ap()
    out = nc.dram_tensor("out_0_dram", (NODES, D), F32, kind="ExternalOutput").ap()
    program(nc, aps, out)
    r = _run(nc, [arrays], core_ids=[0])
    return r.results[0]["out_0_dram"]
```

```python
from contextlib import ExitStack
import concourse.bass as bass
from concourse import mybir

P = 128
F32 = mybir.dt.float32
F32R = mybir.dt.float32r
BF16 = mybir.dt.bfloat16
I32 = mybir.dt.int32
ALU = mybir.AluOpType
ACT = mybir.ActivationFunctionType
AX = mybir.AxisListType
EPS = 1e-5
NEG = -1e30
NODES, EDGES, D = 12500, 200000, 256
HEADS, HD = 8, 32
HS = HD + 1
C = 12
BLOCK = P * C
RING = 3
BLOCKS = -(-(-(-EDGES // BLOCK)) // RING) * RING
PADDED = BLOCKS * BLOCK
NODES_UP = (NODES // P + 2) * P
EXTRA = -(-(NODES // P) // RING) * RING
FAR = 20000
G = 3
SW = HEADS * HS + HEADS
XW = D + HEADS


def setup(nc, src, dst, src_pad, dst_pad, xr_d, rows_d, tabf_d, tabi_d):
    with ExitStack() as ctx:
        sb = lambda n, s, d=F32: ctx.enter_context(nc.sbuf_tensor(n, s, d))
        sem = lambda n: ctx.enter_context(nc.semaphore(n))
        tail = PADDED - EDGES
        tp = 64
        far = sb("far", [tp, tail // tp], I32); nil = sb("nil", [tp, tail // tp], I32)
        zx = sb("zx", [P, XW])
        fi = sb("fi", [1, 2, BLOCKS], I32); ff = sb("ff", [1, 2, BLOCKS])
        sp_f = sb("sp_f", [1, BLOCKS]); sp_i = sb("sp_i", [1, BLOCKS], I32); sh_i = sb("sh_i", [1, BLOCKS], I32)
        rows = sb("rows", [1, 3, BLOCKS]); inc = sb("inc", [1, BLOCKS]); one = sb("one", [1, BLOCKS])
        bc = sb("bc", [EXTRA, 3, BLOCKS]); m1 = sb("m1", [EXTRA, BLOCKS]); m2 = sb("m2", [EXTRA, BLOCKS]); m3 = sb("m3", [EXTRA, BLOCKS])
        siota = sb("siota", [EXTRA, BLOCKS]); j = sb("j", [EXTRA, 1]); j128 = sb("j128", [EXTRA, 1])
        red = sb("red", [EXTRA, 3]); res = sb("res", [EXTRA, 2]); resi = sb("resi", [EXTRA, 2], I32)
        firsti = sb("firsti", [1, BLOCKS], I32); tot = sb("tot", [1, 1]); toti = sb("toti", [1, 1], I32); tmp = sb("tmp", [EXTRA, 1])
        made = sem("setup_made"); filled = sem("filled"); loaded = sem("loaded"); v = sem("table_step"); wrote = sem("table_rows"); back = sem("rows_back"); done = sem("tables_stored"); io = sem("setup_iota")
        block = ctx.enter_context(nc.Block())

        @block.gpsimd
        def _(pool):
            pool.iota(siota[:], [[1, BLOCKS]], base=0, channel_multiplier=0, allow_small_or_imprecise_dtypes=True).then_inc(io, 1)
            pool.iota(j[:], [[0, 1]], base=0, channel_multiplier=1, allow_small_or_imprecise_dtypes=True).then_inc(io, 1)
            pool.iota(j128[:], [[0, 1]], base=P, channel_multiplier=P, allow_small_or_imprecise_dtypes=True).then_inc(io, 1)

        @block.sync
        def _(sp):
            sp.dma_start(dst_pad[0:EDGES].rearrange("(a b) -> a b", a=125), dst.rearrange("(a b) -> a b", a=125)).then_inc(filled, 16)
            sp.dma_start(src_pad[0:EDGES].rearrange("(a b) -> a b", a=125), src.rearrange("(a b) -> a b", a=125)).then_inc(filled, 16)
            sp.wait_ge(made, 3)
            sp.dma_start(dst_pad[EDGES:PADDED].rearrange("(a b) -> a b", a=tp), far[:]).then_inc(filled, 16)
            sp.dma_start(src_pad[EDGES:PADDED].rearrange("(a b) -> a b", a=tp), nil[:]).then_inc(filled, 16)
            sp.dma_start(xr_d[NODES:NODES + P, :], zx[:]).then_inc(filled, 16)
            sp.dma_start(xr_d[NODES + P:NODES_UP, :], zx[0:NODES_UP - NODES - P, :]).then_inc(filled, 16)
            sp.wait_ge(filled, 6 * 16)
            ends = dst_pad.rearrange("(o s e) -> o s e", o=1, e=BLOCK)
            with nc.allow_non_contiguous_dma(reason="one destination of each block"):
                sp.dma_start(fi[:, 0, :], ends[:, :, 0]).then_inc(loaded, 16)
                sp.dma_start(fi[:, 1, :], ends[:, :, BLOCK - 1]).then_inc(loaded, 16)
            sp.wait_ge(v, 8)
            sp.dma_start(rows_d[None, :, :], rows[:]).then_inc(wrote, 16)
            sp.dma_start(tabf_d[None, 0:BLOCKS], rows[:, 2, :]).then_inc(done, 16)
            sp.dma_start(tabi_d[None, 0, 0:BLOCKS], firsti[:]).then_inc(done, 16)
            sp.dma_start(tabi_d[None, 1, BLOCKS + EXTRA:BLOCKS + EXTRA + 1], toti[:]).then_inc(done, 16)
            sp.wait_ge(wrote, 16)
            sp.dma_start(bc[:], rows_d[None, :, :].to_broadcast([EXTRA, 3, BLOCKS])).then_inc(back, 16)
            sp.wait_ge(v, 21)
            with nc.allow_non_contiguous_dma(reason="a table row"):
                sp.dma_start(tabf_d[BLOCKS:BLOCKS + EXTRA, None], res[:, 0:1]).then_inc(done, 16)
                sp.dma_start(tabi_d[0, BLOCKS:BLOCKS + EXTRA, None], resi[:, 0:1]).then_inc(done, 16)
                sp.dma_start(tabi_d[1, BLOCKS:BLOCKS + EXTRA, None], resi[:, 1:2]).then_inc(done, 16)
            sp.wait_ge(done, 6 * 16)

        @block.vector
        def _(dve):
            dve.memset(far[:], FAR).then_inc(made, 1)
            dve.memset(nil[:], 0).then_inc(made, 1)
            dve.memset(zx[:], 0.0).then_inc(made, 1)
            dve.memset(one[:], 1.0)
            dve.wait_ge(loaded, 32)
            n = [0]

            def then(ins):
                n[0] += 1
                ins.then_inc(v, 1)
                dve.wait_ge(v, n[0])
            then(dve.tensor_scalar(ff[:, 0, :], fi[:, 0, :], float(NODES), None, ALU.min))
            then(dve.tensor_scalar(ff[:, 1, :], fi[:, 1, :], float(NODES - 1), None, ALU.min))
            then(dve.tensor_tensor(sp_f[:], ff[:, 1, :], ff[:, 0, :], ALU.subtract))
            then(dve.tensor_scalar(sp_i[:], sp_f[:], 0.0, None, ALU.max))
            then(dve.tensor_scalar(sh_i[:], sp_i[:], 7, None, ALU.arith_shift_right))
            dve.tensor_copy(firsti[:], ff[:, 0, :])
            dve.tensor_copy(rows[:, 2, :], ff[:, 0, :])
            then(dve.tensor_copy(rows[:, 1, :], sh_i[:]))
            then(dve.tensor_tensor_scan(inc[:], one[:], rows[:, 1, :], 0.0, ALU.mult, ALU.add))
            dve.tensor_copy(toti[:], inc[:, BLOCKS - 1:BLOCKS])
            then(dve.tensor_tensor(rows[:, 0, :], inc[:], rows[:, 1, :], ALU.subtract))
            dve.wait_ge(back, 16)
            dve.wait_ge(io, 3)
            then(dve.tensor_scalar(m1[:], bc[:, 0, :], j[:, 0:1], None, ALU.is_le))
            then(dve.tensor_tensor(m2[:], bc[:, 0, :], bc[:, 1, :], ALU.add))
            then(dve.tensor_scalar(m3[:], m2[:], j[:, 0:1], None, ALU.is_gt))
            then(dve.tensor_tensor(m1[:], m1[:], m3[:], ALU.mult))
            then(dve.tensor_scalar(m2[:], bc[:, 0, :], -float(P), j128[:, 0:1], ALU.mult, ALU.add))
            then(dve.tensor_tensor(m2[:], m2[:], bc[:, 2, :], ALU.add))
            then(dve.tensor_tensor(m2[:], m2[:], m1[:], ALU.mult))
            then(dve.tensor_tensor(m3[:], siota[:], m1[:], ALU.mult))
            dve.tensor_reduce(red[:, 0:1], m2[:], AX.X, ALU.add)
            dve.tensor_reduce(red[:, 1:2], m3[:], AX.X, ALU.add)
            then(dve.tensor_reduce(red[:, 2:3], m1[:], AX.X, ALU.add))
            then(dve.tensor_scalar(tmp[:], red[:, 2:3], -float(NODES), float(NODES), ALU.mult, ALU.add))
            dve.tensor_copy(res[:, 1:2], red[:, 1:2])
            then(dve.tensor_tensor(res[:, 0:1], red[:, 0:1], tmp[:], ALU.add))
            then(dve.tensor_copy(resi[:], res[:]))
            then(dve.tensor_copy(tmp[:], res[:, 0:1]))


def edges(nc, passed, att, xl_d, xr_d, src_pad, dst_pad, st_d, tabf_d, tabi_d):
    with ExitStack() as ctx:
        sb = lambda n, s, d=F32: ctx.enter_context(nc.sbuf_tensor(n, s, d))
        ps = lambda n, s, d=F32: ctx.enter_context(nc.psum_tensor(n, s, d))
        sem = lambda n: ctx.enter_context(nc.semaphore(n))
        ring = lambda n: [sem(f"{n}{r}") for r in range(RING)]
        idx = sb("idx", [P, RING, C], I32); dsti = sb("dsti", [P, RING, C], I32); base = sb("base", [P, RING, 1])
        xrw = sb("xrw", [P, RING, XW]); xrp = sb("xrp", [P, RING, 2, D], F32R); xl = sb("xl", [P, RING, C, XW]); px = sb("px", [P, RING, C, HEADS, HS])
        dst8 = sb("dst8", [P, RING, C, HEADS]); rel = sb("rel", [P, RING, C])
        hot = sb("hot", [P, RING, C, P], F32R); hotT = sb("hotT", [P, RING, C * P], F32R)
        s = sb("s", [P, 2, 512 * 3])
        att_sb = sb("att_sb", [P, 2, HEADS])
        e_sb = sb("e_sb", [P, RING, C, HEADS])
        dts = sb("dts", [C * HEADS, P]); reset = sb("reset", [C * HEADS, P + 1]); runmax = sb("runmax", [C * HEADS, P]); lastmax = sb("lastmax", [C * HEADS, P])
        rh = sb("rh", [P, C, 3, HEADS + 1], BF16); rrest = sb("rrest", [P, C, HEADS]); hotb = sb("hotb", [P, RING, C, P], BF16); mh = sb("mh", [P, 3, HEADS], BF16); mrest = sb("mrest", [P, HEADS]); hotTb = sb("hotTb", [P, RING, C * P], BF16); vsum = sb("vsum", [P, C, HEADS]); mback = sb("mback", [P, C * HEADS]); pen = sb("pen", [P, C]); vs = sb("vs", [P, C, HEADS])
        mraw = sb("mraw", [P, HEADS]); m = sb("m", [P, RING, 2 * HEADS]); d = sb("d", [P, C, HEADS]); dm = sb("dm", [P, C, HEADS])
        st = sb("st", [P, RING, SW]); new = sb("new", [P, RING, SW]); mn = sb("mn", [P, HEADS]); dd = sb("dd", [P, 2, HEADS]); ab = sb("ab", [P, 2, HEADS])
        t2 = sb("t2", [P, HEADS * HS]); ones_and_zeros = sb("ones_and_zeros", [P, C, 3])
        ident = sb("ident2", [P, P]); identr = sb("identr", [P, P], F32R); ones = sb("ones2", [P, P]); iota = sb("iota2", [P, P])
        tab = sb("tab", [1, 2, BLOCKS + EXTRA + 1], I32)
        psz = ps("psz", [P, 2, 512]); psot = ps("psot", [P, G, 512], F32R); pss = ps("pss", [P, 512]); psv = ps("psv", [P, 512]); psa = ps("psa", [P, 512])
        ps_e = pss[:, 0:96]
        ps_et = psv[0:96, 0:128]; ps_dt = psv[0:96, 128:256]; ps_fm = psv[:, 256:352]
        ps_v = psv[:, 0:C * 3 * (HEADS + 1)].rearrange("p (c s h) -> p c s h", c=C, s=3); ps_m = psv[:, 0:C * 3 * HEADS].rearrange("p (c s h) -> p c s h", c=C, s=3)
        idx_in = ring("idx_in"); win_in = ring("win_in"); st_in = ring("st_in"); xl_in = ring("xl_in"); stored = ring("stored")
        
        consts = sem("consts2"); cz = sem("cz2"); oz = sem("oz"); attin = sem("attin")
        hot_made = sem("hot_made"); ot_tr = sem("ot_tr"); ot_copied = sem("ot_copied"); z_made = sem("z_made"); s_made = sem("s_made"); e_made = sem("e_made"); e_copied = sem("e_copied")
        rel_made = sem("rel_made"); xh_made = sem("xh_made"); xrp_made = sem("xrp_made")
        et_made = sem("et_made"); dts_made = sem("dts_made"); reset_made = sem("reset_made"); run_made = sem("run_made"); fm_made = sem("fm_made"); fmt_made = sem("fmt_made"); rh_made = sem("rh_made"); rl_made = sem("rl_made"); rrest_made = sem("rrest_made"); rm_made = sem("rm_made"); hotb_made = sem("hotb_made"); mh_made = sem("mh_made"); mrest_made = sem("mrest_made"); mm_made = sem("mm_made"); ml_made = sem("ml_made"); mback_made = sem("mback_made"); vsum_made = sem("vsum_made"); otb_copied = sem("otb_copied")
        v_made = sem("v_made"); pen_made = sem("pen_made"); vs_made = sem("vs_made"); m_made = sem("m_made"); mraw_made = sem("mraw_made"); me_made = sem("me_made"); d_made = sem("d_made"); dm_made = sem("dm_made"); p_made = sem("p_made"); px_made = sem("px_made")
        a_made = sem("a_made"); mn_made = sem("mn_made"); dd_made = sem("dd_made"); ab_made = sem("ab_made"); new_part = sem("new_part"); t2_made = sem("t2_made"); new_made = sem("new_made")
        block = ctx.enter_context(nc.Block())

        def pipeline(eng, slot, first_hot, k0, n):
            first_hot(k0, 0, k0 // RING)
            for k in range(3):
                slot(k0 + k, k, (k0 + k) // RING, a=True, b=k >= 1, c=k >= 2)
            with eng.Fori(1, n // RING - 1) as i:
                for r in range(RING):
                    slot(k0 + RING * i + r, r, i + k0 // RING, a=True, b=True, c=True)
            kk = k0 + n - RING
            for r in range(RING):
                slot(kk + r, r, kk // RING, a=True, b=True, c=True, ahead=r < 2)
            slot(k0 + n, 0, (k0 + n) // RING, a=False, b=True, c=True)
            slot(k0 + n + 1, 1, (k0 + n) // RING, a=False, b=False, c=True)

        @block.sync
        def _(sp):
            sp.wait_ge(consts, 4)
            sp.dma_start(tab[:, 0, 0:BLOCKS + EXTRA], tabi_d[None, 0, 0:BLOCKS + EXTRA]).then_inc(attin, 16)
            sp.dma_start(tab[:, 1, BLOCKS:], tabi_d[None, 1, BLOCKS:]).then_inc(attin, 16)
            with nc.allow_non_contiguous_dma(reason="attention weights by feature"):
                for h in range(HEADS):
                    p0 = h % 4 * HD
                    sp.dma_start(att_sb[p0:p0 + HD, h // 4, h:h + 1], att[h, :, None]).then_inc(attin, 16)
            sp.wait_ge(attin, 16 * 10)
            W = tab[0:1, 0, :]
            B = tab[0:1, 1, :]
            srcv = src_pad.rearrange("(s p j) -> s p j", p=P, j=C)
            dstv = dst_pad.rearrange("(s p j) -> s p j", p=P, j=C)
            one = lambda x: slice(x, x + 1) if isinstance(x, int) else bass.ds(x, 1)
            rows = lambda w: bass.ds(w, P)

            def which(k, extra):
                if not extra:
                    return k
                return sp.value_load(B[:, one(k)], min_val=0, max_val=BLOCKS - 1)

            def window(k):
                return sp.value_load(W[:, one(k)], min_val=0, max_val=NODES)

            def load_idx(k, r, extra):
                sp.dma_start(idx[:, r, :], srcv[one(which(k, extra)), :, :].rearrange("o p j -> p (o j)")).then_inc(idx_in[r], 16)

            def load_window(k, r, extra):
                sp.dma_start(dsti[:, r, :], dstv[one(which(k, extra)), :, :].rearrange("o p j -> p (o j)")).then_inc(win_in[r], 16)
                sp.dma_start(base[:, r, :], tabf_d[one(k)].rearrange("(o k) -> o k", o=1).to_broadcast([P, 1])).then_inc(win_in[r], 16)
                sp.dma_start(xrw[:, r, :], xr_d[rows(window(k)), :]).then_inc(win_in[r], 16)

            def load_state(k, r):
                sp.dma_start(st[:, r, :], st_d[rows(window(k)), :]).then_inc(st_in[r], 16)

            def settle():
                sp.sem_inc(passed, 1)

            def run(k0, n, extra):
                for k in range(3):
                    load_idx(k0 + k, k, extra)
                for k in range(2):
                    load_window(k0 + k, k, extra)
                load_state(k0, 0)

                def slot(k, r, u, a, b, c, ahead_idx=True, ahead_win=True):
                    if ahead_idx:
                        sp.wait_ge(xl_in[r], 16 * C * (u + 1))
                        settle()
                        load_idx(k + 3, r, extra)
                    if ahead_win:
                        q = (r + 2) % RING
                        if not (isinstance(k, int) and k == k0):
                            sp.wait_ge(xrp_made, k)
                            settle()
                            sp.wait_ge(rel_made, 2 * k)
                            settle()
                        load_window(k + 2, q, extra)
                    if c:
                        q = (r + 1) % RING
                        sp.wait_ge(new_made, k - 1)
                        settle()
                        sp.dma_start(st_d[rows(window(k - 2)), :], new[:, q, :]).then_inc(stored[q], 16)
                        sp.wait_ge(stored[q], 16 * (u + 1 if r >= 2 else u))
                        settle()
                    if b:
                        q = (r + 2) % RING
                        if not (isinstance(k, int) and k - 1 == k0):
                            load_state(k - 1, q)
                for k in range(3):
                    slot(k0 + k, k, (k0 + k) // RING, True, k >= 1, k >= 2)
                with sp.Fori(1, n // RING - 1) as i:
                    for r in range(RING):
                        slot(k0 + RING * i + r, r, i + k0 // RING, True, True, True)
                kk = k0 + n - RING
                for r in range(RING):
                    slot(kk + r, r, kk // RING, True, True, True, ahead_idx=False, ahead_win=r == 0)
                slot(k0 + n, 0, (k0 + n) // RING, False, True, True, False, False)
                slot(k0 + n + 1, 1, (k0 + n) // RING, False, False, True, False, False)
            run(0, BLOCKS, False)
            more = sp.value_load(B[:, BLOCKS + EXTRA:BLOCKS + EXTRA + 1], min_val=0, max_val=EXTRA)
            with sp.If(more > 0):
                run(BLOCKS, EXTRA, True)

        @block.gpsimd
        def _(pool):
            pool.memset(ones[:], 1.0).then_inc(cz, 1)
            pool.wait_ge(cz, 1)
            pool.affine_select(out=ident[:], in_=ones[:], compare_op=ALU.is_equal, fill=0.0, base=0, pattern=[[-1, P]], channel_multiplier=1).then_inc(cz, 1)
            pool.iota(iota[:], [[1, P]], base=0, channel_multiplier=0, allow_small_or_imprecise_dtypes=True).then_inc(consts, 1)

            def gathers(k, r, u, free=True):
                pool.wait_ge(idx_in[r], 16 * (u + 1))
                for j in range(C):
                    if j % (C // 2) == 0:
                        pool.sem_inc(passed, 1)
                        if free:
                            pool.wait_ge(px_made, 2 * (k - 3) + 1 + j // (C // 2))
                            pool.sem_inc(passed, 1)
                    pool.indirect_dma_start(xl[:, r, j, :], None, xl_d[:, :], bass.IndirectOffsetOnAxis(idx[:, r, j:j + 1], 0),
                                            bounds_check=NODES - 1, oob_is_err=False).then_inc(xl_in[r], 16)

            def run(k0, n):
                for r in range(RING):
                    gathers(k0 + r, r, k0 // RING, free=k0 > 0)
                with pool.Fori(1, n // RING) as i:
                    for r in range(RING):
                        gathers(k0 + RING * i + r, r, i + k0 // RING)
            run(0, BLOCKS)
            pool.wait_ge(attin, 16 * 10)
            more = pool.value_load(tab[0:1, 1, BLOCKS + EXTRA:BLOCKS + EXTRA + 1], min_val=0, max_val=EXTRA)
            with pool.If(more > 0):
                run(BLOCKS, EXTRA)

        @block.vector
        def _(dve):
            dve.memset(ones_and_zeros[:, :, 0:1], 1.0)
            dve.memset(ones_and_zeros[:, :, 1:3], 0.0).then_inc(oz, 1)
            dve.wait_ge(oz, 1)
            dve.memset(reset[:, 0:1], 0.0)
            dve.memset(reset[:, P:P + 1], -1.0)
            dve.memset(att_sb[:], 0.0).then_inc(consts, 1)
            dve.tensor_copy(rh[:, :, :, HEADS], ones_and_zeros[:]).then_inc(consts, 1)
            dve.wait_ge(cz, 2)
            dve.tensor_copy(identr[:], ident[:]).then_inc(consts, 1)
            dve.wait_ge(consts, 4)

            def make_hot(k, r, u):
                dve.wait_ge(win_in[r], 48 * (u + 1))
                if not (isinstance(k, int) and k < 3):
                    dve.wait_ge(et_made, k - 2)
                if not (isinstance(k, int) and k < 3):
                    dve.wait_ge(z_made, 6 * (k - 2))
                dve.tensor_copy(m[:, r, HEADS:2 * HEADS], xrw[:, r, D:XW])
                dve.tensor_copy(xrp[:, r, 0, :], xrw[:, r, 0:D]).then_inc(xh_made, 1)
                dve.tensor_copy(dst8[:, r, :, :], dsti[:, r, :].unsqueeze(2).to_broadcast([P, C, HEADS])).then_inc(rel_made, 1)
                dve.tensor_scalar(rel[:, r, :], dsti[:, r, :], base[:, r, 0:1], None, ALU.subtract).then_inc(rel_made, 1)
                dve.wait_ge(rel_made, 2 * k + 2)
                dve.wait_ge(xh_made, k + 1)
                dve.tensor_tensor(xrp[:, r, 1, :], xrw[:, r, 0:D], xrp[:, r, 0, :], ALU.subtract).then_inc(xrp_made, 1)
                if not (isinstance(k, int) and k < 3):
                    dve.wait_ge(a_made, k - 2)
                for g in range(G):
                    dve.tensor_tensor(hot[:, r, 4 * g:4 * g + 4, :], iota[:].unsqueeze(1).to_broadcast([P, 4, P]),
                                      rel[:, r, 4 * g:4 * g + 4].unsqueeze(2).to_broadcast([P, 4, P]), ALU.is_equal).then_inc(hot_made, 1)

            def slot(k, r, u, a, b, c, ahead=True):
                qb = (r + 2) % RING
                qc = (r + 1) % RING
                if b:
                    dve.wait_ge(e_made, 3 * k)
                    dve.tensor_tensor(e_sb[:, qb, :, :], xl[:, qb, :, D:XW], ps_e.rearrange("p (c h) -> p c h", h=HEADS), ALU.add).then_inc(e_copied, 1)
                if c:
                    uc = u + 1 if r >= 2 else u
                    dve.wait_ge(st_in[qc], 16 * uc)
                    dve.wait_ge(m_made, k - 1)
                    dve.tensor_tensor(mn[:], st[:, qc, HEADS * HS:SW], m[:, qc, 0:HEADS], ALU.max).then_inc(mn_made, 1)
                    dve.wait_ge(mn_made, k - 1)
                    dve.tensor_tensor(dd[:, 0, :], st[:, qc, HEADS * HS:SW], mn[:], ALU.subtract)
                    dve.tensor_tensor(dd[:, 1, :], m[:, qc, 0:HEADS], mn[:], ALU.subtract).then_inc(dd_made, 1)
                if b:
                    dve.wait_ge(et_made, k)
                    dve.tensor_scalar(dts[:], ps_dt, -NEG, None, ALU.mult).then_inc(dts_made, 1)
                    dve.wait_ge(dts_made, k)
                    dve.tensor_tensor(reset[:, 1:P], dts[:, 0:P - 1], dts[:, 1:P], ALU.subtract).then_inc(reset_made, 1)
                    dve.wait_ge(reset_made, k)
                    dve.tensor_tensor_scan(runmax[:], reset[:, 0:P], ps_et, NEG, ALU.add, ALU.max).then_inc(run_made, 1)
                    dve.wait_ge(run_made, k)
                    dve.scalar_tensor_tensor(out=lastmax[:], in0=reset[:, 1:P + 1], scalar=0.0, in1=runmax[:], op0=ALU.is_lt, op1=ALU.mult).then_inc(fm_made, 1)
                if c:
                    dve.wait_ge(ab_made, k - 1)
                    bro = lambda i: ab[:, i, :].unsqueeze(2).to_broadcast([P, HEADS, HS])
                    hv = lambda x: x.rearrange("p (h f) -> p h f", f=HS)
                    dve.tensor_tensor(hv(new[:, qc, 0:HEADS * HS]), hv(st[:, qc, 0:HEADS * HS]), bro(0), ALU.mult).then_inc(new_part, 1)
                    dve.tensor_copy(new[:, qc, HEADS * HS:SW], mn[:])
                if b:
                    dve.wait_ge(rh_made, k)
                    dve.tensor_tensor(rrest[:], ps_fm.rearrange("p (c h) -> p c h", h=HEADS), rh[:, :, 0, 0:HEADS], ALU.subtract).then_inc(rrest_made, 1)
                    dve.wait_ge(rrest_made, k)
                    dve.tensor_copy(rh[:, :, 1, 0:HEADS], rrest[:]).then_inc(rm_made, 1)
                    dve.wait_ge(rm_made, k)
                    dve.tensor_tensor(rh[:, :, 2, 0:HEADS], rrest[:], rh[:, :, 1, 0:HEADS], ALU.subtract).then_inc(rl_made, 1)
                    dve.wait_ge(v_made, k)
                    dve.tensor_scalar(pen[:], ps_v[:, :, 0, HEADS], 0.0, NEG, ALU.is_equal, ALU.mult).then_inc(pen_made, 1)
                    dve.tensor_reduce(vsum[:], ps_v[:, :, :, 0:HEADS].rearrange("p c s h -> p c h s"), AX.X, ALU.add).then_inc(vsum_made, 1)
                    dve.wait_ge(pen_made, k)
                    dve.wait_ge(vsum_made, k)
                    dve.tensor_tensor(vs[:], vsum[:], pen[:].unsqueeze(2).to_broadcast([P, C, HEADS]), ALU.add).then_inc(vs_made, 1)
                    dve.wait_ge(vs_made, k)
                    dve.tensor_reduce(mraw[:], vs[:].rearrange("p c h -> p h c"), AX.X, ALU.max).then_inc(mraw_made, 1)
                    dve.wait_ge(mraw_made, k)
                    dve.tensor_copy(mh[:, 0, :], mraw[:]).then_inc(mh_made, 1)
                    dve.wait_ge(mh_made, k)
                    dve.tensor_tensor(mrest[:], mraw[:], mh[:, 0, :], ALU.subtract).then_inc(mrest_made, 1)
                    dve.wait_ge(mrest_made, k)
                    dve.tensor_copy(mh[:, 1, :], mrest[:]).then_inc(mm_made, 1)
                    dve.wait_ge(mm_made, k)
                    dve.tensor_tensor(mh[:, 2, :], mrest[:], mh[:, 1, :], ALU.subtract).then_inc(ml_made, 1)
                    dve.tensor_tensor(m[:, qb, 0:HEADS], mraw[:], m[:, qb, HEADS:2 * HEADS], ALU.add).then_inc(m_made, 1)
                if c:
                    dve.wait_ge(a_made, k - 1)
                    dve.tensor_tensor(hv(t2[:]), hv(psa[:, 0:HEADS * HS]), bro(1), ALU.mult).then_inc(t2_made, 1)
                    dve.wait_ge(t2_made, k - 1)
                    dve.wait_ge(new_part, k - 1)
                    dve.tensor_tensor(new[:, qc, 0:HEADS * HS], new[:, qc, 0:HEADS * HS], t2[:], ALU.add).then_inc(new_made, 1)
                if b:
                    dve.wait_ge(me_made, k)
                    dve.tensor_reduce(mback[:].rearrange("p (c h) -> p c h", c=C), ps_m.rearrange("p c s h -> p c h s"), AX.X, ALU.add).then_inc(mback_made, 1)
                    dve.wait_ge(mback_made, k)
                    dve.tensor_tensor(d[:], e_sb[:, qb, :, :], mback[:].rearrange("p (c h) -> p c h", c=C), ALU.subtract).then_inc(d_made, 1)
                    dve.wait_ge(d_made, k)
                    dve.tensor_scalar(dm[:], d[:], 0.0, None, ALU.min).then_inc(dm_made, 1)
                if a and ahead:
                    make_hot(k + 1, (r + 1) % RING, u + 1 if r == 2 else u)
                if b:
                    dve.wait_ge(p_made, k)
                    dve.wait_ge(xl_in[qb], 16 * C * (u if r == 0 else u + 1))
                    for g in range(2):
                        cs = slice(g * C // 2, (g + 1) * C // 2)
                        xv = xl[:, qb, cs, 0:D].rearrange("p c (h f) -> p c h f", f=HD)
                        pv = px[:, qb, cs, :, :]
                        dve.tensor_tensor(pv[:, :, :, 0:HD], xv, pv[:, :, :, HD:HS].to_broadcast([P, C // 2, HEADS, HD]), ALU.mult).then_inc(px_made, 1)

            pipeline(dve, slot, make_hot, 0, BLOCKS)
            dve.wait_ge(attin, 16 * 10)
            more = dve.value_load(tab[0:1, 1, BLOCKS + EXTRA:BLOCKS + EXTRA + 1], min_val=0, max_val=EXTRA)
            with dve.If(more > 0):
                pipeline(dve, slot, make_hot, BLOCKS, EXTRA)

        @block.scalar
        def _(act):
            def copy_hotT(k, r, u):
                for g in range(G):
                    act.wait_ge(ot_tr, 3 * k + g + 1)
                    if not (isinstance(k, int) and k < 3):
                        act.wait_ge(z_made, 6 * (k - 2))
                    act.copy(hotT[:, r, 512 * g:512 * g + 512], psot[:, g, :]).then_inc(ot_copied, 1)

            def slot(k, r, u, a, b, c, ahead=True):
                qb = (r + 2) % RING

                def leaky(g, h):
                    act.wait_ge(z_made, 6 * k + 2 * g + h + 1)
                    if not (isinstance(k, int) and k == 0):
                        act.wait_ge(e_made, 3 * (k - 1) + g + 1)
                    act.activation(s[:, h, 512 * g:512 * g + 512], psz[:, h, :], ACT.Relu, scale=0.8).then_inc(s_made, 1)
                if a:
                    leaky(0, 0)
                    leaky(0, 1)
                if c:
                    act.wait_ge(dd_made, k - 1)
                    if not (isinstance(k, int) and k < 3):
                        act.wait_ge(t2_made, k - 2)
                    act.activation(ab[:], dd[:], ACT.Exp).then_inc(ab_made, 1)
                if a:
                    if not (isinstance(k, int) and k < 3):
                        act.wait_ge(me_made, k - 2)
                    for g in range(G):
                        act.copy(hotTb[:, r, 512 * g:512 * g + 512], psot[:, g, :]).then_inc(otb_copied, 1)
                    act.wait_ge(hot_made, 3 * (k + 1))
                    act.copy(hotb[:, r, :, :], hot[:, r, :, :]).then_inc(hotb_made, 1)
                if b:
                    act.wait_ge(fmt_made, k)
                    act.copy(rh[:, :, 0, 0:HEADS], ps_fm.rearrange("p (c h) -> p c h", h=HEADS)).then_inc(rh_made, 1)
                if a:
                    leaky(1, 0)
                    leaky(1, 1)
                    leaky(2, 0)
                if b:
                    act.wait_ge(dm_made, k)
                    act.activation(px[:, qb, :, :, HD], dm[:], ACT.Exp).then_inc(p_made, 1)
                if a:
                    leaky(2, 1)
                if a and ahead:
                    copy_hotT(k + 1, (r + 1) % RING, u + 1 if r == 2 else u)
            act.wait_ge(consts, 4)
            pipeline(act, slot, copy_hotT, 0, BLOCKS)
            act.wait_ge(attin, 16 * 10)
            more = act.value_load(tab[0:1, 1, BLOCKS + EXTRA:BLOCKS + EXTRA + 1], min_val=0, max_val=EXTRA)
            with act.If(more > 0):
                pipeline(act, slot, copy_hotT, BLOCKS, EXTRA)

        @block.tensor
        def _(pe):
            pe.wait_ge(consts, 4)
            pe.wait_ge(attin, 16 * 10)

            def turn_hot(k, r, u):
                for g in range(G):
                    pe.wait_ge(hot_made, 3 * k + g + 1)
                    if not (isinstance(k, int) and k == 0):
                        pe.wait_ge(otb_copied, 3 * (k - 1) + g + 1)
                    for c_ in range(4):
                        last = pe.transpose(psot[:, g, P * c_:P * c_ + P], hot[:, r, 4 * g + c_, :], identr[:])
                    last.then_inc(ot_tr, 1)

            def slot(k, r, u, a, b, c, ahead=True):
                qb = (r + 2) % RING
                qc = (r + 1) % RING
                first = isinstance(k, int) and k == 0

                def z(g, h):
                    if h == 0:
                        pe.wait_ge(ot_copied, 3 * k + g + 1)
                    if g == 0 and h == 0:
                        pe.wait_ge(xl_in[r], 16 * C * (u + 1))
                        pe.wait_ge(xrp_made, k + 1)
                    if not (first and g == 0):
                        pe.wait_ge(s_made, 6 * k + 2 * g + h - 1)
                    for part in range(2):
                        pe.matmul(psz[:, h, :], xrp[:, r, part, P * h:P * h + P], hotT[:, r, 512 * g:512 * g + 512], start=part == 0, stop=False)
                    for c_ in range(4):
                        last = pe.matmul(psz[:, h, P * c_:P * c_ + P], xl[:, r, 4 * g + c_, P * h:P * h + P], ident[:],
                                         is_transpose=True, start=False, stop=c_ == 3)
                    last.then_inc(z_made, 1)

                def scores(k, g, half):
                    if half == 0:
                        pe.wait_ge(s_made, 6 * k + 2 * g + 2)
                    for c_ in range(2 * half, 2 * half + 2):
                        j = 4 * g + c_
                        for h in range(2):
                            last = pe.matmul(ps_e[:, HEADS * j:HEADS * j + HEADS], s[:, h, P * j:P * j + P], att_sb[:, h, :], start=h == 0, stop=h == 1)
                    if half == 1:
                        last.then_inc(e_made, 1)

                def sums(j0, j1):
                    for j in range(j0, j1):
                        last = pe.matmul(psa[:, 0:HEADS * HS], hot[:, qc, j, :].bitcast(F32), px[:, qc, j, :, :].rearrange("p h f -> p (h f)"), start=j == 0, stop=j == C - 1)
                    if j1 == C:
                        last.then_inc(a_made, 1)
                if a:
                    z(0, 0)
                if b:
                    scores(k - 1, 2, 0)
                if a:
                    z(0, 1)
                if b:
                    scores(k - 1, 2, 1)
                if c:
                    pe.wait_ge(px_made, 2 * (k - 1))
                    if not (isinstance(k, int) and k < 3):
                        pe.wait_ge(t2_made, k - 2)
                    sums(0, 2)
                if b:
                    pe.wait_ge(e_copied, k)
                    if not (isinstance(k, int) and k < 2):
                        pe.wait_ge(mback_made, k - 1)
                    pe.transpose(ps_et, e_sb[:, qb, :, :].rearrange("p c h -> p (c h)"), ident[:])
                    pe.transpose(ps_dt, dst8[:, qb, :, :].rearrange("p c h -> p (c h)"), ident[:]).then_inc(et_made, 1)
                if a:
                    scores(k, 0, 0)
                if c:
                    sums(2, 5)
                if b:
                    pe.wait_ge(fm_made, k)
                    pe.transpose(ps_fm, lastmax[:], ident[0:C * HEADS, 0:C * HEADS]).then_inc(fmt_made, 1)
                if a:
                    scores(k, 0, 1)
                if c:
                    sums(5, 9)
                if b:
                    pe.wait_ge(rl_made, k)
                    pe.wait_ge(hotb_made, k)
                    for j in range(C):
                        last = pe.matmul(ps_v[:, j, :, :], hotb[:, qb, j, :], rh[:, j, :, :], start=True, stop=True)
                    last.then_inc(v_made, 1)
                if c:
                    sums(9, C)
                if a:
                    z(1, 0)
                    z(1, 1)
                if b:
                    pe.wait_ge(ml_made, k)
                    for j in range(C):
                        last = pe.matmul(ps_m[:, j, :, :], hotTb[:, qb, P * j:P * j + P], mh[:], start=True, stop=True)
                    last.then_inc(me_made, 1)
                if a:
                    z(2, 0)
                    scores(k, 1, 0)
                    z(2, 1)
                    scores(k, 1, 1)
                if a and ahead:
                    turn_hot(k + 1, (r + 1) % RING, u + 1 if r == 2 else u)
            pipeline(pe, slot, turn_hot, 0, BLOCKS)
            more = pe.value_load(tab[0:1, 1, BLOCKS + EXTRA:BLOCKS + EXTRA + 1], min_val=0, max_val=EXTRA)
            with pe.If(more > 0):
                pipeline(pe, slot, turn_hot, BLOCKS, EXTRA)


def project(nc, passed, x, Wl, Wr, bl, br, att, xn_d, xl_d, xr_d, st_d):
    T = 4
    ROWS = T * P
    GROUPS = -(-NODES // ROWS)
    with ExitStack() as ctx:
        sb = lambda n, s, d=F32: ctx.enter_context(nc.sbuf_tensor(n, s, d))
        ps = lambda n, s, d=F32: ctx.enter_context(nc.psum_tensor(n, s, d))
        sem = lambda n: ctx.enter_context(nc.semaphore(n))
        xb = sb("xb", [P, 2, T, D]); xnb = sb("xnb", [P, 2, T, D]); xT = sb("xT", [P, 2, 2, ROWS])
        W = sb("W", [P, 2, 2 * D]); bias = sb("bias", [P, 2, D]); att_row = sb("att_row", [P, 2, D]); att_02 = sb("att_02", [P, 2, D])
        lr = sb("lr", [P, 2, T, 2, XW]); weighted = sb("weighted", [P, T, 2, D])
        stats = sb("stats", [P, T, 6]); mv = sb("mv", [P, 2, T, 2]); ve = sb("ve", [P, 2, T]); half = sb("half", [P, T]); rstd = sb("rstd", [P, 2, T])
        ident = sb("ident", [P, P]); ones = sb("ones", [P, P])
        empty = sb("empty", [P, SW]); empty_made = sem("empty_made"); st_filled = sem("st_filled")
        psT = ps("psT", [P, 2, 2, 512]); psY = ps("psY", [P, T, 512])
        consts = sem("consts"); cones = sem("cones"); wload = sem("wload"); att_made = sem("att_made")
        x_in = [sem("x_in0"), sem("x_in1")]
        xn_out = [sem("xn_out0"), sem("xn_out1")]
        lr_out = [sem("lr_out0"), sem("lr_out1")]
        stats_made = sem("stats_made"); mv_made = sem("mv_made"); ve_made = sem("ve_made"); rstd_made = sem("rstd_made"); xn_made = sem("xn_made")
        turned = sem("turned"); xT_made = sem("xT_made"); y_made = sem("y_made"); biased = sem("biased"); weighted_made = sem("weighted_made"); lr_made = sem("lr_made")
        block = ctx.enter_context(nc.Block())

        def rows(a, g):
            at = slice(NODES - ROWS, NODES) if isinstance(g, int) and g == GROUPS - 1 else bass.ds(g * ROWS, ROWS)
            return a[at, :].rearrange("(q p) c -> p q c", p=P)

        def groups(eng, slot):
            slot(0, 0, 0)
            with eng.Fori(1, GROUPS // 2 - 1) as i:
                slot(2 * i - 1, 1, i - 1)
                slot(2 * i, 0, i)
            for g in range(GROUPS - 4, GROUPS):
                slot(g, g % 2, g // 2)

        is_last = lambda g, n: isinstance(g, int) and g + n >= GROUPS

        @block.sync
        def _(sp):
            for h in range(2):
                sp.dma_start(W[:, h, 0:D], Wl[h * P:h * P + P, :]).then_inc(wload, 16)
                sp.dma_start(W[:, h, D:2 * D], Wr[h * P:h * P + P, :]).then_inc(wload, 16)
            sp.dma_start(xb[:, 0, :, :], rows(x, 0)).then_inc(x_in[0], 16)
            sp.dma_start(xb[:, 1, :, :], rows(x, 1)).then_inc(x_in[1], 16)
            for side, b in ((0, bl), (1, br)):
                sp.dma_start(bias[:, side, :], b[None, :].to_broadcast([P, D])).then_inc(wload, 16)
                sp.dma_start(att_row[:, side, :], att.rearrange("(o h) f -> o (h f)", o=1).to_broadcast([P, D])).then_inc(wload, 16)

            def normed(g, b, u):
                sp.wait_ge(xn_made, g + 1)
                if is_last(g, 1):
                    sp.wait_ge(xn_out[1 - b], 16 * u)
                sp.dma_start(rows(xn_d, g), xnb[:, b, :, :]).then_inc(xn_out[b], 16)
                if not is_last(g, 2):
                    sp.dma_start(xb[:, b, :, :], rows(x, g + 2)).then_inc(x_in[b], 16)
            state = lambda q: empty[:].rearrange("p (o c) -> p o c", o=1).to_broadcast([P, q, SW])
            sp.wait_ge(empty_made, 2)
            sp.dma_start(st_d[(GROUPS - 1) * ROWS:NODES_UP, :].rearrange("(q p) c -> p q c", p=P), state(NODES_UP // P - (GROUPS - 1) * T)).then_inc(st_filled, 16)
            normed(0, 0, 0)

            def slot(g, b, u):
                if not is_last(g, 1):
                    sp.dma_start(rows(st_d, g), state(T)).then_inc(st_filled, 16)
                if not is_last(g, 1):
                    normed(g + 1, 1 - b, u + b)
                sp.wait_ge(lr_made, g + 1)
                if is_last(g, 1):
                    sp.wait_ge(lr_out[1 - b], 32 * u)
                sp.dma_start(rows(xl_d, g), lr[:, b, :, 0, :]).then_inc(lr_out[b], 16)
                sp.dma_start(rows(xr_d, g), lr[:, b, :, 1, :]).then_inc(lr_out[b], 16)
            groups(sp, slot)
            sp.wait_ge(st_filled, 16 * GROUPS)
            sp.wait_ge(xn_out[0], 16 * (GROUPS // 2 + 1))
            sp.wait_ge(xn_out[1], 16 * (GROUPS // 2))
            sp.wait_ge(lr_out[0], 32 * (GROUPS // 2 + 1))
            sp.wait_ge(lr_out[1], 32 * (GROUPS // 2))

        @block.gpsimd
        def _(pool):
            pool.memset(ones[:], 1.0).then_inc(cones, 1)
            pool.memset(half[:], -0.5).then_inc(consts, 1)
            pool.memset(empty[:, 0:HEADS * HS], 0.0).then_inc(empty_made, 1)
            pool.memset(empty[:, HEADS * HS:SW], NEG).then_inc(empty_made, 1)
            pool.wait_ge(cones, 1)
            pool.affine_select(out=ident[:], in_=ones[:], compare_op=ALU.is_equal, fill=0.0, base=0, pattern=[[-1, P]], channel_multiplier=1).then_inc(consts, 1)
            pool.wait_ge(consts, 2)

            def inverse_deviation(g, b):
                pool.wait_ge(ve_made, g + 1)
                pool.tensor_tensor(rstd[:, b, :], ve[:, b, :], half[:], ALU.pow).then_inc(rstd_made, 1)
            inverse_deviation(0, 0)
            inverse_deviation(1, 1)
            pool.wait_ge(att_made, 1)

            def slot(g, b, u):
                for q in range(T):
                    pool.wait_ge(biased, T * g + q + 1)
                    if not (isinstance(g, int) and g == 0):
                        pool.wait_ge(lr_made, g)
                    pool.tensor_tensor(weighted[:, q, :, :], lr[:, b, q, :, 0:D], att_02[:], ALU.mult).then_inc(weighted_made, 1)
                if not is_last(g, 2):
                    inverse_deviation(g + 2, b)
            groups(pool, slot)

        @block.vector
        def _(dve):
            def statistics(g, b, u):
                dve.wait_ge(x_in[b], 16 * (u + 1))
                if not (isinstance(g, int) and g == 0):
                    dve.wait_ge(mv_made, g)
                for q in range(T):
                    dve.bn_stats(stats[:, q, :], xb[:, b, q, :]).then_inc(stats_made, 1)
                if not (isinstance(g, int) and g < 2):
                    dve.wait_ge(xn_made, g - 1)
                dve.wait_ge(stats_made, T * (g + 1))
                dve.sem_inc(passed, 1)
                for q in range(T):
                    last = dve.bn_aggr(mv[:, b, q, :], stats[:, q, :])
                last.then_inc(mv_made, 1)
                dve.wait_ge(mv_made, g + 1)
                dve.tensor_scalar(ve[:, b, :], mv[:, b, :, 1], EPS, None, ALU.add).then_inc(ve_made, 1)

            def normalise(g, b, u):
                dve.wait_ge(rstd_made, g + 1)
                if not (isinstance(g, int) and g < 2):
                    dve.wait_ge(xn_out[b], 16 * u)
                    dve.wait_ge(turned, g - 1)
                for q in range(T):
                    last = dve.tensor_scalar(xnb[:, b, q, :], xb[:, b, q, :], mv[:, b, q, 0:1], rstd[:, b, q:q + 1], ALU.subtract, ALU.mult)
                last.then_inc(xn_made, 1)

            def add_bias(g, b, q):
                dve.wait_ge(y_made, T * g + q + 1)
                dve.tensor_tensor(lr[:, b, q, :, 0:D], psY[:, q, :].rearrange("p (s f) -> p s f", s=2), bias[:], ALU.add).then_inc(biased, 1)

            def head_sums(g, b, q):
                dve.wait_ge(weighted_made, T * g + q + 1)
                return dve.tensor_reduce(lr[:, b, q, :, D:XW], weighted[:, q, :, :].rearrange("p s (h f) -> p s h f", f=HD), AX.X, ALU.add)
            statistics(0, 0, 0)
            normalise(0, 0, 0)
            statistics(1, 1, 0)
            dve.wait_ge(wload, 8 * 16)
            dve.tensor_scalar(att_02[:], att_row[:], 0.2, None, ALU.mult).then_inc(att_made, 1)

            def slot(g, b, u):
                if not (isinstance(g, int) and g < 2):
                    dve.wait_ge(lr_out[b], 32 * u)
                add_bias(g, b, 0)
                if not is_last(g, 1):
                    normalise(g + 1, 1 - b, u + b)
                add_bias(g, b, 1)
                head_sums(g, b, 0)
                add_bias(g, b, 2)
                if not is_last(g, 2):
                    statistics(g + 2, b, u + 1)
                add_bias(g, b, 3)
                head_sums(g, b, 1)
                head_sums(g, b, 2)
                head_sums(g, b, 3).then_inc(lr_made, 1)
            groups(dve, slot)

        @block.scalar
        def _(act):
            def copy_turned(g, b):
                act.wait_ge(turned, g + 1)
                if not (isinstance(g, int) and g < 2):
                    act.wait_ge(y_made, T * (g - 1))
                for h in range(2):
                    act.copy(xT[:, b, h, :], psT[:, b, h, :]).then_inc(xT_made, 1)
            copy_turned(0, 0)

            def slot(g, b, u):
                if not is_last(g, 1):
                    copy_turned(g + 1, 1 - b)
            groups(act, slot)

        @block.tensor
        def _(pe):
            pe.wait_ge(consts, 2)

            def turn(g, b):
                pe.wait_ge(xn_made, g + 1)
                if not (isinstance(g, int) and g < 2):
                    pe.wait_ge(xT_made, 2 * (g - 1))
                for q in range(T):
                    for h in range(2):
                        last = pe.transpose(psT[:, b, h, P * q:P * q + P], xnb[:, b, q, P * h:P * h + P], ident[:])
                last.then_inc(turned, 1)
            turn(0, 0)
            pe.wait_ge(wload, 8 * 16)

            def slot(g, b, u):
                pe.wait_ge(xT_made, 2 * (g + 1))
                for q in range(T):
                    if q == T - 1 and not is_last(g, 1):
                        turn(g + 1, 1 - b)
                    if not (isinstance(g, int) and g == 0):
                        pe.wait_ge(biased, T * (g - 1) + q + 1)
                    for h in range(2):
                        last = pe.matmul(psY[:, q, :], xT[:, b, h, P * q:P * q + P], W[:, h, :], start=h == 0, stop=h == 1)
                    last.then_inc(y_made, 1)
            groups(pe, slot)


HID, EXPERTS = 1024, 8
HC = HID // P
T4 = 4
GROUP = T4 * P
GROUPS = -(-NODES // GROUP)
LAST0 = NODES - GROUP
REPEATED = (GROUPS - 1) * GROUP - LAST0
CAP = (NODES // P + 2) * P
RW = D + 4
ETILES = (NODES + EXPERTS * (P - 1)) // P
ROUTED = EXPERTS * CAP + P
NOWHERE = float(1 << 20)


def nodes(nc, passed, x, bias, gamma, beta, W1, b1, Wg, bg, Wd, wd, xn_d, st_d, routed_d, etab_d):
    with ExitStack() as ctx:
        sb = lambda n, s, d=F32: ctx.enter_context(nc.sbuf_tensor(n, s, d))
        ps = lambda n, s, d=F32: ctx.enter_context(nc.psum_tensor(n, s, d))
        sem = lambda n: ctx.enter_context(nc.semaphore(n))
        stb = sb("n_st", [P, RING, T4, SW]); xnb = sb("n_xn", [P, RING, T4, D]); xb = sb("n_x", [P, RING, T4, D]); znorm = sb("znorm", [P, T4, D]); scaled = sb("scaled", [P, T4, D])
        rden = sb("rden", [P, T4, HEADS]); z = sb("z", [P, T4, D]); y = sb("n_y", [P, T4, D]); neg = sb("neg", [P, T4, D]); eneg = sb("eneg", [P, T4, D])
        stats = sb("n_stats", [P, T4, 6]); mv = sb("n_mv", [P, T4, 2]); ve = sb("n_ve", [P, T4]); rstd = sb("n_rstd", [P, T4])
        row = sb("row", [P, RING, T4, RW]); x2n = sb("x2n", [P, T4, D]); x2T = sb("x2T", [P, 2, GROUP]); H = sb("H", [P, HC, GROUP])
        bias_r = sb("bias_r", [P, D]); gamma_r = sb("gamma_r", [P, D]); beta_r = sb("beta_r", [P, D]); bg_r = sb("bg_r", [P, EXPERTS])
        w1 = sb("w1", [P, 2, HID]); b1c = sb("b1c", [P, HC]); wg = sb("wg", [P, HC, EXPERTS])
        lg = sb("lg", [P, T4, EXPERTS]); lmax = sb("lmax", [P, T4]); ex = sb("ex", [P, T4, EXPERTS]); pr = sb("pr", [P, T4, EXPERTS])
        one = sb("one_hot", [P, T4, EXPERTS]); before = sb("before", [P, T4 + 1, EXPERTS]); cnt = sb("cnt", [P, EXPERTS]); cap0 = sb("cap0", [P, EXPERTS])
        prio = sb("prio", [P, EXPERTS]); top = sb("top", [P, T4]); rk = sb("rk", [P, T4, EXPERTS]); posf = sb("posf", [P, T4]); posi = sb("posi", [P, RING, T4], I32)
        valid = sb("valid", [P, T4]); invalid = sb("invalid", [P, T4]); half = sb("n_half", [P, T4]); ident = sb("n_ident", [P, P]); ones = sb("n_ones", [P, P]); tri = sb("tri", [P, P])
        pid = sb("pid", [P, 1]); nodei = sb("nodei", [P, T4])
        j128 = sb("n_j128", [P, 1]); nti = sb("nti", [P, EXPERTS], I32); ntf = sb("ntf", [P, EXPERTS]); w = sb("n_w", [P, 6, EXPERTS]); red = sb("n_red", [P, 4]); et = sb("et", [P, 2]); eti = sb("eti", [P, 2], I32)
        pad = sb("pad", [P, RW]); padpos = sb("padpos", [P, EXPERTS], I32)
        psx = ps("psx", [P, 2, GROUP]); psh = ps("psh", [P, 4, GROUP]); psl_ = ps("psl", [P, 512]); psr_ = ps("psr", [P, 512])
        psl = psl_[:, 0:T4 * EXPERTS].rearrange("p (t e) -> p t e", e=EXPERTS); psr = psr_[:, 0:(T4 + 1) * EXPERTS].rearrange("p (t e) -> p t e", e=EXPERTS)
        cz = sem("n_cz"); consts = sem("n_consts"); wload = sem("n_wload"); loaded = [sem(f"n_loaded{q}") for q in range(RING)]; xnb_done = sem("xnb_done"); zn_done = sem("zn_done"); scaled_done = sem("scaled_done"); shifted = sem("shifted")
        x1_done = sem("x1_done"); z_done = sem("z_done"); ve_made = sem("n_ve_made"); rstd_made = sem("n_rstd_made"); neg_done = sem("neg_done"); eneg_done = sem("eneg_done"); x2_done = sem("x2_done")
        xT = sem("n_xT"); xT_copied = sem("xT_copied"); h_made = sem("h_made"); gelu_done = sem("gelu_done"); l_part = sem("l_part"); lm_done = sem("lm_done"); ex_done = sem("ex_done")
        hot_done = sem("n_hot_done"); r_made = sem("r_made"); pos_done = sem("pos_done"); scattered = [sem(f"scattered{q}") for q in range(RING)];
        rowbase = sb("rowbase", [P, 1]); top_done = sem("top_done"); masked = sem("masked"); masked2 = sem("masked2"); rk_s = sem("rk_step"); pf_done = sem("pf_done")
        wd_in = sem("wd_in"); link_s = sem("node_step"); lg_done = sem("lg_done"); route_s = sem("route_step"); tabs = sem("n_tabs"); padded = sem("padded"); tstep = sem("tstep"); tstored = sem("tstored")
        block = ctx.enter_context(nc.Block())
        bro = lambda v, s: v.to_broadcast(s)

        def slots(eng, first, slot):
            first()
            for g in range(RING):
                slot(g, g, 0, route=g >= 1)
            with eng.Fori(1, (GROUPS - 1) // RING) as i:
                for b in range(RING):
                    slot(RING * i + b, b, i)
            slot(GROUPS - 1, (GROUPS - 1) % RING, (GROUPS - 1) // RING, ahead=False)
            slot(GROUPS, GROUPS % RING, GROUPS // RING, hidden=False, ahead=False)

        def after(b, u):
            return ((b + 1) % RING, u + 1 if b == RING - 1 else u)

        def previous(b, u):
            return ((b - 1) % RING, u - 1 if b == 0 else u)

        def rows(g):
            return LAST0 if isinstance(g, int) and g == GROUPS - 1 else g * GROUP

        def grouped(a, g):
            r0 = rows(g)
            return a[bass.ds(r0, GROUP), :].rearrange("(t p) c -> p t c", p=P)

        @block.sync
        def _(sp):
            def load(g, b):
                sp.dma_start(stb[:, b, :, :], grouped(st_d, g)).then_inc(loaded[b], 16)
                sp.dma_start(xnb[:, b, :, :], grouped(xn_d, g)).then_inc(loaded[b], 16)
                sp.dma_start(xb[:, b, :, :], grouped(x, g)).then_inc(loaded[b], 16)
            load(0, 0)
            rb = lambda a, n: a.rearrange("(o c) -> o c", o=1).to_broadcast([P, n])
            sp.dma_start(bias_r[:], rb(bias, D)).then_inc(wload, 16)
            sp.dma_start(gamma_r[:], rb(gamma, D)).then_inc(wload, 16)
            sp.dma_start(beta_r[:], rb(beta, D)).then_inc(wload, 16)
            sp.dma_start(bg_r[:], rb(bg, EXPERTS)).then_inc(wload, 16)
            sp.dma_start(w1[:], W1.rearrange("(k p) c -> p k c", p=P)).then_inc(wload, 16)
            sp.dma_start(wg[:], Wg.rearrange("(k p) c -> p k c", p=P)).then_inc(wload, 16)
            with nc.allow_non_contiguous_dma(reason="bias by hidden unit"):
                sp.dma_start(b1c[:], b1.rearrange("(k p) -> p k", p=P)).then_inc(wload, 16)

            for g in range(1, RING):
                load(g, g)
            with sp.Fori(0, (GROUPS - 4) // RING) as i:
                for b in range(RING):
                    g = RING * i + b
                    sp.wait_ge(x1_done, g + 1)
                    sp.sem_inc(passed, 1)
                    load(g + RING, b)
                sp.dma_start(wd[:, bass.ds(i, 1), :, :].rearrange("p o k c -> p (o k) c"),
                             Wd[bass.ds(i, 1), :, :].rearrange("o (k p) c -> p (o k) c", p=P)).then_inc(wd_in, 16)
            sp.dma_start(wd[:, EXPERTS - 1, :, :], Wd[EXPERTS - 1, :, :].rearrange("(k p) c -> p k c", p=P)).then_inc(wd_in, 16)
            sp.wait_ge(x1_done, GROUPS - RING)
            load(GROUPS - 1, (GROUPS - 1) % RING)
            sp.wait_ge(tabs, 1)
            with nc.allow_non_contiguous_dma(reason="a table row"):
                sp.dma_start(etab_d[0, :, None], eti[0:ETILES, 0:1]).then_inc(tstored, 16)
                sp.dma_start(etab_d[1, :, None], eti[0:ETILES, 1:2]).then_inc(tstored, 16)
            sp.dma_start(routed_d[EXPERTS * CAP:ROUTED, :], pad[:]).then_inc(tstored, 16)
            sp.wait_ge(tstored, 48)
            sp.wait_ge(wd_in, 16 * EXPERTS)

        @block.gpsimd
        def _(pool):
            pool.memset(ones[:], 1.0).then_inc(cz, 1)
            pool.memset(half[:], -0.5).then_inc(consts, 1)
            pool.memset(valid[:], 1.0).then_inc(cz, 1)
            pool.iota(pid[:], [[0, 1]], base=0, channel_multiplier=1, allow_small_or_imprecise_dtypes=True).then_inc(consts, 1)
            pool.iota(nodei[:], [[P, T4]], base=0, channel_multiplier=1, allow_small_or_imprecise_dtypes=True).then_inc(consts, 1)
            pool.iota(cap0[:], [[CAP, EXPERTS]], base=0, channel_multiplier=0, allow_small_or_imprecise_dtypes=True).then_inc(consts, 1)
            pool.iota(prio[:], [[-1, EXPERTS]], base=EXPERTS, channel_multiplier=0, allow_small_or_imprecise_dtypes=True).then_inc(consts, 1)
            pool.iota(j128[:], [[0, 1]], base=0, channel_multiplier=P, allow_small_or_imprecise_dtypes=True).then_inc(consts, 1)
            pool.wait_ge(cz, 2)
            pool.affine_select(out=ident[:], in_=ones[:], compare_op=ALU.is_equal, fill=0.0, base=0, pattern=[[-1, P]], channel_multiplier=1).then_inc(consts, 1)
            pool.affine_select(out=tri[:], in_=ones[:], compare_op=ALU.is_gt, fill=0.0, base=0, pattern=[[1, P]], channel_multiplier=-1).then_inc(consts, 1)
            pool.affine_select(out=valid[:], in_=ones[:, 0:T4], compare_op=ALU.is_ge, fill=0.0, base=-REPEATED, pattern=[[P, T4]], channel_multiplier=1).then_inc(consts, 1)

            def rsqrt(g, n):
                pool.wait_ge(ve_made, 2 * g + n + 1)
                pool.tensor_tensor(rstd[:], ve[:], half[:], ALU.pow).then_inc(rstd_made, 1)

            def scatter(g, b):
                pool.wait_ge(pos_done, g + 1)
                pool.sem_inc(passed, 1)
                for t in range(T4):
                    pool.indirect_dma_start(routed_d[:, :], bass.IndirectOffsetOnAxis(posi[:, b, t:t + 1], 0), row[:, b, t, :], None,
                                            bounds_check=ROUTED - 1, oob_is_err=False).then_inc(scattered[b], 16)
            def add_node_bias(g, b, u):
                pool.wait_ge(loaded[b], 48 * (u + 1))
                pool.tensor_tensor(xnb[:, b, :, :], xnb[:, b, :, :], bias_r[:].unsqueeze(1).to_broadcast([P, T4, D]), ALU.add).then_inc(xnb_done, 1)

            def scale_shift(g):
                pool.wait_ge(zn_done, g + 1)
                pool.tensor_tensor(scaled[:], znorm[:], gamma_r[:].unsqueeze(1).to_broadcast([P, T4, D]), ALU.mult).then_inc(scaled_done, 1)
                pool.wait_ge(scaled_done, g + 1)
                pool.tensor_tensor(z[:], scaled[:], beta_r[:].unsqueeze(1).to_broadcast([P, T4, D]), ALU.add).then_inc(shifted, 1)

            def first():
                pool.wait_ge(wload, 7 * 16)
                add_node_bias(0, 0, 0)
                rsqrt(0, 0)
                scale_shift(0)
                rsqrt(0, 1)

            def slot(g, b, u, hidden=True, ahead=True, route=True):
                if ahead:
                    add_node_bias(g + 1, *after(b, u))
                    rsqrt(g + 1, 0)
                    scale_shift(g + 1)
                if route:
                    scatter(g - 1, previous(b, u)[0])
                if ahead:
                    rsqrt(g + 1, 1)
            slots(pool, first, slot)
            pool.wait_ge(tabs, 1)
            for q in range(RING):
                pool.wait_ge(scattered[q], 16 * T4 * len(range(q, GROUPS, RING)))
            for e in range(EXPERTS):
                pool.indirect_dma_start(routed_d[:, :], bass.IndirectOffsetOnAxis(padpos[:, e:e + 1], 0), pad[:, :], None,
                                        bounds_check=ROUTED - 1, oob_is_err=False).then_inc(padded, 16)
            pool.wait_ge(padded, 16 * EXPERTS)

        @block.vector
        def _(dve):
            dve.memset(cnt[:], 0.0)
            dve.memset(before[:, 0, :], 0.0)
            dve.memset(pad[:, 0:RW - 1], 0.0)
            dve.memset(pad[:, RW - 1:RW], NOWHERE)
            dve.wait_ge(consts, 9)
            dve.wait_ge(wload, 7 * 16)
            dve.tensor_scalar(invalid[:], valid[:], -NOWHERE, NOWHERE, ALU.mult, ALU.add)

            N_STEPS, R_STEPS = [None], [None]

            def chain(s, g, total):
                n = [0]

                def then(ins, wait=True):
                    n[0] += 1
                    ins.then_inc(s, 1)
                    if wait:
                        dve.wait_ge(s, total * g + n[0])
                return then, n

            def lg_step(g):
                dve.wait_ge(l_part, HC * (g + 1))
                dve.tensor_tensor(lg[:], psl, bg_r[:].unsqueeze(1).to_broadcast([P, T4, EXPERTS]), ALU.add).then_inc(lg_done, 1)

            def moments(g, src, k):
                for t in range(T4):
                    ins = dve.bn_stats(stats[:, t, :], src[:, t, :])
                ins.then_inc(z_done, 1)
                dve.wait_ge(z_done, 4 * g + 2 * k + 1)
                dve.sem_inc(passed, 1)
                for t in range(T4):
                    ins = dve.bn_aggr(mv[:, t, :], stats[:, t, :])
                ins.then_inc(z_done, 1)
                dve.wait_ge(z_done, 4 * g + 2 * k + 2)
                dve.tensor_scalar(ve[:], mv[:, :, 1], EPS, None, ALU.add).then_inc(ve_made, 1)

            NT = 7

            def node_start(g, b, u, logits):
                then, n = chain(link_s, g, NT)
                heads = lambda v: v.rearrange("p t (h f) -> p t h f", f=HS)
                acc = heads(stb[:, b, :, 0:HEADS * HS])
                dve.wait_ge(loaded[b], 48 * (u + 1))
                then(dve.tensor_scalar(rden[:], acc[:, :, :, HD], 0.0, None, ALU.is_equal))
                then(dve.tensor_tensor(rden[:], rden[:], acc[:, :, :, HD], ALU.add))
                then(dve.reciprocal(rden[:], rden[:]))
                then(dve.tensor_tensor(y[:].rearrange("p t (h f) -> p t h f", f=HD), acc[:, :, :, 0:HD], rden[:].unsqueeze(3).to_broadcast([P, T4, HEADS, HD]), ALU.mult))
                dve.wait_ge(xnb_done, g + 1)
                then(dve.tensor_tensor(y[:], y[:], xnb[:, b, :, :], ALU.add))
                if logits:
                    lg_step(g - 2)
                moments(g, y, 0)
                dve.wait_ge(rstd_made, 2 * g + 1)
                for t in range(T4):
                    ins = dve.tensor_scalar(znorm[:, t, :], y[:, t, :], mv[:, t, 0:1], rstd[:, t:t + 1], ALU.subtract, ALU.mult)
                ins.then_inc(zn_done, 1)

            def node_middle(g, b, u):
                dve.wait_ge(shifted, g + 1)
                dve.tensor_scalar(neg[:], z[:], 0.0, None, ALU.min).then_inc(neg_done, 1)
                if not (isinstance(u, int) and u == 0):
                    dve.wait_ge(scattered[b], 16 * T4 * u)
                dve.scalar_tensor_tensor(out=row[:, b, :, 0:D], in0=z[:], scalar=0.0, in1=xb[:, b, :, :], op0=ALU.max, op1=ALU.add).then_inc(link_s, 1)

            def node_end(g, b, u):
                dve.wait_ge(link_s, NT * g + 6)
                dve.wait_ge(eneg_done, g + 1)
                dve.scalar_tensor_tensor(out=row[:, b, :, 0:D], in0=eneg[:], scalar=-1.0, in1=row[:, b, :, 0:D], op0=ALU.add, op1=ALU.add).then_inc(x1_done, 1)
                dve.wait_ge(x1_done, g + 1)
                moments(g, row[:, b, :, 0:D], 1)
                dve.wait_ge(rstd_made, 2 * g + 2)
                dve.tensor_copy(row[:, b, :, D], mv[:, :, 0])
                dve.tensor_copy(row[:, b, :, D + 1], rstd[:]).then_inc(link_s, 1)
                dve.wait_ge(link_s, NT * g + 7)
                if not (isinstance(g, int) and g == 0):
                    dve.wait_ge(xT, g)
                for t in range(T4):
                    ins = dve.tensor_scalar(x2n[:, t, :], row[:, b, t, 0:D], mv[:, t, 0:1], rstd[:, t:t + 1], ALU.subtract, ALU.mult)
                ins.then_inc(x2_done, 1)

            RT = 9
            def choose(g, b, last=False):
                then, n = chain(route_s, g, RT)
                e3 = lambda v: v.unsqueeze(2).to_broadcast([P, T4, EXPERTS])
                dve.wait_ge(lg_done, g + 1)
                then(dve.tensor_reduce(lmax[:], lg[:], AX.X, ALU.max))
                dve.tensor_tensor(lg[:], lg[:], e3(lmax[:]), ALU.subtract).then_inc(lm_done, 1)
                dve.wait_ge(ex_done, g + 1)
                then(dve.tensor_reduce(lmax[:], ex[:], AX.X, ALU.add))
                then(dve.reciprocal(lmax[:], lmax[:]))
                then(dve.tensor_tensor(pr[:], ex[:], e3(lmax[:]), ALU.mult))
                dve.tensor_reduce(top[:], pr[:], AX.X, ALU.max).then_inc(top_done, 1)
                dve.wait_ge(top_done, g + 1)
                dve.tensor_copy(row[:, b, :, D + 2], top[:])
                dve.tensor_scalar(row[:, b, :, D + 3], nodei[:], rowbase[:, 0:1], None, ALU.add)
                then(dve.tensor_tensor(one[:], pr[:], e3(top[:]), ALU.is_equal))
                then(dve.tensor_tensor(one[:], one[:], prio[:].unsqueeze(1).to_broadcast([P, T4, EXPERTS]), ALU.mult))
                then(dve.tensor_reduce(top[:], one[:], AX.X, ALU.max))
                then(dve.tensor_tensor(one[:], prio[:].unsqueeze(1).to_broadcast([P, T4, EXPERTS]), e3(top[:]), ALU.is_equal))
                if last:
                    dve.tensor_tensor(one[:], one[:], e3(valid[:]), ALU.mult).then_inc(masked, 1)
                    dve.wait_ge(masked, 1)
                for t in range(T4):
                    dve.tensor_tensor(before[:, t + 1, :], before[:, t, :], one[:, t, :], ALU.add).then_inc(hot_done, 1)
                    dve.wait_ge(hot_done, 4 * g + t + 1)
                assert n[0] == RT - 1, n

            def place(g, b, last=False):
                dve.wait_ge(r_made, g + 1)
                then = lambda ins: (ins.then_inc(route_s, 1), dve.wait_ge(route_s, RT * (g + 1)))
                then(dve.tensor_tensor(rk[:], psr[:, 0:T4, :], cnt[:].unsqueeze(1).to_broadcast([P, T4, EXPERTS]), ALU.add))
                dve.tensor_tensor(rk[:], rk[:], cap0[:].unsqueeze(1).to_broadcast([P, T4, EXPERTS]), ALU.add).then_inc(rk_s, 1)
                dve.wait_ge(rk_s, 2 * g + 1)
                dve.tensor_tensor(rk[:], rk[:], one[:], ALU.mult).then_inc(rk_s, 1)
                dve.tensor_tensor(cnt[:], cnt[:], psr[:, T4, :], ALU.add)
                dve.wait_ge(rk_s, 2 * g + 2)
                dve.tensor_reduce(posf[:], rk[:], AX.X, ALU.add).then_inc(pf_done, 1)
                dve.tensor_scalar(rowbase[:], rowbase[:], float(GROUP), None, ALU.add)
                dve.wait_ge(pf_done, g + 1)
                if last:
                    dve.tensor_tensor(posf[:], posf[:], invalid[:], ALU.add).then_inc(masked, 1)
                    dve.wait_ge(masked, 2)
                dve.tensor_copy(posi[:, b, :], posf[:]).then_inc(pos_done, 1)

            dve.memset(rowbase[:], 0.0)
            def first():
                node_start(0, 0, 0, False)
                node_middle(0, 0, 0)
                node_end(0, 0, 0)

            def slot(g, b, u, hidden=True, ahead=True, route=True):
                nb, nu = after(b, u)
                pb = previous(b, u)[0]
                last = isinstance(g, int) and g == GROUPS
                if last:
                    dve.wait_ge(pos_done, GROUPS - 1)
                    dve.memset(rowbase[:], float(LAST0)).then_inc(masked2, 1)
                    dve.wait_ge(masked2, 1)
                if ahead:
                    node_start(g + 1, nb, nu, route)
                elif route:
                    lg_step(g - 1)
                if route:
                    choose(g - 1, pb, last)
                if ahead:
                    node_middle(g + 1, nb, nu)
                if route:
                    place(g - 1, pb, last)
                if ahead:
                    node_end(g + 1, nb, nu)
            slots(dve, first, slot)
            q = [0]

            def then(ins):
                q[0] += 1
                ins.then_inc(tstep, 1)
                dve.wait_ge(tstep, q[0])
            then(dve.tensor_scalar(nti[:], cnt[:], float(P - 1), None, ALU.add))
            then(dve.tensor_scalar(nti[:], nti[:], 7, None, ALU.arith_shift_right))
            then(dve.tensor_copy(ntf[:], nti[:]))
            then(dve.memset(w[:, 0, :], 1.0))
            then(dve.tensor_tensor_scan(w[:, 1, :], w[:, 0, :], ntf[:], 0.0, ALU.mult, ALU.add))
            then(dve.tensor_tensor(w[:, 2, :], w[:, 1, :], ntf[:], ALU.subtract))
            then(dve.tensor_scalar(w[:, 3, :], w[:, 1, :], pid[:, 0:1], None, ALU.is_gt))
            then(dve.tensor_scalar(w[:, 4, :], w[:, 2, :], pid[:, 0:1], None, ALU.is_le))
            then(dve.tensor_tensor(w[:, 3, :], w[:, 3, :], w[:, 4, :], ALU.mult))
            then(dve.tensor_scalar(w[:, 4, :], w[:, 2, :], -float(P), j128[:, 0:1], ALU.mult, ALU.add))
            then(dve.tensor_tensor(w[:, 4, :], w[:, 4, :], cap0[:], ALU.add))
            then(dve.tensor_tensor(w[:, 4, :], w[:, 4, :], w[:, 3, :], ALU.mult))
            then(dve.tensor_scalar(w[:, 5, :], prio[:], -1.0, float(EXPERTS), ALU.mult, ALU.add))
            then(dve.tensor_tensor(w[:, 5, :], w[:, 5, :], w[:, 3, :], ALU.mult))
            then(dve.tensor_reduce(red[:, 0:1], w[:, 3, :], AX.X, ALU.add))
            then(dve.tensor_reduce(red[:, 1:2], w[:, 4, :], AX.X, ALU.add))
            then(dve.tensor_reduce(et[:, 1:2], w[:, 5, :], AX.X, ALU.add))
            then(dve.tensor_scalar(red[:, 2:3], red[:, 0:1], -float(EXPERTS * CAP), float(EXPERTS * CAP), ALU.mult, ALU.add))
            then(dve.tensor_tensor(et[:, 0:1], red[:, 1:2], red[:, 2:3], ALU.add))
            then(dve.tensor_copy(eti[:], et[:]))
            then(dve.tensor_tensor(w[:, 0, :], cnt[:], cap0[:], ALU.add))
            then(dve.tensor_scalar(padpos[:], w[:, 0, :], pid[:, 0:1], None, ALU.add))
            dve.tensor_copy(red[:, 3:4], red[:, 0:1]).then_inc(tabs, 1)

        @block.scalar
        def _(act):
            act.wait_ge(wload, 7 * 16)

            def elu(g):
                act.wait_ge(neg_done, g + 1)
                act.activation(eneg[:], neg[:], ACT.Exp).then_inc(eneg_done, 1)

            def softmax(g):
                act.wait_ge(lm_done, g + 1)
                act.activation(ex[:], lg[:], ACT.Exp).then_inc(ex_done, 1)

            def copy_turned(g):
                act.wait_ge(xT, g + 1)
                if not (isinstance(g, int) and g == 0):
                    act.wait_ge(h_made, HC * g)
                act.copy(x2T[:], psx[:]).then_inc(xT_copied, 1)

            def gelu(g, c):
                act.wait_ge(h_made, HC * g + c + 1)
                if not (isinstance(g, int) and g == 0):
                    act.wait_ge(l_part, HC * (g - 1) + c + 1)
                act.activation(H[:, c, :], psh[:, c % 4, :], ACT.Gelu, bias=b1c[:, c:c + 1]).then_inc(gelu_done, 1)

            def first():
                elu(0)
                copy_turned(0)

            def slot(g, b, u, hidden=True, ahead=True, route=True):
                if hidden:
                    gelu(g, 0)
                    gelu(g, 1)
                if route:
                    softmax(g - 1)
                if hidden:
                    for c in range(2, 4):
                        gelu(g, c)
                if ahead:
                    elu(g + 1)
                if hidden:
                    for c in range(4, HC):
                        gelu(g, c)
                if ahead:
                    copy_turned(g + 1)
            slots(act, first, slot)

        @block.tensor
        def _(pe):
            pe.wait_ge(consts, 9)
            pe.wait_ge(wload, 7 * 16)

            def turn(g):
                pe.wait_ge(x2_done, g + 1)
                if not (isinstance(g, int) and g == 0):
                    pe.wait_ge(xT_copied, g)
                for h in range(2):
                    for t in range(T4):
                        last = pe.transpose(psx[:, h, P * t:P * t + P], x2n[:, t, P * h:P * h + P], ident[:])
                last.then_inc(xT, 1)

            def up(g, c):
                if not (isinstance(g, int) and g == 0 and c < 4):
                    pe.wait_ge(gelu_done, HC * g + c - 3)
                pe.matmul(psh[:, c % 4, :], w1[:, 0, P * c:P * c + P], x2T[:, 0, :], start=True, stop=False)
                pe.matmul(psh[:, c % 4, :], w1[:, 1, P * c:P * c + P], x2T[:, 1, :], start=False, stop=True).then_inc(h_made, 1)

            def logits(g, c):
                pe.wait_ge(gelu_done, HC * g + c + 1)
                if c == 0 and not (isinstance(g, int) and g == 0):
                    pe.wait_ge(lg_done, g)
                for t in range(T4):
                    last = pe.matmul(psl[:, t, :], H[:, c, P * t:P * t + P], wg[:, c, :], start=c == 0 and t == 0, stop=c == HC - 1, skip_group_check=True)
                last.then_inc(l_part, 1)

            def ranks(g):
                pe.wait_ge(hot_done, 4 * g + 4)
                if not (isinstance(g, int) and g == 0):
                    pe.wait_ge(pos_done, g)
                flat = lambda v: v.rearrange("p t e -> p (t e)")
                pe.matmul(flat(psr[:, 0:T4, :]), tri[:], flat(one[:]), start=True, stop=False, skip_group_check=True)
                pe.matmul(flat(psr[:, 0:T4, :]), ones[:], flat(before[:, 0:T4, :]), start=False, stop=True, skip_group_check=True)
                pe.matmul(psr[:, T4, :], ones[:], before[:, T4, :], start=True, stop=True, skip_group_check=True).then_inc(r_made, 1)

            def slot(g, b, u, hidden=True, ahead=True, route=True):
                if hidden:
                    pe.wait_ge(xT_copied, g + 1)
                    up(g, 0)
                    for c in range(1, 4):
                        up(g, c)
                        logits(g, c - 1)
                if route:
                    ranks(g - 1)
                if hidden:
                    for c in range(4, HC):
                        up(g, c)
                        if c == HC - 1 and ahead:
                            turn(g + 1)
                        logits(g, c - 1)
                    logits(g, HC - 1)
            slots(pe, lambda: turn(0), slot)


def experts(nc, passed, W1, b1, wd, bd, routed_d, etab_d, out):
    with ExitStack() as ctx:
        sb = lambda n, s, d=F32: ctx.enter_context(nc.sbuf_tensor(n, s, d))
        ps = lambda n, s, d=F32: ctx.enter_context(nc.psum_tensor(n, s, d))
        sem = lambda n: ctx.enter_context(nc.semaphore(n))
        ring = lambda n: [sem(f"{n}{r}") for r in range(RING)]
        bdr = sb("bdr", [P, EXPERTS, D]); w1 = sb("x_w1", [P, 2, HID]); b1c = sb("x_b1c", [P, HC])
        row = sb("x_row", [P, RING, RW]); x2 = sb("x_x2", [P, D]); x2T = sb("x_x2T", [P, RING, 2, P]); H = sb("x_H", [P, RING, HC, P])
        y = sb("x_y", [P, RING, D]); res = sb("x_res", [P, RING, D]); node = sb("x_node", [P, RING, 1], I32)
        ident = sb("x_ident", [P, P]); ones = sb("x_ones", [P, P]); tab = sb("x_tab", [1, 2, ETILES], I32)
        psx = ps("x_psx", [P, 2, 256]); psh = ps("x_psh", [P, 2, 512]); psy = ps("x_psy", [P, 3, 512])
        cz = sem("x_cz"); consts = sem("x_consts"); wload = sem("x_wload"); row_in = ring("row_in"); x2_done = sem("x_x2_done"); xT = sem("x_xT"); xT_copied = sem("x_xT_copied")
        h_made = sem("x_h_made"); gelu = sem("x_gelu"); y_made = sem("x_y_made"); y1 = sem("x_y1"); res_done = sem("x_res"); stored = ring("x_stored")
        block = ctx.enter_context(nc.Block())
        one = lambda t: slice(t, t + 1) if isinstance(t, int) else bass.ds(t, 1)

        def slots(eng, slot):
            slot(0, 0, 0, down=False)
            slot(1, 1, 0)
            slot(2, 2, 0)
            with eng.Fori(1, ETILES // RING - 1) as i:
                for r in range(RING):
                    slot(RING * i + r, r, i)
            for t in range(ETILES - RING, ETILES):
                slot(t, t % RING, t // RING, turn=t + 1 < ETILES)
            slot(ETILES, 0, ETILES // RING, up=False, turn=False)

        def run(eng, step):
            for t in range(RING):
                step(t, t, 0)
            with eng.Fori(1, ETILES // RING) as i:
                for r in range(RING):
                    step(RING * i + r, r, i)

        @block.sync
        def _(sp):
            sp.dma_start(tab[:], etab_d[None, :, :]).then_inc(wload, 16)
            sp.dma_start(w1[:], W1.rearrange("(k p) c -> p k c", p=P)).then_inc(wload, 16)
            with nc.allow_non_contiguous_dma(reason="bias by hidden unit"):
                sp.dma_start(b1c[:], b1.rearrange("(k p) -> p k", p=P)).then_inc(wload, 16)
            sp.dma_start(bdr[:], bd.rearrange("(o e) d -> o e d", o=1).to_broadcast([P, EXPERTS, D])).then_inc(wload, 16)
            sp.wait_ge(wload, 16 * 4)

            def step(t, r, u):
                first = sp.value_load(tab[0:1, 0, one(t)], min_val=0, max_val=ROUTED - P)
                if not (isinstance(u, int) and u == 0):
                    sp.wait_ge(res_done, t - 2)
                    sp.sem_inc(passed, 1)
                sp.dma_start(row[:, r, :], routed_d[bass.ds(first, P), :]).then_inc(row_in[r], 16)
            run(sp, step)

        @block.gpsimd
        def _(pool):
            pool.memset(ones[:], 1.0).then_inc(cz, 1)
            pool.wait_ge(cz, 1)
            pool.affine_select(out=ident[:], in_=ones[:], compare_op=ALU.is_equal, fill=0.0, base=0, pattern=[[-1, P]], channel_multiplier=1).then_inc(consts, 1)

            def step(t, r, u):
                pool.wait_ge(res_done, t + 1)
                pool.sem_inc(passed, 1)
                pool.indirect_dma_start(out[:, :], bass.IndirectOffsetOnAxis(node[:, r, :], 0), res[:, r, :], None, bounds_check=NODES - 1, oob_is_err=False).then_inc(stored[r], 16)
            run(pool, step)
            for r in range(RING):
                pool.wait_ge(stored[r], 16 * (ETILES // RING))

        @block.vector
        def _(dve):
            def normal(t, r, u):
                dve.wait_ge(row_in[r], 16 * (u + 1))
                if not (isinstance(t, int) and t == 0):
                    dve.wait_ge(xT, t)
                dve.tensor_scalar(x2[:], row[:, r, 0:D], row[:, r, D:D + 1], row[:, r, D + 1:D + 2], ALU.subtract, ALU.mult).then_inc(x2_done, 1)

            def finish(t, r, u):
                e = dve.value_load(tab[0:1, 1, one(t)], min_val=0, max_val=EXPERTS - 1)
                dve.wait_ge(y_made, t + 1)
                dve.sem_inc(passed, 1)
                dve.tensor_tensor(y[:, r, :], psy[:, r, 0:D], bdr[:, one2(e), :].rearrange("p o d -> p (o d)"), ALU.add).then_inc(y1, 1)
                if not (isinstance(u, int) and u == 0):
                    dve.wait_ge(stored[r], 16 * u)
                dve.tensor_copy(node[:, r, :], row[:, r, D + 3:D + 4])
                dve.wait_ge(y1, t + 1)
                dve.scalar_tensor_tensor(out=res[:, r, :], in0=y[:, r, :], scalar=row[:, r, D + 2:D + 3], in1=row[:, r, 0:D], op0=ALU.mult, op1=ALU.add).then_inc(res_done, 1)
            one2 = lambda e: bass.ds(e, 1)
            dve.wait_ge(wload, 16 * 4)
            normal(0, 0, 0)

            def slot(t, r, u, up=True, turn=True, down=True):
                if turn:
                    normal(t + 1, (r + 1) % RING, u + 1 if r == 2 else u)
                if down:
                    finish(t - 1, (r + 2) % RING, u - 1 if r == 0 else u)
            slots(dve, slot)

        @block.scalar
        def _(act):
            act.wait_ge(wload, 16 * 4)

            def copy_turned(t, r):
                act.wait_ge(xT, t + 1)
                act.copy(x2T[:, r, :, :], psx[:, :, 0:P]).then_inc(xT_copied, 1)
            copy_turned(0, 0)

            def slot(t, r, u, up=True, turn=True, down=True):
                if up:
                    for half in range(2):
                        act.wait_ge(h_made, 2 * t + half + 1)
                        for c in range(HC // 2):
                            last = act.activation(H[:, r, HC // 2 * half + c, :], psh[:, half, P * c:P * c + P], ACT.Gelu, bias=b1c[:, HC // 2 * half + c:HC // 2 * half + c + 1])
                        last.then_inc(gelu, 1)
                if turn:
                    copy_turned(t + 1, (r + 1) % RING)
            slots(act, slot)

        @block.tensor
        def _(pe):
            pe.wait_ge(wload, 16 * 4)
            pe.wait_ge(consts, 1)

            def project_down(t, r, e, c0, c1):
                if c0 == 0:
                    pe.wait_ge(gelu, 2 * t + 2)
                    if not (isinstance(t, int) and t < 3):
                        pe.wait_ge(y1, t - 2)
                    pe.sem_inc(passed, 1)
                for c in range(c0, c1):
                    last = pe.matmul(psy[:, r, 0:D], H[:, r, c, :], wd[:, bass.ds(e, 1), c, :].rearrange("p o d -> p (o d)"), start=c == 0, stop=c == HC - 1)
                if c1 == HC:
                    last.then_inc(y_made, 1)

            def turn_rows(t, r):
                pe.wait_ge(x2_done, t + 1)
                if not (isinstance(t, int) and t == 0):
                    pe.wait_ge(xT_copied, t)
                for h in range(2):
                    last = pe.transpose(psx[:, h, 0:P], x2[:, P * h:P * h + P], ident[:])
                last.then_inc(xT, 1)

            def hidden(t, r, half):
                if not (isinstance(t, int) and t == 0):
                    pe.wait_ge(gelu, 2 * t + half - 1)
                for c in range(HC // 2):
                    for h in range(2):
                        at = P * (HC // 2 * half + c)
                        last = pe.matmul(psh[:, half, P * c:P * c + P], w1[:, h, at:at + P], x2T[:, r, h, :], start=h == 0, stop=h == 1)
                last.then_inc(h_made, 1)
            turn_rows(0, 0)

            def slot(t, r, u, up=True, turn=True, down=True):
                if down:
                    e = pe.value_load(tab[0:1, 1, one(t - 1)], min_val=0, max_val=EXPERTS - 1)
                if up:
                    pe.wait_ge(xT_copied, t + 1)
                    hidden(t, r, 0)
                    hidden(t, r, 1)
                if down:
                    project_down(t - 1, (r + 2) % RING, e, 0, HC // 2)
                if turn:
                    turn_rows(t + 1, (r + 1) % RING)
                if down:
                    project_down(t - 1, (r + 2) % RING, e, HC // 2, HC)
            slots(pe, slot)



_INS = ['x', 'src', 'dst', 'L0_gnn_Wl', 'L0_gnn_bl', 'L0_gnn_Wr', 'L0_gnn_br', 'L0_gnn_att', 'L0_gnn_bias', 'L0_gnn_gamma',
        'L0_gnn_beta', 'L0_ffn_W1', 'L0_ffn_b1', 'L0_ffn_Wg', 'L0_ffn_bg', 'L0_ffn_Wd', 'L0_ffn_bd']


def program(nc, i, out):
    scratch = lambda name, shape, dt=F32: nc.dram_tensor(name, shape, dt).ap()
    xn_d = scratch("xn_d", (NODES, D))
    xl_d = scratch("xl_d", (NODES, XW))
    xr_d = scratch("xr_d", (NODES_UP, XW))
    st_d = scratch("st_d", (NODES_UP, SW))
    src_pad = scratch("src_pad", (PADDED,), I32)
    dst_pad = scratch("dst_pad", (PADDED,), I32)
    rows_d = scratch("rows_d", (3, BLOCKS))
    tabf_d = scratch("tabf_d", (BLOCKS + EXTRA,))
    tabi_d = scratch("tabi_d", (2, BLOCKS + EXTRA + 1), I32)
    routed_d = scratch("routed_d", (ROUTED, RW))
    etab_d = scratch("etab_d", (2, ETILES), I32)
    with nc.semaphore("passed") as passed:
        project(nc, passed, i['x'], i['L0_gnn_Wl'], i['L0_gnn_Wr'], i['L0_gnn_bl'], i['L0_gnn_br'], i['L0_gnn_att'], xn_d, xl_d, xr_d, st_d)
        setup(nc, i['src'], i['dst'], src_pad, dst_pad, xr_d, rows_d, tabf_d, tabi_d)
        edges(nc, passed, i['L0_gnn_att'], xl_d, xr_d, src_pad, dst_pad, st_d, tabf_d, tabi_d)
        with nc.sbuf_tensor("wd", [P, EXPERTS, HC, D], F32) as wd:
            nodes(nc, passed, i['x'], i['L0_gnn_bias'], i['L0_gnn_gamma'], i['L0_gnn_beta'], i['L0_ffn_W1'], i['L0_ffn_b1'], i['L0_ffn_Wg'],
                  i['L0_ffn_bg'], i['L0_ffn_Wd'], wd, xn_d, st_d, routed_d, etab_d)
            experts(nc, passed, i['L0_ffn_W1'], i['L0_ffn_b1'], wd, i['L0_ffn_bd'], routed_d, etab_d, out)


def kernel(**inputs):
    import numpy as _np
    import concourse.bacc as _bacc
    from concourse.bass_utils import run_bass_kernel_spmd as _run

    nc = _bacc.Bacc("TRN2", target_bir_lowering=False, num_devices=1)
    arrays, aps = {}, {}
    for name in _INS:
        a = _np.ascontiguousarray(inputs[name])
        arrays[f"in_{name}_dram"] = a
        aps[name] = nc.dram_tensor(f"in_{name}_dram", a.shape, mybir.dt.from_np(a.dtype), kind="ExternalInput").ap()
    out = nc.dram_tensor("out_0_dram", (NODES, D), F32, kind="ExternalOutput").ap()
    program(nc, aps, out)
    r = _run(nc, [arrays], core_ids=[0])
    return r.results[0]["out_0_dram"]
```
